# Optimizing a Trainium2 kernel written in Bass

```python
import numpy as np
import jax
import jax.numpy as jnp

def _softmax(x, axis=-1):
    return jax.nn.softmax(x, axis=axis)

def _gelu(x):
    return jax.nn.gelu(x, approximate=True)

def _silu(x):
    return jax.nn.silu(x)

def _sigmoid(x):
    return jax.nn.sigmoid(x)

def _layernorm(x, axis=-1, eps=1e-05):
    m = jnp.mean(x, axis=axis, keepdims=True)
    v = jnp.var(x, axis=axis, keepdims=True)
    return (x - m) / jnp.sqrt(v + eps)

def _scatter_add(tgt, idx, src, axis=0):
    return tgt.at[idx].add(src)

def _segment_sum(src, seg, n):
    return jax.ops.segment_sum(src, seg, n)
kernel_name = 'mk_gnn_resnorm_d4_gnn_r32_93dcd5'

def setup_inputs(seed: int=0):
    np.random.seed(seed)
    _w = jnp.asarray

    def _rec_inputs():
        import jax
        import jax.numpy as jnp
        _gk = jax.random.key(seed)
        x = -0.0003713 + 1 * jax.random.normal(jax.random.fold_in(_gk, 1), (50000, 128), jnp.float32)
        src = jax.random.randint(jax.random.fold_in(_gk, 2), (25000,), 0, 50000, jnp.int32)
        dst = jnp.minimum((50000 * jax.random.uniform(jax.random.fold_in(_gk, 3), (25000,)) ** 2.0).astype(jnp.int32), 49999)
        _o = jnp.argsort(dst, stable=True)
        src = src[_o]
        dst = dst[_o]
        edge_attr_32 = 0.000196303 + 1.00016 * jax.random.normal(jax.random.fold_in(_gk, 11), (25000, 32), jnp.float32)
        return (x, src, dst, edge_attr_32)
    x, src, dst, edge_attr_32 = _rec_inputs()

    def _L0_gnn_setup():
        import jax, jax.numpy as jnp
        import numpy as np
        N = 3125
        E = 18750
        D_IN = 128
        D = 128
        L = 3

        def gru_cell(m, h, w_ih, w_hh, b_ih, b_hh):
            gi = m @ w_ih.T + b_ih
            gh = h @ w_hh.T + b_hh
            ir, iz, inn = jnp.split(gi, 3, axis=-1)
            hr, hz, hn = jnp.split(gh, 3, axis=-1)
            r = jax.nn.sigmoid(ir + hr)
            z = jax.nn.sigmoid(iz + hz)
            n = jnp.tanh(inn + r * hn)
            return (1.0 - z) * n + z * h
        key = jax.random.key(seed)
        ks = jax.random.split(key, 10)
        s = 1.0 / np.sqrt(D)
        x = jax.random.normal(ks[0], (N, D_IN), dtype=jnp.float32)
        edge_index = jax.random.randint(ks[1], (2, E), 0, N, dtype=jnp.int64)
        lin_w = jax.random.normal(ks[2], (D, D_IN), dtype=jnp.float32) * (1.0 / np.sqrt(D_IN))
        lin_b = jnp.zeros((D,), dtype=jnp.float32)
        weight = jax.random.normal(ks[3], (L, D, D), dtype=jnp.float32) * s
        w_ih = jax.random.normal(ks[4], (3 * D, D), dtype=jnp.float32) * s
        w_hh = jax.random.normal(ks[5], (3 * D, D), dtype=jnp.float32) * s
        b_ih = jnp.zeros((3 * D,), dtype=jnp.float32)
        b_hh = jnp.zeros((3 * D,), dtype=jnp.float32)
        return {'x': x, 'lin_w': lin_w, 'lin_b': lin_b, 'weight': weight, 'w_ih': w_ih, 'w_hh': w_hh, 'b_ih': b_ih, 'b_hh': b_hh, 'edge_index': edge_index}
    _L0_gnn_all = _L0_gnn_setup()
    _L0_gnn_in = {k: v for k, v in _L0_gnn_all.items() if k in ('lin_w', 'lin_b', 'weight', 'w_ih', 'w_hh', 'b_ih', 'b_hh')}
    del _L0_gnn_all

    def _L1_gnn_setup():
        import jax, jax.numpy as jnp
        import numpy as np
        N = 3125
        E = 50000
        IN = 128
        OUT = 128
        H = 4
        FH = OUT // H
        EPS = 1e-05
        NEG_SLOPE = 0.2

        def _gat(x, src, dst, W, a_src, a_dst, b):
            n = x.shape[0]
            xw = (x @ W).reshape(n, H, FH)
            al_s = jnp.einsum('nhf,hf->nh', xw, a_src)
            al_d = jnp.einsum('nhf,hf->nh', xw, a_dst)
            e = jax.nn.leaky_relu(al_s[src] + al_d[dst], NEG_SLOPE)
            m = jax.ops.segment_max(e, dst, num_segments=n)
            ee = jnp.exp(e - m[dst])
            den = jax.ops.segment_sum(ee, dst, num_segments=n)
            alpha = ee / den[dst]
            out = jax.ops.segment_sum(alpha[:, :, None] * xw[src], dst, num_segments=n)
            return out.reshape(n, H * FH) + b

        def _bn(x, gamma, beta):
            mu = x.mean(0)
            var = x.var(0)
            return gamma * (x - mu) * jax.lax.rsqrt(var + EPS) + beta
        key = jax.random.key(seed)
        ks = jax.random.split(key, 10)
        x = jax.random.normal(ks[0], (N, IN), jnp.float32)
        edge_index = jax.random.randint(ks[1], (2, E), 0, N, dtype=jnp.int32)
        W1 = jax.random.normal(ks[2], (IN, OUT), jnp.float32) / np.float32(np.sqrt(IN))
        a1_src = jax.random.normal(ks[3], (H, FH), jnp.float32) * 0.1
        a1_dst = jax.random.normal(ks[4], (H, FH), jnp.float32) * 0.1
        b1 = jnp.zeros((OUT,), jnp.float32)
        g1 = jnp.ones((OUT,), jnp.float32)
        beta1 = jnp.zeros((OUT,), jnp.float32)
        W2 = jax.random.normal(ks[5], (OUT, OUT), jnp.float32) / np.float32(np.sqrt(OUT))
        a2_src = jax.random.normal(ks[6], (H, FH), jnp.float32) * 0.1
        a2_dst = jax.random.normal(ks[7], (H, FH), jnp.float32) * 0.1
        b2 = jnp.zeros((OUT,), jnp.float32)
        g2 = jnp.ones((OUT,), jnp.float32)
        beta2 = jnp.zeros((OUT,), jnp.float32)
        return dict(x=x, edge_index=edge_index, W1=W1, a1_src=a1_src, a1_dst=a1_dst, b1=b1, g1=g1, beta1=beta1, W2=W2, a2_src=a2_src, a2_dst=a2_dst, b2=b2, g2=g2, beta2=beta2)
    _L1_gnn_all = _L1_gnn_setup()
    _L1_gnn_in = {k: v for k, v in _L1_gnn_all.items() if k in ('W1', 'a1_src', 'a1_dst', 'b1', 'g1', 'beta1', 'W2', 'a2_src', 'a2_dst', 'b2', 'g2', 'beta2')}
    del _L1_gnn_all

    def _L2_gnn_setup():
        import jax, jax.numpy as jnp
        import numpy as np
        N_NODES = 50000
        N_EDGES = 25000
        HID = 128
        EDGE_DIM = 32
        N_LAYERS = 2
        key = jax.random.key(seed)
        ks = jax.random.split(key, 8)
        x = jax.random.normal(ks[0], (N_NODES, HID), dtype=jnp.float32)
        edge_index = jax.random.randint(ks[1], (2, N_EDGES), 0, N_NODES, dtype=jnp.int32)
        edge_attr = jax.random.normal(ks[2], (N_EDGES, EDGE_DIM), dtype=jnp.float32)
        s = 1.0 / np.sqrt(HID)
        se = 1.0 / np.sqrt(EDGE_DIM)
        W_l = jax.random.normal(ks[3], (N_LAYERS, HID, HID), dtype=jnp.float32) * s
        b_l = jnp.zeros((N_LAYERS, HID), dtype=jnp.float32)
        W_r = jax.random.normal(ks[4], (N_LAYERS, HID, HID), dtype=jnp.float32) * s
        W_e = jax.random.normal(ks[5], (N_LAYERS, HID, EDGE_DIM), dtype=jnp.float32) * se
        b_e = jnp.zeros((N_LAYERS, HID), dtype=jnp.float32)
        return {'x': x, 'edge_index': edge_index, 'edge_attr': edge_attr, 'W_l': W_l, 'b_l': b_l, 'W_r': W_r, 'W_e': W_e, 'b_e': b_e}
    _L2_gnn_all = _L2_gnn_setup()
    _L2_gnn_in = {k: v for k, v in _L2_gnn_all.items() if k in ('W_l', 'b_l', 'W_r', 'W_e', 'b_e')}
    del _L2_gnn_all

    def _L3_gnn_setup():
        import jax, jax.numpy as jnp
        import numpy as np
        N, DIM, K = (50000, 128, 9)
        FFN = 4 * DIM
        EPS = 1e-05

        def layer_norm(x, g, b):
            mu = jnp.mean(x, axis=-1, keepdims=True)
            var = jnp.mean(jnp.square(x - mu), axis=-1, keepdims=True)
            return (x - mu) * jax.lax.rsqrt(var + EPS) * g + b
        key = jax.random.key(seed)
        ks = jax.random.split(key, 12)
        E = N * K
        src = jax.random.randint(ks[0], (E,), 0, N)
        dst = jnp.repeat(jnp.arange(N), K)
        edge_index = jnp.stack([src, dst]).astype(jnp.int64)
        s = lambda k, shape, fan_in: jax.random.normal(k, shape, jnp.float32) / np.sqrt(fan_in)
        return {'x': jax.random.normal(ks[1], (N, DIM), jnp.float32), 'edge_index': edge_index, 'W_in_w': s(ks[2], (DIM, DIM), DIM), 'W_in_b': jnp.zeros((DIM,), jnp.float32), 'W_upd_w': s(ks[3], (2 * DIM, DIM), 2 * DIM), 'W_upd_b': jnp.zeros((DIM,), jnp.float32), 'W_out_w': s(ks[4], (DIM, DIM), DIM), 'W_out_b': jnp.zeros((DIM,), jnp.float32), 'ln1_g': jnp.ones((DIM,), jnp.float32), 'ln1_b': jnp.zeros((DIM,), jnp.float32), 'ln2_g': jnp.ones((DIM,), jnp.float32), 'ln2_b': jnp.zeros((DIM,), jnp.float32), 'ffn1_w': s(ks[5], (DIM, FFN), DIM), 'ffn1_b': jnp.zeros((FFN,), jnp.float32), 'ffn2_w': s(ks[6], (FFN, DIM), FFN), 'ffn2_b': jnp.zeros((DIM,), jnp.float32)}
    _L3_gnn_all = _L3_gnn_setup()
    _L3_gnn_in = {k: v for k, v in _L3_gnn_all.items() if k in ('W_in_w', 'W_in_b', 'W_upd_w', 'W_upd_b', 'W_out_w', 'W_out_b', 'ln1_g', 'ln1_b', 'ln2_g', 'ln2_b', 'ffn1_w', 'ffn1_b', 'ffn2_w', 'ffn2_b')}
    del _L3_gnn_all
    return {'x': x, 'src': src, 'dst': dst, 'edge_attr_32': edge_attr_32, 'L0_gnn_lin_w': _L0_gnn_in['lin_w'], 'L0_gnn_lin_b': _L0_gnn_in['lin_b'], 'L0_gnn_weight': _L0_gnn_in['weight'], 'L0_gnn_w_ih': _L0_gnn_in['w_ih'], 'L0_gnn_w_hh': _L0_gnn_in['w_hh'], 'L0_gnn_b_ih': _L0_gnn_in['b_ih'], 'L0_gnn_b_hh': _L0_gnn_in['b_hh'], 'L1_gnn_W1': _L1_gnn_in['W1'], 'L1_gnn_a1_src': _L1_gnn_in['a1_src'], 'L1_gnn_a1_dst': _L1_gnn_in['a1_dst'], 'L1_gnn_b1': _L1_gnn_in['b1'], 'L1_gnn_g1': _L1_gnn_in['g1'], 'L1_gnn_beta1': _L1_gnn_in['beta1'], 'L1_gnn_W2': _L1_gnn_in['W2'], 'L1_gnn_a2_src': _L1_gnn_in['a2_src'], 'L1_gnn_a2_dst': _L1_gnn_in['a2_dst'], 'L1_gnn_b2': _L1_gnn_in['b2'], 'L1_gnn_g2': _L1_gnn_in['g2'], 'L1_gnn_beta2': _L1_gnn_in['beta2'], 'L2_gnn_W_l': _L2_gnn_in['W_l'], 'L2_gnn_b_l': _L2_gnn_in['b_l'], 'L2_gnn_W_r': _L2_gnn_in['W_r'], 'L2_gnn_W_e': _L2_gnn_in['W_e'], 'L2_gnn_b_e': _L2_gnn_in['b_e'], 'L3_gnn_W_in_w': _L3_gnn_in['W_in_w'], 'L3_gnn_W_in_b': _L3_gnn_in['W_in_b'], 'L3_gnn_W_upd_w': _L3_gnn_in['W_upd_w'], 'L3_gnn_W_upd_b': _L3_gnn_in['W_upd_b'], 'L3_gnn_W_out_w': _L3_gnn_in['W_out_w'], 'L3_gnn_W_out_b': _L3_gnn_in['W_out_b'], 'L3_gnn_ln1_g': _L3_gnn_in['ln1_g'], 'L3_gnn_ln1_b': _L3_gnn_in['ln1_b'], 'L3_gnn_ln2_g': _L3_gnn_in['ln2_g'], 'L3_gnn_ln2_b': _L3_gnn_in['ln2_b'], 'L3_gnn_ffn1_w': _L3_gnn_in['ffn1_w'], 'L3_gnn_ffn1_b': _L3_gnn_in['ffn1_b'], 'L3_gnn_ffn2_w': _L3_gnn_in['ffn2_w'], 'L3_gnn_ffn2_b': _L3_gnn_in['ffn2_b']}

def reference(x, src, dst, edge_attr_32, L0_gnn_lin_w, L0_gnn_lin_b, L0_gnn_weight, L0_gnn_w_ih, L0_gnn_w_hh, L0_gnn_b_ih, L0_gnn_b_hh, L1_gnn_W1, L1_gnn_a1_src, L1_gnn_a1_dst, L1_gnn_b1, L1_gnn_g1, L1_gnn_beta1, L1_gnn_W2, L1_gnn_a2_src, L1_gnn_a2_dst, L1_gnn_b2, L1_gnn_g2, L1_gnn_beta2, L2_gnn_W_l, L2_gnn_b_l, L2_gnn_W_r, L2_gnn_W_e, L2_gnn_b_e, L3_gnn_W_in_w, L3_gnn_W_in_b, L3_gnn_W_upd_w, L3_gnn_W_upd_b, L3_gnn_W_out_w, L3_gnn_W_out_b, L3_gnn_ln1_g, L3_gnn_ln1_b, L3_gnn_ln2_g, L3_gnn_ln2_b, L3_gnn_ffn1_w, L3_gnn_ffn1_b, L3_gnn_ffn2_w, L3_gnn_ffn2_b):
    import jax
    import jax.numpy as jnp

    def _L0_gnn_ref(x, lin_w, lin_b, weight, w_ih, w_hh, b_ih, b_hh, edge_index):
        import jax, jax.numpy as jnp
        import numpy as np
        N = 3125
        E = 18750
        D_IN = 128
        D = 128
        L = 3

        def gru_cell(m, h, w_ih, w_hh, b_ih, b_hh):
            gi = m @ w_ih.T + b_ih
            gh = h @ w_hh.T + b_hh
            ir, iz, inn = jnp.split(gi, 3, axis=-1)
            hr, hz, hn = jnp.split(gh, 3, axis=-1)
            r = jax.nn.sigmoid(ir + hr)
            z = jax.nn.sigmoid(iz + hz)
            n = jnp.tanh(inn + r * hn)
            return (1.0 - z) * n + z * h
        h = x @ lin_w.T + lin_b
        src, dst = (edge_index[0], edge_index[1])
        n_nodes = h.shape[0]
        for i in range(weight.shape[0]):
            m = h @ weight[i]
            agg = jax.ops.segment_sum(m[src], dst, num_segments=n_nodes)
            h = gru_cell(agg, h, w_ih, w_hh, b_ih, b_hh)
        return h

    def _L1_gnn_ref(x, edge_index, W1, a1_src, a1_dst, b1, g1, beta1, W2, a2_src, a2_dst, b2, g2, beta2):
        import jax, jax.numpy as jnp
        import numpy as np
        N = 3125
        E = 50000
        IN = 128
        OUT = 128
        H = 4
        FH = OUT // H
        EPS = 1e-05
        NEG_SLOPE = 0.2

        def _gat(x, src, dst, W, a_src, a_dst, b):
            n = x.shape[0]
            xw = (x @ W).reshape(n, H, FH)
            al_s = jnp.einsum('nhf,hf->nh', xw, a_src)
            al_d = jnp.einsum('nhf,hf->nh', xw, a_dst)
            e = jax.nn.leaky_relu(al_s[src] + al_d[dst], NEG_SLOPE)
            m = jax.ops.segment_max(e, dst, num_segments=n)
            ee = jnp.exp(e - m[dst])
            den = jax.ops.segment_sum(ee, dst, num_segments=n)
            alpha = ee / den[dst]
            out = jax.ops.segment_sum(alpha[:, :, None] * xw[src], dst, num_segments=n)
            return out.reshape(n, H * FH) + b

        def _bn(x, gamma, beta):
            mu = x.mean(0)
            var = x.var(0)
            return gamma * (x - mu) * jax.lax.rsqrt(var + EPS) + beta
        n = x.shape[0]
        loops = jnp.arange(n, dtype=edge_index.dtype)
        src = jnp.concatenate([edge_index[0], loops])
        dst = jnp.concatenate([edge_index[1], loops])
        h = jax.nn.elu(_bn(_gat(x, src, dst, W1, a1_src, a1_dst, b1), g1, beta1))
        h = jax.nn.elu(_bn(_gat(h, src, dst, W2, a2_src, a2_dst, b2), g2, beta2))
        return h

    def _L2_gnn_ref(x, edge_index, edge_attr, W_l, b_l, W_r, W_e, b_e):
        import jax, jax.numpy as jnp
        import numpy as np
        N_NODES = 50000
        N_EDGES = 25000
        HID = 128
        EDGE_DIM = 32
        N_LAYERS = 2
        src = edge_index[0]
        dst = edge_index[1]
        n = x.shape[0]
        cnt = jax.ops.segment_sum(jnp.ones((src.shape[0],), dtype=x.dtype), dst, num_segments=n)
        inv_cnt = (1.0 / jnp.maximum(cnt, 1.0))[:, None]
        for l in range(N_LAYERS):
            msg = x[src] + jnp.einsum('ed,hd->eh', edge_attr, W_e[l]) + b_e[l]
            aggr = jax.ops.segment_sum(msg, dst, num_segments=n) * inv_cnt
            x = jax.nn.relu(jnp.einsum('nd,hd->nh', aggr, W_l[l]) + b_l[l] + jnp.einsum('nd,hd->nh', x, W_r[l]))
        return x

    def _L3_gnn_ref(x, edge_index, W_in_w, W_in_b, W_upd_w, W_upd_b, W_out_w, W_out_b, ln1_g, ln1_b, ln2_g, ln2_b, ffn1_w, ffn1_b, ffn2_w, ffn2_b):
        import jax, jax.numpy as jnp
        import numpy as np
        N, DIM, K = (50000, 128, 9)
        FFN = 4 * DIM
        EPS = 1e-05

        def layer_norm(x, g, b):
            mu = jnp.mean(x, axis=-1, keepdims=True)
            var = jnp.mean(jnp.square(x - mu), axis=-1, keepdims=True)
            return (x - mu) * jax.lax.rsqrt(var + EPS) * g + b
        src, dst = (edge_index[0], edge_index[1])
        n = x.shape[0]
        h = x @ W_in_w + W_in_b
        diff = h[src] - h[dst]
        seg_max = jax.ops.segment_max(diff, dst, num_segments=n)
        counts = jax.ops.segment_sum(jnp.ones_like(dst, jnp.int32), dst, num_segments=n)
        max_diff = jnp.where((counts > 0)[:, None], seg_max, 0.0)
        h = jnp.concatenate([h, max_diff], axis=-1) @ W_upd_w + W_upd_b
        h = h @ W_out_w + W_out_b
        x = layer_norm(x + h, ln1_g, ln1_b)
        f = jax.nn.gelu(x @ ffn1_w + ffn1_b, approximate=False) @ ffn2_w + ffn2_b
        return layer_norm(x + f, ln2_g, ln2_b)
    edge_index = jnp.stack([src, dst])
    x = _layernorm(x + _L0_gnn_ref(x, L0_gnn_lin_w, L0_gnn_lin_b, L0_gnn_weight, L0_gnn_w_ih, L0_gnn_w_hh, L0_gnn_b_ih, L0_gnn_b_hh, edge_index), axis=-1)
    x = _layernorm(x + _L1_gnn_ref(x, edge_index, L1_gnn_W1, L1_gnn_a1_src, L1_gnn_a1_dst, L1_gnn_b1, L1_gnn_g1, L1_gnn_beta1, L1_gnn_W2, L1_gnn_a2_src, L1_gnn_a2_dst, L1_gnn_b2, L1_gnn_g2, L1_gnn_beta2), axis=-1)
    x = _layernorm(x + _L2_gnn_ref(x, edge_index, edge_attr_32, L2_gnn_W_l, L2_gnn_b_l, L2_gnn_W_r, L2_gnn_W_e, L2_gnn_b_e), axis=-1)
    x = _layernorm(x + _L3_gnn_ref(x, edge_index, L3_gnn_W_in_w, L3_gnn_W_in_b, L3_gnn_W_upd_w, L3_gnn_W_upd_b, L3_gnn_W_out_w, L3_gnn_W_out_b, L3_gnn_ln1_g, L3_gnn_ln1_b, L3_gnn_ln2_g, L3_gnn_ln2_b, L3_gnn_ffn1_w, L3_gnn_ffn1_b, L3_gnn_ffn2_w, L3_gnn_ffn2_b), axis=-1)
    return x

_drawn_inputs = setup_inputs


def setup_inputs(seed=0):
    import zlib

    import numpy as np

    out = dict(_drawn_inputs(seed))
    spreads = {'L0_gnn_lin_b': (0.0, 0.1),
     'L0_gnn_b_ih': (0.0, 0.1),
     'L0_gnn_b_hh': (0.0, 0.1),
     'L1_gnn_b1': (0.0, 2.0),
     'L1_gnn_g1': (1.0, 0.2),
     'L1_gnn_beta1': (0.0, 0.31),
     'L1_gnn_b2': (0.0, 2.0),
     'L1_gnn_g2': (1.0, 0.2),
     'L1_gnn_beta2': (0.0, 0.1),
     'L2_gnn_b_l': (0.0, 0.1),
     'L2_gnn_b_e': (0.0, 0.1),
     'L3_gnn_W_in_b': (0.0, 0.1),
     'L3_gnn_W_upd_b': (0.0, 0.1),
     'L3_gnn_W_out_b': (0.0, 0.1),
     'L3_gnn_ln1_g': (1.0, 0.2),
     'L3_gnn_ln1_b': (0.0, 0.1),
     'L3_gnn_ln2_g': (1.0, 0.2),
     'L3_gnn_ln2_b': (0.0, 0.1),
     'L3_gnn_ffn1_b': (0.0, 0.1),
     'L3_gnn_ffn2_b': (0.0, 0.1)}
    factors = {'L1_gnn_a1_dst': 10.503, 'L1_gnn_a2_dst': 18.972}
    for name, (base, spread) in spreads.items():
        noise = np.random.default_rng([zlib.crc32(name.encode()), seed]).standard_normal(out[name].shape)
        drawn = base * np.exp(spread * noise) if base else spread * noise
        out[name] = jnp.asarray(drawn.astype(out[name].dtype))
    for name, factor in factors.items():
        out[name] = (out[name] * factor).astype(out[name].dtype)
    return out
```

```python
from contextlib import ExitStack

import concourse.bass as bass
from concourse import mybir

F32 = mybir.dt.float32
BF16 = mybir.dt.bfloat16
I32 = mybir.dt.int32
ALU = mybir.AluOpType
ACT = mybir.ActivationFunctionType
AX = mybir.AxisListType

P = 128
D = 128
N = 50000
E = 25000
ED = 32
HEADS = 4
FH = D // HEADS
HW = FH + 1
GW = HEADS * HW
GT = GW + HEADS
FFN = 4 * D

STEP = 2 * P
U = 4
GROUPS = -(-N // (STEP * U))
STEPS = GROUPS * U
NP = STEPS * STEP
LAST = (N - (STEPS - 1) * STEP) // 2

PSEUDO = 32
NEW = P - 1
TILES = -(-E // (NEW * U)) * U
NAT = -(-E // (P * U)) * U
PAD = 25600
OUTSIDE = 1.0e6
BIG = 1.0e30
EPS = 1e-5

assert STEPS * STEP >= N and (STEPS - 1) * STEP < N and N % 2 == 0


def wait(eng, sem, value):
    if isinstance(value, int) and value <= 0:
        return
    eng.wait_ge(sem, value)


def turns(eng, n):
    yield 0, False
    with eng.Fori(1, n - 1) as k:
        yield k, False
    yield n - 1, True


def pipeline(eng, n, dist, ahead, main):
    for j in range(dist):
        ahead(0, j)
    for k, last in turns(eng, n):
        for j in range(U):
            if not last or j + dist < U:
                ahead(k + (j + dist) // U, (j + dist) % U)
            main(k, j)


class Link:

    def __init__(self, eng, sem, per_step):
        self.eng, self.sem, self.per_step, self.n, self.base = eng, sem, per_step, 0, 0

    def begin(self, step):
        assert self.n in (0, self.per_step), self.n
        self.base, self.n = step * self.per_step, 0

    def __call__(self, ins):
        ins.then_inc(self.sem, 1)
        self.n += 1
        self.eng.wait_ge(self.sem, self.base + self.n)


class Stage:

    def __init__(self, nc, name):
        self.nc, self.name, self.ctx, self.sems = nc, name, ExitStack(), []

    def __enter__(self):
        self.ctx.__enter__()
        return self

    def sb(self, name, shape, dt=F32):
        return self.ctx.enter_context(self.nc.sbuf_tensor(f"{self.name}_{name}", shape, dt))

    def bank(self, name, shape=(P, 512)):
        return self.ctx.enter_context(self.nc.psum_tensor(f"{self.name}_{name}", list(shape), F32))

    def sem(self, name):
        s = self.nc.alloc_semaphore(name=f"{self.name}_{name}")
        self.sems.append(s)
        return s

    def block(self):
        return self.ctx.enter_context(self.nc.Block())

    def __exit__(self, *exc):
        self.ctx.__exit__(*exc)
        if exc[0] is None:
            self.nc.clear_and_free_semaphores(self.sems)
            self.nc.all_engine_barrier()


def rows(table, step, width):
    return table[bass.ds(step * STEP, STEP), 0:width].rearrange("(p j) d -> p j d", j=2)




def prepare_weights(nc, A, C):
    with Stage(nc, "prep") as st:
        gw = st.sb("gw", [P, 3, D])
        wih = st.sb("wih", [P, 3 * D])
        g1 = st.sb("g1", [P, 2, D])
        a_blk = st.sb("a_blk", [P, 2, 8])
        web = st.sb("web", [P, 2, ED + 1])
        updT = st.sb("updT", [P, 2 * D])
        wout = st.sb("wout", [P, D])
        bupd = st.sb("bupd", [P, 1])
        brow = st.sb("brow", [1, C.NB])
        bmore = st.sb("bmore", [1, 2 * D])
        bout = st.sb("bout", [1, D])
        parts = st.sb("parts", [1, 3, C.NB], BF16)
        rest = st.sb("rest", [1, C.NB])
        acc = [st.bank(f"acc{i}") for i in range(8)]
        loaded, blocks_zero, placed = st.sem("loaded"), st.sem("blocks_zero"), st.sem("placed")
        ident0 = st.sem("ident0")
        ones_set = st.sem("ones_set")
        made, copied, own = st.sem("made"), st.sem("copied"), st.sem("own")
        parts_out, parts_in, split = st.sem("parts_out"), st.sem("parts_in"), st.sem("split")
        block = st.block()
        loads = [
            (gw[:, :, :], A["gru_wT"].rearrange("l m k -> m l k")),
            (wih[:, 0:D], A["w_ihT"][:, 2 * D:3 * D]), (wih[:, D:3 * D], A["w_ihT"][:, 0:2 * D]),
            (C.whh[:, :], A["w_hhT"]), (C.lin[:, :], A["lin_wT"]),
            (g1[:, 0, :], A["gat_W1T"]), (g1[:, 1, :], A["gat_W2T"]),
            (C.gat[:, 0, 0:D], A["gat_W1"]), (C.gat[:, 1, 0:D], A["gat_W2"]),
            (web[:, :, 0:ED], A["W_e"].rearrange("l h d -> h l d")),
            (web[:, :, ED:ED + 1], A["b_e"].rearrange("l (h o) -> h l o", o=1)),
            (C.wl[:, :, :], A["W_lT"].rearrange("l d h -> d l h")),
            (C.wr[:, :, :], A["W_rT"].rearrange("l d h -> d l h")),
            (C.win[:, :], A["W_in_w"]), (updT[:, :], A["W_updT"]), (wout[:, :], A["W_out_w"]),
            (bupd[:, :], A["W_upd_b"].rearrange("(p o) -> p o", o=1)),
            (C.ffn1[:, :], A["ffn1_w"]),
            (C.ffn2[:, :, :], A["ffn2_w"].rearrange("(b p) n -> p b n", p=P)),
            (C.ffn1_b[:, :], A["ffn1_b"].rearrange("(b p) -> p b", p=P)),
            (brow[:, C.B_LIN:C.B_LIN + D], A["lin_b"]),
            (brow[:, C.B_GRU:C.B_GRU + D], A["b_ih"][:, 2 * D:3 * D]),
            (brow[:, C.B_GRU + D:C.B_GRU + 3 * D], A["b_ih"][:, 0:2 * D]),
            (brow[:, C.B_GRU + 3 * D:C.B_GRU + 4 * D], A["b_hh"][:, 2 * D:3 * D]),
            (bmore[:, :], A["b_hh"][:, 0:2 * D]),
            (brow[:, C.B_L:C.B_L + 2 * D], A["b_l"]),
            (brow[:, C.B_IN:C.B_IN + D], A["W_in_b"]),
            (bout[:, :], A["W_out_b"]),
            (brow[:, C.B_F2:C.B_F2 + D], A["ffn2_b"]),
        ]
        for i, name in enumerate(C.BC):
            loads.append((C.bc[:, i, :], A[name].partition_broadcast(P)))
        n_loads = len(loads)

        @block.sync
        def _(sp):
            for out, in_ in loads:
                sp.dma_start(out, in_, allow_slow_non_contiguous=True).then_inc(loaded, 16)
            sp.wait_ge(blocks_zero, 1)
            for layer in range(2):
                for which, name in enumerate(("src", "dst")):
                    for h in range(HEADS):
                        src = A[f"a{layer + 1}_{name}"][h:h + 1, :].rearrange("o f -> f o")
                        sp.dma_start(a_blk[h * FH:(h + 1) * FH, layer, 4 * which + h:4 * which + h + 1],
                                     src, allow_slow_non_contiguous=True).then_inc(placed, 16)
            sp.wait_ge(split, 1)
            sp.dma_start(C.bias_dram.rearrange("(o a) n -> o a n", o=1), parts[:, :, :]).then_inc(parts_out, 16)
            sp.wait_ge(parts_out, 16)
            sp.dma_start(C.bias[:, :], C.bias_dram).then_inc(parts_in, 16)
            sp.wait_ge(parts_in, 16)
            sp.wait_ge(loaded, 16 * n_loads)

        @block.gpsimd
        def _(pool):
            pool.memset(C.ident[:, :], 0.0).then_inc(ident0, 1)
            pool.wait_ge(ident0, 1)
            pool.affine_select(out=C.ident[:, :], in_=C.ident[:, :], compare_op=ALU.not_equal, fill=1.0,
                               base=0, pattern=[[-1, P]], channel_multiplier=1).then_inc(ones_set, 1)
            pool.memset(C.ones[:, :], 1.0).then_inc(ones_set, 1)
            pool.memset(C.ones3[:, :], 1.0).then_inc(ones_set, 1)
            pool.memset(C.minus_half[:, :], -0.5).then_inc(ones_set, 1)

        @block.tensor
        def _(pe):
            pe.wait_ge(loaded, 16 * n_loads)
            pe.wait_ge(placed, 16 * 16)
            for i in range(3):
                pe.matmul(acc[i][:, 0:3 * D], gw[:, i, :], wih[:, :], start=True, stop=True)
            for i in range(2):
                pe.matmul(acc[3][:, 8 * i:8 * i + 8], g1[:, i, :], a_blk[:, i, :], start=True, stop=True)
            for i in range(2):
                pe.matmul(acc[4][0:ED + 1, i * D:(i + 1) * D], web[:, i, :], C.wl[:, i, :], start=True, stop=True)
            for i in range(2):
                pe.matmul(acc[5][:, i * D:(i + 1) * D], updT[:, i * D:(i + 1) * D], wout[:, :], start=True, stop=True)
            pe.matmul(acc[6][0:1, 0:D], bupd[:, :], wout[:, :], start=True, stop=True).then_inc(made, 1)

        @block.vector
        def _(dve):
            dve.memset(a_blk[:, :, :], 0.0).then_inc(blocks_zero, 1)
            dve.wait_ge(made, 1)
            for i in range(3):
                dve.tensor_copy(C.wc[:, i, :], acc[i][:, 0:3 * D]).then_inc(copied, 1)
            dve.tensor_copy(C.gat[:, :, D:D + 8], acc[3][:, 0:16].rearrange("p (l c) -> p l c", l=2)).then_inc(copied, 1)
            dve.tensor_copy(C.wel[:, :, :], acc[4][0:ED + 1, 0:2 * D].rearrange("p (l c) -> p l c", l=2)).then_inc(copied, 1)
            dve.tensor_copy(C.wf[:, :, :], acc[5][:, 0:2 * D].rearrange("p (l c) -> p l c", l=2)).then_inc(copied, 1)
            dve.tensor_tensor(brow[:, C.B_F:C.B_F + D], acc[6][0:1, 0:D], bout[:, :], ALU.add).then_inc(copied, 1)
            g = slice(C.B_GRU + D, C.B_GRU + 3 * D)
            dve.tensor_tensor(brow[:, g], brow[:, g], bmore[:, :], ALU.add).then_inc(copied, 1)
            dve.wait_ge(copied, 8)
            link = Link(dve, own, 4)
            link.begin(0)
            link(dve.tensor_copy(parts[:, 0, :], brow[:, :]))
            link(dve.tensor_tensor(rest[:, :], brow[:, :], parts[:, 0, :], ALU.subtract))
            link(dve.tensor_copy(parts[:, 1, :], rest[:, :]))
            link(dve.tensor_tensor(rest[:, :], rest[:, :], parts[:, 1, :], ALU.subtract))
            dve.tensor_copy(parts[:, 2, :], rest[:, :]).then_inc(split, 1)




def prepare_edges(nc, A, C):
    with Stage(nc, "pads") as st:
        ints = st.sb("ints", [125, 3, 200], I32)
        vals = st.sb("vals", [125, 3, 200])
        edge = st.sb("edge", [1, 3, 601])
        loaded, numbered, filled, turned, stored = (st.sem(n) for n in ("loaded", "numbered", "filled", "turned", "stored"))
        block = st.block()

        @block.sync
        def _(sp):
            sp.dma_start(ints[:, 0, :], A["src"].rearrange("(p c) -> p c", c=200)).then_inc(loaded, 16)
            sp.dma_start(ints[:, 1, :], A["dst"].rearrange("(p c) -> p c", c=200)).then_inc(loaded, 16)
            sp.wait_ge(filled, 4)
            for i in range(3):
                sp.dma_start(C.pad[i:i + 1, 0:1], edge[:, i, 0:1]).then_inc(stored, 16)
                sp.dma_start(C.pad[i:i + 1, E + 1:PAD], edge[:, i, 1:PAD - E]).then_inc(stored, 16)
            sp.wait_ge(turned, 1)
            for i in range(3):
                sp.dma_start(C.pad[i, 1:E + 1].rearrange("(p c) -> p c", c=200), vals[:, i, :]).then_inc(stored, 16)
            sp.wait_ge(stored, 16 * 9)

        @block.gpsimd
        def _(pool):
            pool.iota(ints[:, 2, :], pattern=[[1, 200]], base=0, channel_multiplier=200).then_inc(numbered, 1)

        @block.vector
        def _(dve):
            dve.memset(edge[:, 0, :], 0.0).then_inc(filled, 1)
            dve.memset(edge[:, 2, :], 0.0).then_inc(filled, 1)
            dve.memset(edge[:, 1, 0:1], -1.0).then_inc(filled, 1)
            dve.memset(edge[:, 1, 1:], OUTSIDE).then_inc(filled, 1)
            dve.wait_ge(loaded, 32)
            dve.wait_ge(numbered, 1)
            dve.tensor_copy(vals[:, :, :], ints[:, :, :]).then_inc(turned, 1)

    with Stage(nc, "lists") as st:
        t_src, t_dst, t_num, t_nxt, t_put = (st.sb(n, [P, 2, P]) for n in ("src", "dst", "num", "nxt", "put"))
        n_src, n_dst, n_nxt, n_prv, n_put, n_bias = (st.sb(n, [P, 2, P]) for n in ("nsrc", "ndst", "nnxt", "nprv", "nput", "nbias"))
        tps = [st.bank(f"tps{i}") for i in range(4)]
        loaded, own, ready, turned, stored, spread, done = (
            st.sem(n) for n in ("loaded", "own", "ready", "turned", "stored", "spread", "done"))
        block = st.block()
        sizes = [(0, P), (1, TILES - P)]
        nat_sizes = [(0, P), (1, NAT - P)]

        def load(sp, out, i, first, rowlen, n, b, c0, c1):
            at = 1 + first + b * P * rowlen
            src = C.pad[i, at:at + n * rowlen].rearrange("(t q) -> t q", q=rowlen)
            sp.dma_start(out[0:n, b, c0:c1], src[:, 0:c1 - c0], allow_slow_non_contiguous=True).then_inc(loaded, 16)
            return 1

        @block.sync
        def _(sp):
            n_loads = 0
            for b, n in sizes:
                for out, i, off in ((t_src, 0, 0), (t_dst, 1, 0), (t_num, 2, 0), (t_nxt, 1, 1)):
                    n_loads += load(sp, out, i, off + NEW - 1, NEW, n, b, 0, 1)
                    n_loads += load(sp, out, i, off, NEW, n, b, 1, PSEUDO)
                    n_loads += load(sp, out, i, off - 1, NEW, n, b, PSEUDO, PSEUDO + 1)
                    n_loads += load(sp, out, i, off + PSEUDO - 1, NEW, n, b, PSEUDO + 1, P)
            for b, n in nat_sizes:
                for out, i, off in ((n_src, 0, 0), (n_dst, 1, 0), (n_nxt, 1, 1), (n_prv, 1, -1)):
                    n_loads += load(sp, out, i, off, P, n, b, 0, P)
            assert n_loads == N_LIST_LOADS
            sp.wait_ge(loaded, 16 * n_loads)
            for b, n in sizes:
                sp.dma_start(C.dst_row[0, b * P * P:(b * P + n) * P].rearrange("(t q) -> t q", q=P),
                             t_dst[0:n, b, :]).then_inc(stored, 16)
            sp.wait_ge(ready, 1)
            for b, n in nat_sizes:
                sp.dma_start(C.bias_row[0, b * P * P:(b * P + n) * P].rearrange("(t q) -> t q", q=P),
                             n_bias[0:n, b, :]).then_inc(stored, 16)
            sp.wait_ge(stored, 64)
            sp.dma_start(C.targets[:, :], C.dst_row[0:1, :].partition_broadcast(P)).then_inc(spread, 16)
            sp.wait_ge(spread, 16)

        @block.vector
        def _(dve):
            link = Link(dve, own, 3 * 4 + 1 + 4)
            link.begin(0)
            dve.wait_ge(loaded, 16 * N_LIST_LOADS)
            for dst, nxt, put, sz in ((t_dst, t_nxt, t_put, sizes), (n_dst, n_nxt, n_put, nat_sizes)):
                for b, n in sz:
                    v = lambda x: x[0:n, b, :]
                    link(dve.tensor_tensor(v(nxt), v(dst), v(nxt), ALU.not_equal))
                    link(dve.scalar_tensor_tensor(out=v(put), in0=v(dst), scalar=-OUTSIDE, in1=v(nxt), op0=ALU.add, op1=ALU.mult))
                    link(dve.tensor_scalar(v(put), v(put), OUTSIDE, None, ALU.add))
            link(dve.memset(t_put[:, :, PSEUDO:PSEUDO + 1], OUTSIDE))
            for b, n in nat_sizes:
                link(dve.tensor_tensor(n_prv[0:n, b, :], n_dst[0:n, b, :], n_prv[0:n, b, :], ALU.is_equal))
                link(dve.tensor_scalar(n_bias[0:n, b, :], n_prv[0:n, b, :], BIG, -BIG, ALU.mult, ALU.add))
            dve.memset(n_prv[:, :, :], 0.0).then_inc(ready, 1)
            dve.wait_ge(turned, 1)
            for b, n in sizes:
                dve.tensor_copy(C.lists[:, b * P:b * P + n, :],
                                tps[b][:, :].rearrange("p (c t) -> p t c", c=4)[:, 0:n, :]).then_inc(done, 1)
            for b, n in nat_sizes:
                dve.tensor_copy(C.nat_lists[:, b * P:b * P + n, :],
                                tps[2 + b][:, 0:2 * P].rearrange("p (c t) -> p t c", c=2)[:, 0:n, :]).then_inc(done, 1)

        @block.tensor
        def _(pe):
            pe.wait_ge(ready, 1)
            for b, n in sizes:
                for c, x in enumerate((t_src, t_put, t_num, t_dst)):
                    pe.transpose(tps[b][:, c * P:c * P + n], x[0:n, b, :], C.ident[0:n, 0:n])
            for b, n in nat_sizes:
                for c, x in enumerate((n_src, n_put)):
                    last = pe.transpose(tps[2 + b][:, c * P:c * P + n], x[0:n, b, :], C.ident[0:n, 0:n])
            last.then_inc(turned, 1)


N_LIST_LOADS = 2 * 4 * 4 + 2 * 4


def clear_tables(nc, C, tables):
    with Stage(nc, "clear") as st:
        zeros = st.sb("zeros", [P, 8 * GT])
        lows = st.sb("lows", [P, 8, GT])
        filled, own, stored = st.sem("filled"), st.sem("own"), st.sem("stored")
        block = st.block()
        per = NP // P

        @block.sync
        def _(sp):
            sp.wait_ge(filled, 2)
            n = 0
            for table, width, low in tables:
                v = table.rearrange("(p r) d -> p r d", p=P)
                src = lows[:, :, :] if low else zeros[:, 0:8 * width].rearrange("p (r d) -> p r d", r=8)
                for r in range(0, per, 8):
                    sp.dma_start(v[:, r:r + 8, :], src).then_inc(stored, 16)
                    n += 1
            sp.wait_ge(stored, 16 * n)

        @block.vector
        def _(dve):
            dve.memset(zeros[:, :], 0.0).then_inc(filled, 1)
            dve.memset(lows[:, :, 0:GW], 0.0).then_inc(own, 1)
            dve.wait_ge(own, 1)
            dve.memset(lows[:, :, GW:GT], -BIG).then_inc(filled, 1)




def sum_edges(nc, C, name, table, width, sums, ones=False):
    total = width + ones
    first = 1 if ones else 0
    g_col, p_col = (1, 0) if ones else (0, 1)
    with Stage(nc, name) as st:
        msg = [st.sb(f"msg{j}", [P, total]) for j in range(U)]
        sel = [st.sb(f"sel{j}", [P, P]) for j in range(U)]
        out = [st.sb(f"out{j}", [P, total]) for j in range(U)]
        ids = [st.sb(f"ids{j}", [P, 2], I32) for j in range(U)]
        acc = [st.bank(f"acc{j}") for j in range(U)]
        listed, selected, carried, summed, copied, zeroed, issued = (
            st.sem(n) for n in ("listed", "selected", "carried", "summed", "copied", "zeroed", "issued"))
        gathered = [st.sem(f"gathered{j}") for j in range(U)]
        put = [st.sem(f"put{j}") for j in range(U)]
        block = st.block()
        n_turns = TILES // U

        @block.vector
        def _(dve):
            for j in range(U):
                if ones:
                    dve.memset(msg[j][:, :], 1.0).then_inc(zeroed, 1)
                dve.memset(out[j][:, :], 0.0).then_inc(zeroed, 1)
            for k, _ in turns(dve, n_turns):
                for j in range(U):
                    t = U * k + j
                    wait(dve, put[j], 16 * k)
                    dve.tensor_copy(ids[j][:, :], C.lists[:, bass.ds(t, 1), first:first + 2].rearrange("p o c -> p (o c)")).then_inc(listed, 1)
                    wait(dve, summed, t - U + 1)
                    dve.tensor_scalar(sel[j][:, :], C.targets[:, bass.ds(t * P, P)],
                                      C.lists[:, bass.ds(t, 1), 3:4].rearrange("p o c -> p (o c)"), None, ALU.is_equal).then_inc(selected, 1)

        @block.gpsimd
        def _(pool):
            pool.wait_ge(zeroed, U * (1 + ones))

            def gather(k, j):
                t = U * k + j
                wait(pool, listed, t + 1)
                wait(pool, summed, t - U + 1)
                pool.sem_inc(issued, 1)
                pool.indirect_dma_start(out=msg[j][:, 0:width], out_offset=None, in_=table,
                                        in_offset=bass.IndirectOffsetOnAxis(ap=ids[j][:, g_col:g_col + 1], axis=0),
                                        bounds_check=table.shape[0] - 1, oob_is_err=False).then_inc(gathered[j], 16)

            def scatter(k, j):
                wait(pool, copied, U * k + j + 1)
                pool.sem_inc(issued, 1)
                pool.indirect_dma_start(out=sums, out_offset=bass.IndirectOffsetOnAxis(ap=ids[j][:, p_col:p_col + 1], axis=0),
                                        in_=out[j][:, :], in_offset=None,
                                        bounds_check=NP - 1, oob_is_err=False).then_inc(put[j], 16)

            pipeline(pool, n_turns, 3, gather, scatter)
            for j in range(U):
                pool.wait_ge(put[j], 16 * n_turns)

        @block.scalar
        def _(act):
            act.wait_ge(zeroed, U * (1 + ones))
            for k, _ in turns(act, n_turns):
                for j in range(U):
                    t = U * k + j
                    act.wait_ge(gathered[j], 16 * (k + 1))
                    wait(act, copied, t)
                    act.activation(msg[j][PSEUDO:PSEUDO + 1, :], out[(j - 1) % U][0:1, :], ACT.Copy).then_inc(carried, 1)
                    act.wait_ge(summed, t + 1)
                    wait(act, put[j], 16 * k)
                    act.activation(out[j][:, :], acc[j][:, 0:total], ACT.Copy).then_inc(copied, 1)

        @block.tensor
        def _(pe):
            for k, _ in turns(pe, n_turns):
                for j in range(U):
                    t = U * k + j
                    pe.wait_ge(selected, t + 1)
                    pe.wait_ge(carried, t + 1)
                    wait(pe, copied, t - U + 1)
                    pe.matmul(acc[j][:, 0:total], sel[j][:, :], msg[j][:, :], start=True, stop=True).then_inc(summed, 1)


def max_edges(nc, C, name, table, maxima):
    with Stage(nc, name) as st:
        msg = [st.sb(f"msg{j}", [P, D]) for j in range(U)]
        run = [st.sb(f"run{j}", [P, P]) for j in range(U)]
        out = [st.sb(f"out{j}", [P, D]) for j in range(U)]
        ids = [st.sb(f"ids{j}", [P, 2], I32) for j in range(U)]
        turned_ps = [st.bank(f"turned{i}") for i in range(2)]
        back_ps = [st.bank(f"back{i}") for i in range(2)]
        biased, listed, turned, scanned, back, copied, issued, low = (
            st.sem(n) for n in ("biased", "listed", "turned_", "scanned", "back_", "copied", "issued", "low"))
        gathered = [st.sem(f"gathered{j}") for j in range(U)]
        put = [st.sem(f"put{j}") for j in range(U)]
        block = st.block()
        n_turns = NAT // U
        bias = C.targets

        @block.sync
        def _(sp):
            sp.dma_start(bias[:, 0:NAT * P], C.bias_row[0:1, :].partition_broadcast(P)).then_inc(biased, 16)

        @block.gpsimd
        def _(pool):
            def gather(k, j):
                t = U * k + j
                wait(pool, listed, t + 1)
                wait(pool, turned, t - U + 1)
                pool.sem_inc(issued, 1)
                pool.indirect_dma_start(out=msg[j][:, :], out_offset=None, in_=table,
                                        in_offset=bass.IndirectOffsetOnAxis(ap=ids[j][:, 0:1], axis=0),
                                        bounds_check=NP - 1, oob_is_err=False).then_inc(gathered[j], 16)

            def scatter(k, j):
                wait(pool, copied, U * k + j + 1)
                pool.sem_inc(issued, 1)
                pool.indirect_dma_start(out=maxima, out_offset=bass.IndirectOffsetOnAxis(ap=ids[j][:, 1:2], axis=0),
                                        in_=out[j][:, :], in_offset=None,
                                        bounds_check=NP - 1, oob_is_err=False).then_inc(put[j], 16)

            pipeline(pool, n_turns, 3, gather, scatter)
            for j in range(U):
                pool.wait_ge(put[j], 16 * n_turns)

        @block.vector
        def _(dve):
            dve.memset(run[U - 1][:, :], -BIG).then_inc(low, 1)
            dve.wait_ge(low, 1)
            dve.wait_ge(biased, 16)

            def indices(k, j):
                wait(dve, put[j], 16 * k)
                dve.tensor_copy(ids[j][:, :], C.nat_lists[:, bass.ds(U * k + j, 1), :].rearrange("p o c -> p (o c)")).then_inc(listed, 1)

            def scan(k, j):
                t = U * k + j
                dve.wait_ge(turned, t + 1)
                wait(dve, scanned, t)
                wait(dve, back, t - U + 1)
                dve.tensor_tensor_scan(run[j][:, :], bias[:, bass.ds(t * P, P)], turned_ps[j % 2][:, 0:P],
                                       run[(j - 1) % U][:, P - 1:P], ALU.add, ALU.max).then_inc(scanned, 1)

            pipeline(dve, n_turns, 3, indices, scan)

        @block.tensor
        def _(pe):
            def turn(k, j):
                t = U * k + j
                pe.wait_ge(gathered[j], 16 * (k + 1))
                wait(pe, scanned, t - 1)
                pe.transpose(turned_ps[j % 2][:, 0:P], msg[j][:, :], C.ident[:, :]).then_inc(turned, 1)

            def turn_back(k, j):
                t = U * k + j
                pe.wait_ge(scanned, t + 1)
                wait(pe, copied, t - 1)
                pe.transpose(back_ps[j % 2][:, 0:D], run[j][:, :], C.ident[:, :]).then_inc(back, 1)

            pipeline(pe, n_turns, 1, turn, turn_back)

        @block.scalar
        def _(act):
            for k, _ in turns(act, n_turns):
                for j in range(U):
                    act.wait_ge(back, U * k + j + 1)
                    wait(act, put[j], 16 * k)
                    act.activation(out[j][:, :], back_ps[j % 2][:, 0:D], ACT.Copy).then_inc(copied, 1)


def attend_edges(nc, C, name, table, dst_logits, result):
    with Stage(nc, name) as st:
        msg = [st.sb(f"msg{j}", [P, GT]) for j in range(U)]
        ald = [st.sb(f"ald{j}", [P, HEADS]) for j in range(U)]
        sel = [st.sb(f"sel{j}", [P, P]) for j in range(U)]
        low = [st.sb(f"low{j}", [P, P]) for j in range(U)]
        logit = [st.sb(f"logit{j}", [P, HEADS]) for j in range(U)]
        masked = [st.sb(f"masked{j}", [P, HEADS, P]) for j in range(2)]
        wgt = [st.sb(f"wgt{j}", [P, HEADS]) for j in range(U)]
        out = [st.sb(f"out{j}", [P, GT]) for j in range(U)]
        ids = [st.sb(f"ids{j}", [P, 2], I32) for j in range(U)]
        idd = [st.sb(f"idd{j}", [P, 1], I32) for j in range(U)]
        spread_ps = [st.bank(f"spread{i}") for i in range(2)]
        acc = [st.bank(f"acc{i}") for i in range(2)]
        zeroed, listed, selected, own, issued = (st.sem(n) for n in ("zeroed", "listed", "selected", "own", "issued"))
        blend, spread, peak, weight, weighed, carried, message, summed, copied = (
            st.sem(n) for n in ("blend", "spread_", "peak", "weight", "weighed", "carried", "message", "summed", "copied"))
        gathered = [st.sem(f"gathered{j}") for j in range(U)]
        put = [st.sem(f"put{j}") for j in range(U)]
        block = st.block()
        n_turns = TILES // U

        @block.gpsimd
        def _(pool):
            def gather(k, j):
                t = U * k + j
                wait(pool, listed, t + 1)
                wait(pool, message, t - U + 1)
                pool.sem_inc(issued, 1)
                pool.indirect_dma_start(out=msg[j][:, :], out_offset=None, in_=table,
                                        in_offset=bass.IndirectOffsetOnAxis(ap=ids[j][:, 0:1], axis=0),
                                        bounds_check=NP - 1, oob_is_err=False).then_inc(gathered[j], 16)
                pool.indirect_dma_start(out=ald[j][:, :], out_offset=None, in_=dst_logits,
                                        in_offset=bass.IndirectOffsetOnAxis(ap=idd[j][:, 0:1], axis=0),
                                        bounds_check=NP - 1, oob_is_err=False).then_inc(gathered[j], 16)

            def scatter(k, j):
                wait(pool, copied, U * k + j + 1)
                pool.sem_inc(issued, 1)
                pool.indirect_dma_start(out=result, out_offset=bass.IndirectOffsetOnAxis(ap=ids[j][:, 1:2], axis=0),
                                        in_=out[j][:, :], in_offset=None,
                                        bounds_check=NP - 1, oob_is_err=False).then_inc(put[j], 16)

            pool.wait_ge(zeroed, 2 * U)
            pipeline(pool, n_turns, 3, gather, scatter)
            for j in range(U):
                pool.wait_ge(put[j], 16 * n_turns)

        @block.vector
        def _(dve):
            link = Link(dve, own, 3)
            for j in range(U):
                dve.memset(out[j][:, :], 0.0).then_inc(zeroed, 1)
                dve.memset(ald[j][:, :], 0.0).then_inc(zeroed, 1)
            dve.wait_ge(zeroed, 2 * U)

            def select(k, j):
                t = U * k + j
                wait(dve, put[j], 16 * k)
                dve.tensor_copy(ids[j][:, :], C.lists[:, bass.ds(t, 1), 0:2].rearrange("p o c -> p (o c)"))
                dve.tensor_scalar(idd[j][:, :], C.lists[:, bass.ds(t, 1), 3:4].rearrange("p o c -> p (o c)"),
                                  0.0, None, ALU.max).then_inc(listed, 1)
                wait(dve, summed, t - U + 1)
                dve.tensor_scalar(sel[j][:, :], C.targets[:, bass.ds(t * P, P)],
                                  C.lists[:, bass.ds(t, 1), 3:4].rearrange("p o c -> p (o c)"), None, ALU.is_equal).then_inc(selected, 1)
                dve.wait_ge(selected, t + 1)
                dve.tensor_scalar(low[j][:, :], sel[j][:, :], BIG, -BIG, ALU.mult, ALU.add)

            def weigh(k, j):
                t = U * k + j
                link.begin(t)
                dve.wait_ge(gathered[j], 32 * (k + 1))
                link(dve.tensor_tensor(logit[j][:, :], msg[j][:, GW:GT], ald[j][:, :], ALU.add))
                link(dve.scalar_tensor_tensor(out=logit[j][:, :], in0=logit[j][:, :], scalar=0.2, in1=logit[j][:, :],
                                              op0=ALU.mult, op1=ALU.max))
                wait(dve, peak, t)
                link(dve.tensor_copy(logit[j][PSEUDO:PSEUDO + 1, :], out[(j - 1) % U][0:1, GW:GT]))
                wait(dve, spread, t - 1)
                dve.tensor_tensor(masked[j % 2][:, :, :],
                                  low[j][:, :].unsqueeze(1).to_broadcast([P, HEADS, P]),
                                  logit[j][:, :].unsqueeze(2).to_broadcast([P, HEADS, P]), ALU.add).then_inc(blend, 1)
                dve.wait_ge(spread, t + 1)
                wait(dve, put[j], 16 * k)
                dve.tensor_reduce(out[j][:, GW:GT], spread_ps[j % 2][:, :].rearrange("p (h e) -> p h e", h=HEADS),
                                  AX.X, ALU.max).then_inc(peak, 1)
                dve.wait_ge(peak, t + 1)
                dve.tensor_tensor(wgt[j][:, :], logit[j][:, :], out[j][:, GW:GT], ALU.subtract).then_inc(weight, 1)
                dve.wait_ge(weighed, t + 1)
                dve.wait_ge(carried, t + 1)
                dve.tensor_tensor(msg[j][:, 0:GW].rearrange("p (h f) -> p h f", h=HEADS),
                                  msg[j][:, 0:GW].rearrange("p (h f) -> p h f", h=HEADS),
                                  wgt[j][:, :].unsqueeze(2).to_broadcast([P, HEADS, HW]), ALU.mult).then_inc(message, 1)

            pipeline(dve, n_turns, 3, select, weigh)

        @block.scalar
        def _(act):
            act.wait_ge(zeroed, 2 * U)
            for k, _ in turns(act, n_turns):
                for j in range(U):
                    t = U * k + j
                    act.wait_ge(gathered[j], 32 * (k + 1))
                    wait(act, copied, t)
                    act.activation(msg[j][PSEUDO:PSEUDO + 1, 0:GW], out[(j - 1) % U][0:1, 0:GW], ACT.Copy).then_inc(carried, 1)
                    act.wait_ge(weight, t + 1)
                    act.activation(wgt[j][:, :], wgt[j][:, :], ACT.Exp).then_inc(weighed, 1)
                    act.wait_ge(summed, t + 1)
                    wait(act, put[j], 16 * k)
                    act.activation(out[j][:, 0:GW], acc[j % 2][:, 0:GW], ACT.Copy).then_inc(copied, 1)

        @block.tensor
        def _(pe):
            for k, _ in turns(pe, n_turns):
                for j in range(U):
                    t = U * k + j
                    pe.wait_ge(blend, t + 1)
                    wait(pe, peak, t - 1)
                    for h in range(HEADS):
                        last = pe.transpose(spread_ps[j % 2][:, h * P:(h + 1) * P], masked[j % 2][:, h, :], C.ident[:, :])
                    last.then_inc(spread, 1)
                    pe.wait_ge(message, t + 1)
                    wait(pe, copied, t - 1)
                    pe.matmul(acc[j % 2][:, 0:GW], sel[j][:, :], msg[j][:, 0:GW], start=True, stop=True).then_inc(summed, 1)




def load_rows(sp, buf, table, k, j, loaded, external):
    s = U * k + j
    width = buf.shape[-1]
    if external and isinstance(s, int) and s == STEPS - 1:
        src = table[s * STEP:N, 0:width].rearrange("(p j) d -> p j d", j=2)
        sp.dma_start(buf[0:LAST, :, :], src).then_inc(loaded[j], 16)
    else:
        sp.dma_start(buf[:, :, :], rows(table, s, width)).then_inc(loaded[j], 16)


def store_rows(sp, table, buf, k, j, stored, external=False):
    s = U * k + j
    width = buf.shape[-1]
    if external and isinstance(s, int) and s == STEPS - 1:
        dst = table[s * STEP:N, 0:width].rearrange("(p j) d -> p j d", j=2)
        sp.dma_start(dst, buf[0:LAST, :, :]).then_inc(stored[j], 16)
    else:
        sp.dma_start(rows(table, s, width), buf[:, :, :]).then_inc(stored[j], 16)


def sync_program(sp, n_in, loads, n_out, stores, loaded, used, stored, ready):
    def load(k, j):
        wait(sp, used, U * k + j - U + 1)
        loads(k, j)

    def store(k, j):
        wait(sp, ready, U * k + j + 1)
        stores(k, j)

    pipeline(sp, GROUPS, U - 1, load, store)
    for j in range(U):
        sp.wait_ge(stored[j], 16 * n_out * GROUPS)


def gru(nc, C, name, layer, h_in, sums, h_out):
    with Stage(nc, name) as st:
        h = [st.sb(f"h{j}", [P, 2, D]) for j in range(U)]
        agg = [st.sb(f"agg{j}", [P, 2, D]) for j in range(U)]
        out = [st.sb(f"out{j}", [P, 2, D]) for j in range(U)]
        hT = [st.sb(f"hT{i}", [P, 4, P]) for i in range(2)]
        rz = [st.sb(f"rz{i}", [P, 2, 2 * D]) for i in range(2)]
        cand = [st.sb(f"cand{i}", [P, 2, D]) for i in range(2)]
        t_ps = [st.bank(f"t{i}") for i in range(2)]
        g_ps = [st.bank(f"g{i}", (P, 2, 512)) for i in range(2)]
        loaded = [st.sem(f"loaded{j}") for j in range(U)]
        stored = [st.sem(f"stored{j}") for j in range(U)]
        turned, copied, gates, squashed, before, cands, own, done = (
            st.sem(n) for n in ("turned", "copied", "gates", "squashed", "before", "cands", "own", "done"))
        block = st.block()

        @block.sync
        def _(sp):
            def loads(k, j):
                load_rows(sp, h[j], h_in, k, j, loaded, False)
                load_rows(sp, agg[j], sums, k, j, loaded, False)

            sync_program(sp, 2, loads, 1, lambda k, j: store_rows(sp, h_out, out[j], k, j, stored),
                         loaded, done, stored, done)

        @block.tensor
        def _(pe):
            def turn(k, j):
                s = U * k + j
                pe.wait_ge(loaded[j], 32 * (k + 1))
                wait(pe, copied, s - 1)
                for i in range(2):
                    pe.transpose(t_ps[j % 2][:, i * P:(i + 1) * P], agg[j][:, i, :], C.ident[:, :])
                for i in range(2):
                    last = pe.transpose(t_ps[j % 2][:, (2 + i) * P:(3 + i) * P], h[j][:, i, :], C.ident[:, :])
                last.then_inc(turned, 1)

            def multiply(k, j):
                s = U * k + j
                pe.wait_ge(copied, s + 1)
                wait(pe, before, s - 1)
                for i in range(2):
                    g = g_ps[j % 2][:, i, :]
                    pe.matmul(g, C.ones3[:, :], C.bias[:, C.B_GRU:C.B_GRU + 4 * D], start=True, stop=False)
                    pe.matmul(g[:, 0:3 * D], hT[j % 2][:, i, :], C.wc[:, layer, :], start=False, stop=False)
                    last = pe.matmul(g[:, D:4 * D], hT[j % 2][:, 2 + i, :], C.whh[:, :], start=False, stop=True)
                last.then_inc(gates, 1)

            pipeline(pe, GROUPS, 1, turn, multiply)

        @block.scalar
        def _(act):
            def copy(k, j):
                s = U * k + j
                act.wait_ge(turned, s + 1)
                wait(act, gates, s - 1)
                act.activation(hT[j % 2][:, :, :], t_ps[j % 2][:, :].rearrange("p (a b) -> p a b", a=4), ACT.Copy).then_inc(copied, 1)

            def squash(k, j):
                s = U * k + j
                act.wait_ge(gates, s + 1)
                wait(act, done, s - 1)
                act.activation(rz[j % 2][:, :, :], g_ps[j % 2][:, :, D:3 * D], ACT.Sigmoid).then_inc(squashed, 1)
                act.wait_ge(before, s + 1)
                act.activation(cand[j % 2][:, :, :], cand[j % 2][:, :, :], ACT.Tanh).then_inc(cands, 1)

            pipeline(act, GROUPS, 1, copy, squash)

        @block.vector
        def _(dve):
            link = Link(dve, own, 3)
            for k, _ in turns(dve, GROUPS):
                for j in range(U):
                    s = U * k + j
                    link.begin(s)
                    c, r, z = cand[j % 2][:, :, :], rz[j % 2][:, :, 0:D], rz[j % 2][:, :, D:2 * D]
                    dve.wait_ge(squashed, s + 1)
                    link(dve.tensor_tensor(c, g_ps[j % 2][:, :, 3 * D:4 * D], r, ALU.mult))
                    dve.tensor_tensor(c, g_ps[j % 2][:, :, 0:D], c, ALU.add).then_inc(before, 1)
                    dve.wait_ge(cands, s + 1)
                    wait(dve, stored[j], 16 * k)
                    link(dve.tensor_tensor(out[j][:, :, :], h[j][:, :, :], c, ALU.subtract))
                    link(dve.tensor_tensor(out[j][:, :, :], out[j][:, :, :], z, ALU.mult))
                    dve.tensor_tensor(out[j][:, :, :], out[j][:, :, :], c, ALU.add).then_inc(done, 1)


class Norm:
    LINKS = 5

    def __init__(self, st, name):
        self.stats = [st.sb(f"{name}_stats{j}", [P, 2, 6]) for j in range(2)]
        self.mv = [st.sb(f"{name}_mv{j}", [P, 2, 2]) for j in range(2)]
        self.rstd = [st.sb(f"{name}_rstd{j}", [P, 2]) for j in range(2)]
        self.counted = st.sem(f"{name}_counted")
        self.varied, self.rooted = st.sem(f"{name}_varied"), st.sem(f"{name}_rooted")

    def power(self, pool, C, s, j):
        pool.wait_ge(self.varied, s + 1)
        pool.tensor_tensor(self.rstd[j % 2][:, :], self.mv[j % 2][:, :, 1:2].rearrange("p j o -> p (j o)"),
                           C.minus_half[:, :], ALU.pow).then_inc(self.rooted, 1)

    def statistics(self, dve, link, x, s, j):
        st, mv = self.stats[j % 2], self.mv[j % 2]
        for i in range(2):
            ins = dve.bn_stats(st[:, i, :], x[:, i, :])
            if i:
                link(ins)
        dve.sem_inc(self.counted, 1)
        for i in range(2):
            ins = dve.bn_aggr(mv[:, i, :], st[:, i, :])
            if i:
                link(ins)
        dve.tensor_scalar(mv[:, :, 1:2], mv[:, :, 1:2], EPS, None, ALU.add).then_inc(self.varied, 1)

    def scale(self, dve, out, x, s, j, i):
        mv, rstd = self.mv[j % 2], self.rstd[j % 2]
        return dve.tensor_scalar(out[:, i, :], x[:, i, :], mv[:, i, 0:1], rstd[:, i:i + 1], ALU.subtract, ALU.mult)


def transform(nc, C, name, front, a, b=None, bn=None, x_out=None, project=None, p_out=None, external=False):
    gat = project is not None and project[0] == "gat"
    with Stage(nc, name) as st:
        has_b = b is not None
        xa = [st.sb(f"xa{j}", [P, 2, D]) for j in range(U)]
        xb = [st.sb(f"xb{j}", [P, 2, D]) for j in range(U)] if has_b else None
        x = [st.sb(f"x{j}", [P, 2, D]) for j in range(U)]
        ex = [st.sb(f"ex{j}", [P, 2, D]) for j in range(U)] if bn is not None else None
        width = D + 8 if gat else D
        if project is not None:
            xT = [st.sb(f"xT{i}", [P, 2, P]) for i in range(2)]
            t_ps = [st.bank(f"t{i}") for i in range(2)]
            p_ps = [st.bank(f"p{i}") for i in range(2)]
            po = [st.sb(f"po{j}", [P, 2, GT if gat else D]) for j in range(U)]
            pd = [st.sb(f"pd{j}", [P, 2, HEADS]) for j in range(U)] if gat else None
        ln = Norm(st, "ln") if front in ("ln", "bn_ln") else None
        loaded = [st.sem(f"loaded{j}") for j in range(U)]
        stored = [st.sem(f"stored{j}") for j in range(U)]
        own, fronted, turned, copied, multiplied, projected, low, exps, ones_set = (
            st.sem(n) for n in ("own", "fronted", "turned", "copied", "multiplied", "projected", "low", "exps", "ones_set"))
        n_in = 1 + has_b
        n_out = (x_out is not None) + (project is not None) + gat
        ready = projected if project is not None else fronted
        block = st.block()

        @block.sync
        def _(sp):
            def loads(k, j):
                load_rows(sp, xa[j], a, k, j, loaded, external)
                if has_b:
                    load_rows(sp, xb[j], b, k, j, loaded, False)

            def stores(k, j):
                if x_out is not None:
                    store_rows(sp, x_out, x[j], k, j, stored)
                if project is not None:
                    store_rows(sp, p_out[0] if gat else p_out, po[j], k, j, stored)
                if gat:
                    store_rows(sp, p_out[1], pd[j], k, j, stored)

            sync_program(sp, n_in, loads, n_out, stores, loaded, ready, stored, ready)

        n_links = {"copy": 0, "ln": 4, "bn": 3, "bn_ln": 7}[front]

        @block.vector
        def _(dve):
            link = Link(dve, own, n_links)
            if gat:
                for j in range(U):
                    dve.memset(po[j][:, :, :], 1.0).then_inc(ones_set, 1)
                dve.wait_ge(ones_set, U)

            def make(k, j):
                s = U * k + j
                link.begin(s)
                dve.wait_ge(loaded[j], 16 * n_in * (k + 1))
                wait(dve, stored[j], 16 * n_out * k)
                xj, src = x[j], xa[j]
                if bn is not None:
                    sc, sh = (v[:, :].unsqueeze(1).to_broadcast([P, 2, D]) for v in bn)
                    link(dve.tensor_tensor(xj[:, :, :], xa[j][:, :, :], sc, ALU.mult))
                    link(dve.tensor_tensor(xj[:, :, :], xj[:, :, :], sh, ALU.add))
                    dve.tensor_scalar(ex[j][:, :, :], xj[:, :, :], 0.0, None, ALU.min).then_inc(low, 1)
                    dve.wait_ge(exps, s + 1)
                    ins = dve.scalar_tensor_tensor(out=xj[:, :, :], in0=xj[:, :, :], scalar=0.0, in1=ex[j][:, :, :],
                                                   op0=ALU.max, op1=ALU.add)
                    if front == "bn":
                        link(ins)
                        dve.tensor_scalar(xj[:, :, :], xj[:, :, :], -1.0, None, ALU.add).then_inc(fronted, 1)
                        return
                    link(ins)
                    link(dve.scalar_tensor_tensor(out=xj[:, :, :], in0=xj[:, :, :], scalar=-1.0, in1=xb[j][:, :, :],
                                                  op0=ALU.add, op1=ALU.add))
                elif has_b:
                    link(dve.tensor_tensor(xj[:, :, :], xa[j][:, :, :], xb[j][:, :, :], ALU.add))
                if front == "copy":
                    return
                ln.statistics(dve, link, xj, s, j)
                dve.wait_ge(ln.rooted, s + 1)
                link(ln.scale(dve, xj, xj, s, j, 0))
                ln.scale(dve, xj, xj, s, j, 1).then_inc(fronted, 1)

            def put(k, j):
                s = U * k + j
                dve.wait_ge(multiplied, s + 1)
                wait(dve, stored[j], 16 * n_out * k)
                v = p_ps[j % 2][:, 0:2 * width].rearrange("p (a c) -> p a c", a=2)
                if gat:
                    for i in range(2):
                        dve.tensor_copy(po[j][:, i, 0:GW].rearrange("p (h f) -> p h f", h=HEADS)[:, :, 0:FH],
                                        v[:, i, 0:D].rearrange("p (h f) -> p h f", h=HEADS))
                    dve.tensor_copy(po[j][:, :, GW:GT], v[:, :, D:D + 4])
                    dve.tensor_copy(pd[j][:, :, :], v[:, :, D + 4:D + 8]).then_inc(projected, 1)
                else:
                    dve.tensor_copy(po[j][:, :, :], v).then_inc(projected, 1)

            if project is None:
                for k, _ in turns(dve, GROUPS):
                    for j in range(U):
                        make(k, j)
            elif front == "copy":
                for k, _ in turns(dve, GROUPS):
                    for j in range(U):
                        put(k, j)
            else:
                pipeline(dve, GROUPS, 1, make, put)

        if ln is not None:
            @block.gpsimd
            def _(pool):
                for k, _ in turns(pool, GROUPS):
                    for j in range(U):
                        ln.power(pool, C, U * k + j, j)

        if project is not None:
            @block.tensor
            def _(pe):
                if gat:
                    w = C.gat[:, project[1], :]
                else:
                    w = project[0]

                def turn(k, j):
                    s = U * k + j
                    src = xa[j] if front == "copy" else x[j]
                    if front == "copy":
                        pe.wait_ge(loaded[j], 16 * (k + 1))
                    else:
                        pe.wait_ge(fronted, s + 1)
                    wait(pe, copied, s - 1)
                    for i in range(2):
                        last = pe.transpose(t_ps[j % 2][:, i * P:(i + 1) * P], src[:, i, :], C.ident[:, :])
                    last.then_inc(turned, 1)

                def multiply(k, j):
                    s = U * k + j
                    pe.wait_ge(copied, s + 1)
                    wait(pe, projected, s - 1)
                    for i in range(2):
                        g = p_ps[j % 2][:, i * width:(i + 1) * width]
                        if not gat:
                            pe.matmul(g, C.ones3[:, :], C.bias[:, project[1]:project[1] + D], start=True, stop=False)
                        last = pe.matmul(g, xT[j % 2][:, i, :], w, start=gat, stop=True)
                    last.then_inc(multiplied, 1)

                pipeline(pe, GROUPS, 1, turn, multiply)

        if project is not None or bn is not None:
            @block.scalar
            def _(act):
                def lift(k, j):
                    act.wait_ge(low, U * k + j + 1)
                    act.activation(ex[j][:, :, :], ex[j][:, :, :], ACT.Exp).then_inc(exps, 1)

                def copy(k, j):
                    s = U * k + j
                    act.wait_ge(turned, s + 1)
                    wait(act, multiplied, s - 1)
                    act.activation(xT[j % 2][:, :, :], t_ps[j % 2][:, 0:2 * P].rearrange("p (a b) -> p a b", a=2), ACT.Copy).then_inc(copied, 1)

                for k, _ in turns(act, GROUPS):
                    for j in range(U):
                        if bn is not None:
                            lift(k, j)
                        if project is not None:
                            copy(k, j)


def merge_attention(nc, C, name, sums, table, dst_logits, out_table, gb, bn):
    with Stage(nc, name) as st:
        sm = [st.sb(f"sm{j}", [P, 2, GT]) for j in range(U)]
        tb = [st.sb(f"tb{j}", [P, 2, GT]) for j in range(U)]
        ad = [st.sb(f"ad{j}", [P, 2, HEADS]) for j in range(U)]
        lg = [st.sb(f"lg{j}", [P, 2, HEADS]) for j in range(2)]
        mx = [st.sb(f"mx{j}", [P, 2, HEADS]) for j in range(2)]
        df = [st.sb(f"df{j}", [P, 2, 2, HEADS]) for j in range(2)]
        rc = [st.sb(f"rc{j}", [P, 2, HEADS]) for j in range(2)]
        sq = [st.sb(f"sq{j}", [P, 2, D]) for j in range(2)]
        out = [st.sb(f"out{j}", [P, 2, D]) for j in range(U)]
        st1 = st.sb("st1", [P, 8, D])
        acc, acc2 = st.bank("acc"), st.bank("acc2")
        loaded = [st.sem(f"loaded{j}") for j in range(U)]
        stored = [st.sem(f"stored{j}") for j in range(U)]
        own, apart, factors, done, squared, counted, own2, varied, rooted = (
            st.sem(n) for n in ("own", "apart", "factors", "done", "squared", "counted", "own2", "varied", "rooted"))
        block = st.block()

        @block.sync
        def _(sp):
            def loads(k, j):
                load_rows(sp, sm[j], sums, k, j, loaded, False)
                load_rows(sp, tb[j], table, k, j, loaded, False)
                load_rows(sp, ad[j], dst_logits, k, j, loaded, False)

            sync_program(sp, 3, loads, 1, lambda k, j: store_rows(sp, out_table, out[j], k, j, stored),
                         loaded, done, stored, done)

        @block.vector
        def _(dve):
            link = Link(dve, own, 7)
            heads = lambda v: v[:, :, 0:GW].rearrange("p j (h f) -> p j h f", h=HEADS)

            def apart_(k, j):
                s = U * k + j
                link.begin(s)
                dve.wait_ge(loaded[j], 48 * (k + 1))
                l, m, d = lg[j % 2], mx[j % 2], df[j % 2]
                link(dve.tensor_tensor(l[:, :, :], tb[j][:, :, GW:GT], ad[j][:, :, :], ALU.add))
                link(dve.scalar_tensor_tensor(out=l[:, :, :], in0=l[:, :, :], scalar=0.2, in1=l[:, :, :], op0=ALU.mult, op1=ALU.max))
                link(dve.tensor_tensor(m[:, :, :], l[:, :, :], sm[j][:, :, GW:GT], ALU.max))
                dve.tensor_tensor(d[:, 0, :, :], sm[j][:, :, GW:GT], m[:, :, :], ALU.subtract)
                dve.tensor_tensor(d[:, 1, :, :], l[:, :, :], m[:, :, :], ALU.subtract).then_inc(apart, 1)
                dve.wait_ge(factors, s + 1)
                f = [d[:, i, :, :].unsqueeze(3).to_broadcast([P, 2, HEADS, HW]) for i in range(2)]
                dve.tensor_tensor(heads(sm[j]), heads(sm[j]), f[0], ALU.mult)
                link(dve.tensor_tensor(heads(tb[j]), heads(tb[j]), f[1], ALU.mult))
                link(dve.tensor_tensor(heads(sm[j]), heads(sm[j]), heads(tb[j]), ALU.add))
                link(dve.reciprocal(rc[j % 2][:, :, :].unsqueeze(3), heads(sm[j])[:, :, :, FH:HW]))
                wait(dve, stored[j], 16 * k)
                wait(dve, counted, s - U + 1)
                link(dve.tensor_tensor(out[j][:, :, :].rearrange("p j (h f) -> p j h f", h=HEADS), heads(sm[j])[:, :, :, 0:FH],
                                       rc[j % 2][:, :, :].unsqueeze(3).to_broadcast([P, 2, HEADS, FH]),
                                       ALU.mult))
                wait(dve, counted, s - 1)
                dve.tensor_tensor(sq[j % 2][:, :, :], out[j][:, :, :], out[j][:, :, :], ALU.mult).then_inc(done, 1)

            for k, _ in turns(dve, GROUPS):
                for j in range(U):
                    apart_(k, j)
            dve.wait_ge(counted, STEPS)
            g, be, bb = (C.bc[:, i, :] for i in gb)
            w = lambda i: st1[:, i, :]
            fin = Link(dve, own2, 8)
            fin.begin(0)
            fin(dve.tensor_copy(st1[:, 0:4, :], acc[:, :].rearrange("p (a d) -> p a d", a=4)))
            fin(dve.tensor_tensor(st1[:, 4:5, :], st1[:, 0:1, :], st1[:, 1:2, :], ALU.add))
            fin(dve.tensor_tensor(st1[:, 5:6, :], st1[:, 2:3, :], st1[:, 3:4, :], ALU.add))
            fin(dve.tensor_scalar(st1[:, 4:6, :], st1[:, 4:6, :], 1.0 / N, None, ALU.mult))
            fin(dve.tensor_tensor(w(0), w(4), w(4), ALU.mult))
            fin(dve.tensor_tensor(w(0), w(5), w(0), ALU.subtract))
            dve.tensor_scalar(w(0), w(0), EPS, None, ALU.add).then_inc(varied, 1)
            dve.memset(w(1), -0.5).then_inc(varied, 1)
            dve.wait_ge(rooted, 1)
            sc, sh = bn
            fin(dve.tensor_tensor(sc[:, :], w(2), g, ALU.mult))
            fin(dve.tensor_tensor(w(4), w(4), bb, ALU.add))
            dve.tensor_tensor(w(6), bb, w(4), ALU.subtract).then_inc(varied, 1)
            dve.wait_ge(varied, 3)
            dve.tensor_tensor(w(6), w(6), sc[:, :], ALU.mult).then_inc(varied, 1)
            dve.wait_ge(varied, 4)
            dve.tensor_tensor(sh[:, :], w(6), be, ALU.add).then_inc(varied, 1)

        @block.gpsimd
        def _(pool):
            pool.wait_ge(varied, 2)
            pool.tensor_tensor(st1[:, 2, :], st1[:, 0, :], st1[:, 1, :], ALU.pow).then_inc(rooted, 1)

        @block.scalar
        def _(act):
            for k, _ in turns(act, GROUPS):
                for j in range(U):
                    s = U * k + j
                    act.wait_ge(apart, s + 1)
                    act.activation(df[j % 2][:, :, :, :], df[j % 2][:, :, :, :], ACT.Exp).then_inc(factors, 1)

        @block.tensor
        def _(pe):
            for k, last in turns(pe, GROUPS):
                for j in range(U):
                    s = U * k + j
                    pe.wait_ge(done, s + 1)
                    end = last and j == U - 1
                    n = LAST if end else P
                    start = isinstance(k, int) and k == 0 and j == 0
                    pe.matmul(acc[:, 0:2 * D], C.ones[0:n, :], out[j][0:n, :, :].rearrange("p j d -> p (j d)"),
                              start=start, stop=False, skip_group_check=True)
                    pe.matmul(acc[:, 2 * D:4 * D], C.ones[0:n, :], sq[j % 2][0:n, :, :].rearrange("p j d -> p (j d)"),
                              start=False, stop=end, skip_group_check=True).then_inc(counted, 1)


def convolve(nc, C, name, layer, x_in, sums, edge_sums, y_out):
    with Stage(nc, name) as st:
        x = [st.sb(f"x{j}", [P, 2, D]) for j in range(U)]
        agg = [st.sb(f"agg{j}", [P, 2, D]) for j in range(U)]
        ea = [st.sb(f"ea{j}", [P, 2, ED + 1]) for j in range(U)]
        inv = [st.sb(f"inv{j}", [P, 2]) for j in range(2)]
        out = [st.sb(f"out{j}", [P, 2, D]) for j in range(U)]
        xT = [st.sb(f"xT{i}", [P, 4, P]) for i in range(2)]
        eT = [st.sb(f"eT{i}", [ED + 1, 2, P]) for i in range(2)]
        t_ps = [st.bank(f"t{i}") for i in range(2)]
        e_ps = [st.bank(f"e{i}") for i in range(2)]
        p_ps = [st.bank(f"p{i}") for i in range(2)]
        loaded = [st.sem(f"loaded{j}") for j in range(U)]
        stored = [st.sem(f"stored{j}") for j in range(U)]
        own, scaled, turned, copied, e_copied, multiplied, done = (
            st.sem(n) for n in ("own", "scaled", "turned", "copied", "e_copied", "multiplied", "done"))
        block = st.block()

        @block.sync
        def _(sp):
            def loads(k, j):
                load_rows(sp, x[j], x_in, k, j, loaded, False)
                load_rows(sp, agg[j], sums, k, j, loaded, False)
                load_rows(sp, ea[j], edge_sums, k, j, loaded, False)

            sync_program(sp, 3, loads, 1, lambda k, j: store_rows(sp, y_out, out[j], k, j, stored),
                         loaded, done, stored, done)

        @block.vector
        def _(dve):
            link = Link(dve, own, 2)

            def scale(k, j):
                s = U * k + j
                link.begin(s)
                dve.wait_ge(loaded[j], 48 * (k + 1))
                v = inv[j % 2]
                link(dve.tensor_scalar(v[:, :].unsqueeze(2), ea[j][:, :, ED:ED + 1], 1.0, None, ALU.max))
                link(dve.reciprocal(v[:, :], v[:, :]))
                dve.tensor_tensor(agg[j][:, :, :], agg[j][:, :, :], v[:, :].unsqueeze(2).to_broadcast([P, 2, D]), ALU.mult)
                dve.tensor_tensor(ea[j][:, :, :], ea[j][:, :, :], v[:, :].unsqueeze(2).to_broadcast([P, 2, ED + 1]),
                                  ALU.mult).then_inc(scaled, 1)

            def copy_e(k, j):
                s = U * k + j
                dve.wait_ge(turned, s + 1)
                wait(dve, multiplied, s - 1)
                dve.tensor_copy(eT[j % 2][:, :, :], e_ps[j % 2][0:ED + 1, 0:2 * P].rearrange("p (a b) -> p a b", a=2)).then_inc(e_copied, 1)

            pipeline(dve, GROUPS, 1, scale, copy_e)

        @block.tensor
        def _(pe):
            def turn(k, j):
                s = U * k + j
                pe.wait_ge(scaled, s + 1)
                wait(pe, copied, s - 1)
                wait(pe, e_copied, s - 1)
                for i in range(2):
                    pe.transpose(t_ps[j % 2][:, i * P:(i + 1) * P], agg[j][:, i, :], C.ident[:, :])
                    pe.transpose(t_ps[j % 2][:, (2 + i) * P:(3 + i) * P], x[j][:, i, :], C.ident[:, :])
                    last = pe.transpose(e_ps[j % 2][0:ED + 1, i * P:(i + 1) * P], ea[j][:, i, :], C.ident[:, :])
                last.then_inc(turned, 1)

            def multiply(k, j):
                s = U * k + j
                pe.wait_ge(copied, s + 1)
                pe.wait_ge(e_copied, s + 1)
                wait(pe, done, s - 1)
                for i in range(2):
                    g = p_ps[j % 2][:, i * D:(i + 1) * D]
                    pe.matmul(g, C.ones3[:, :], C.bias[:, C.B_L + layer * D:C.B_L + (layer + 1) * D], start=True, stop=False)
                    pe.matmul(g, xT[j % 2][:, i, :], C.wl[:, layer, :], start=False, stop=False)
                    pe.matmul(g, eT[j % 2][:, i, :], C.wel[:, layer, :], start=False, stop=False)
                    last = pe.matmul(g, xT[j % 2][:, 2 + i, :], C.wr[:, layer, :], start=False, stop=True)
                last.then_inc(multiplied, 1)

            pipeline(pe, GROUPS, 1, turn, multiply)

        @block.scalar
        def _(act):
            def copy(k, j):
                s = U * k + j
                act.wait_ge(turned, s + 1)
                wait(act, multiplied, s - 1)
                act.activation(xT[j % 2][:, :, :], t_ps[j % 2][:, :].rearrange("p (a b) -> p a b", a=4), ACT.Copy).then_inc(copied, 1)

            def rectify(k, j):
                s = U * k + j
                act.wait_ge(multiplied, s + 1)
                wait(act, stored[j], 16 * k)
                act.activation(out[j][:, :, :], p_ps[j % 2][:, 0:2 * D].rearrange("p (a b) -> p a b", a=2), ACT.Relu).then_inc(done, 1)

            pipeline(act, GROUPS, 1, copy, rectify)


def update(nc, C, name, x_in, h_in, maxima, edge_sums, x_out):
    with Stage(nc, name) as st:
        x = [st.sb(f"x{j}", [P, 2, D]) for j in range(U)]
        h = [st.sb(f"h{j}", [P, 2, D]) for j in range(U)]
        mx = [st.sb(f"mx{j}", [P, 2, D]) for j in range(U)]
        ea = [st.sb(f"ea{j}", [P, 2, ED + 1]) for j in range(U)]
        has = [st.sb(f"has{j}", [P, 2]) for j in range(2)]
        out = [st.sb(f"out{j}", [P, 2, D]) for j in range(U)]
        xT = [st.sb(f"xT{i}", [P, 4, P]) for i in range(2)]
        t_ps = [st.bank(f"t{i}") for i in range(2)]
        p_ps = [st.bank(f"p{i}") for i in range(2)]
        ln = Norm(st, "ln")
        loaded = [st.sem(f"loaded{j}") for j in range(U)]
        stored = [st.sem(f"stored{j}") for j in range(U)]
        own, own2, parted, turned, copied, multiplied, added, done = (
            st.sem(n) for n in ("own", "own2", "parted", "turned", "copied", "multiplied", "added", "done"))
        block = st.block()

        @block.sync
        def _(sp):
            def loads(k, j):
                load_rows(sp, x[j], x_in, k, j, loaded, False)
                load_rows(sp, h[j], h_in, k, j, loaded, False)
                load_rows(sp, mx[j], maxima, k, j, loaded, False)
                load_rows(sp, ea[j], edge_sums, k, j, loaded, False)

            sync_program(sp, 4, loads, 1, lambda k, j: store_rows(sp, x_out, out[j], k, j, stored),
                         loaded, done, stored, done)

        @block.vector
        def _(dve):
            link, link2 = Link(dve, own, 1), Link(dve, own2, 4)

            def part(k, j):
                s = U * k + j
                link.begin(s)
                dve.wait_ge(loaded[j], 64 * (k + 1))
                dve.tensor_scalar(has[j % 2][:, :].unsqueeze(2), ea[j][:, :, ED:ED + 1], 1.0, None, ALU.min)
                link(dve.tensor_tensor(mx[j][:, :, :], mx[j][:, :, :], h[j][:, :, :], ALU.subtract))
                dve.tensor_tensor(mx[j][:, :, :], mx[j][:, :, :], has[j % 2][:, :].unsqueeze(2).to_broadcast([P, 2, D]),
                                  ALU.mult).then_inc(parted, 1)

            def finish(k, j):
                s = U * k + j
                link2.begin(s)
                o = out[j]
                dve.wait_ge(multiplied, s + 1)
                wait(dve, stored[j], 16 * k)
                dve.tensor_tensor(o[:, :, :], p_ps[j % 2][:, 0:2 * D].rearrange("p (a b) -> p a b", a=2), x[j][:, :, :],
                                  ALU.add).then_inc(added, 1)
                dve.wait_ge(added, s + 1)
                ln.statistics(dve, link2, o, s, j)
                dve.wait_ge(ln.rooted, s + 1)
                ln.scale(dve, o, o, s, j, 0)
                link2(ln.scale(dve, o, o, s, j, 1))
                link2(dve.tensor_tensor(o[:, :, :], o[:, :, :], C.bcast("ln1_g"), ALU.mult))
                dve.tensor_tensor(o[:, :, :], o[:, :, :], C.bcast("ln1_b"), ALU.add).then_inc(done, 1)

            pipeline(dve, GROUPS, 1, part, finish)

        @block.gpsimd
        def _(pool):
            for k, _ in turns(pool, GROUPS):
                for j in range(U):
                    ln.power(pool, C, U * k + j, j)

        @block.tensor
        def _(pe):
            def turn(k, j):
                s = U * k + j
                pe.wait_ge(parted, s + 1)
                wait(pe, copied, s - 1)
                for i in range(2):
                    pe.transpose(t_ps[j % 2][:, i * P:(i + 1) * P], h[j][:, i, :], C.ident[:, :])
                    last = pe.transpose(t_ps[j % 2][:, (2 + i) * P:(3 + i) * P], mx[j][:, i, :], C.ident[:, :])
                last.then_inc(turned, 1)

            def multiply(k, j):
                s = U * k + j
                pe.wait_ge(copied, s + 1)
                wait(pe, added, s - 1)
                for i in range(2):
                    g = p_ps[j % 2][:, i * D:(i + 1) * D]
                    pe.matmul(g, C.ones3[:, :], C.bias[:, C.B_F:C.B_F + D], start=True, stop=False)
                    pe.matmul(g, xT[j % 2][:, i, :], C.wf[:, 0, :], start=False, stop=False)
                    last = pe.matmul(g, xT[j % 2][:, 2 + i, :], C.wf[:, 1, :], start=False, stop=True)
                last.then_inc(multiplied, 1)

            pipeline(pe, GROUPS, 1, turn, multiply)

        @block.scalar
        def _(act):
            for k, _ in turns(act, GROUPS):
                for j in range(U):
                    s = U * k + j
                    act.wait_ge(turned, s + 1)
                    wait(act, multiplied, s - 1)
                    act.activation(xT[j % 2][:, :, :], t_ps[j % 2][:, :].rearrange("p (a b) -> p a b", a=4), ACT.Copy).then_inc(copied, 1)


def feed_forward(nc, C, name, x4_in, x3_in, y_out):
    HB = FFN // P
    with Stage(nc, name) as st:
        x4 = [st.sb(f"x4{j}", [P, 2, D]) for j in range(U)]
        x3 = [st.sb(f"x3{j}", [P, 2, D]) for j in range(U)]
        out = [st.sb(f"out{j}", [P, 2, D]) for j in range(U)]
        xT = [st.sb(f"xT{i}", [P, 2 * P]) for i in range(2)]
        hid = [st.sb(f"hid{i}", [P, HB, 2 * P]) for i in range(2)]
        t_ps = [st.bank(f"t{i}") for i in range(2)]
        h_ps = [st.bank(f"h{i}") for i in range(HB)]
        p_ps = [st.bank(f"p{i}") for i in range(2)]
        ln2, ln = Norm(st, "lnb"), Norm(st, "ln")
        loaded = [st.sem(f"loaded{j}") for j in range(U)]
        stored = [st.sem(f"stored{j}") for j in range(U)]
        own, turned, copied, hidden, active, multiplied, added, done = (
            st.sem(n) for n in ("own", "turned", "copied", "hidden", "active", "multiplied", "added", "done"))
        block = st.block()

        @block.sync
        def _(sp):
            def loads(k, j):
                load_rows(sp, x4[j], x4_in, k, j, loaded, False)
                load_rows(sp, x3[j], x3_in, k, j, loaded, False)

            sync_program(sp, 2, loads, 1, lambda k, j: store_rows(sp, y_out, out[j], k, j, stored, external=True),
                         loaded, done, stored, done)

        @block.tensor
        def _(pe):
            def grow(k, j):
                s = U * k + j
                pe.wait_ge(loaded[j], 32 * (k + 1))
                wait(pe, copied, s - 1)
                for i in range(2):
                    last = pe.transpose(t_ps[j % 2][:, i * P:(i + 1) * P], x4[j][:, i, :], C.ident[:, :])
                last.then_inc(turned, 1)
                pe.wait_ge(copied, s + 1)
                for q in range(HB // 2):
                    wait(pe, active, (HB // 2) * (s - 2) + q + 1)
                    for b in range(2 * q, 2 * q + 2):
                        last = pe.matmul(h_ps[2 * (j % 2) + q][:, (b % 2) * 2 * P:(b % 2 + 1) * 2 * P],
                                         C.ffn1[:, b * P:(b + 1) * P], xT[j % 2][:, :], start=True, stop=True)
                    last.then_inc(hidden, 1)

            def shrink(k, j):
                s = U * k + j
                pe.wait_ge(active, (HB // 2) * (s + 1))
                wait(pe, added, s - 1)
                for i in range(2):
                    g = p_ps[j % 2][:, i * D:(i + 1) * D]
                    pe.matmul(g, C.ones3[:, :], C.bias[:, C.B_F2:C.B_F2 + D], start=True, stop=False)
                    for b in range(HB):
                        last = pe.matmul(g, hid[j % 2][:, b, i * P:(i + 1) * P], C.ffn2[:, b, :],
                                         start=False, stop=(b == HB - 1))
                last.then_inc(multiplied, 1)

            pipeline(pe, GROUPS, 1, grow, shrink)

        @block.scalar
        def _(act):
            for k, _ in turns(act, GROUPS):
                for j in range(U):
                    s = U * k + j
                    act.wait_ge(turned, s + 1)
                    wait(act, hidden, (HB // 2) * (s - 1))
                    act.activation(xT[j % 2][:, :], t_ps[j % 2][:, 0:2 * P], ACT.Copy).then_inc(copied, 1)
                    wait(act, multiplied, s - 1)
                    for q in range(HB // 2):
                        act.wait_ge(hidden, (HB // 2) * s + q + 1)
                        for b in range(2 * q, 2 * q + 2):
                            last = act.activation(hid[j % 2][:, b, :], h_ps[2 * (j % 2) + q][:, (b % 2) * 2 * P:(b % 2 + 1) * 2 * P],
                                                  ACT.Gelu, bias=C.ffn1_b[:, b:b + 1])
                        last.then_inc(active, 1)

        @block.vector
        def _(dve):
            link = Link(dve, own, 9)
            for k, _ in turns(dve, GROUPS):
                for j in range(U):
                    s = U * k + j
                    link.begin(s)
                    o = out[j]
                    dve.wait_ge(multiplied, s + 1)
                    wait(dve, stored[j], 16 * k)
                    dve.tensor_tensor(o[:, :, :], p_ps[j % 2][:, 0:2 * D].rearrange("p (a b) -> p a b", a=2), x4[j][:, :, :],
                                      ALU.add).then_inc(added, 1)
                    dve.wait_ge(added, s + 1)
                    ln2.statistics(dve, link, o, s, j)
                    dve.wait_ge(ln2.rooted, s + 1)
                    link(ln2.scale(dve, o, o, s, j, 0))
                    link(ln2.scale(dve, o, o, s, j, 1))
                    link(dve.tensor_tensor(o[:, :, :], o[:, :, :], C.bcast("ln2_g"), ALU.mult))
                    link(dve.tensor_tensor(o[:, :, :], o[:, :, :], C.bcast("ln2_b"), ALU.add))
                    link(dve.tensor_tensor(o[:, :, :], o[:, :, :], x3[j][:, :, :], ALU.add))
                    ln.statistics(dve, link, o, s, j)
                    dve.wait_ge(ln.rooted, s + 1)
                    ln.scale(dve, o, o, s, j, 0)
                    ln.scale(dve, o, o, s, j, 1).then_inc(done, 1)

        @block.gpsimd
        def _(pool):
            for k, _ in turns(pool, GROUPS):
                for j in range(U):
                    ln2.power(pool, C, U * k + j, j)
                    ln.power(pool, C, U * k + j, j)




class Constants:
    BC = ["bn_g1", "bn_be1", "bn_b1", "bn_g2", "bn_be2", "bn_b2", "ln1_g", "ln1_b", "ln2_g", "ln2_b"]
    B_LIN, B_GRU, B_L, B_IN, B_F, B_F2 = 0, D, 5 * D, 7 * D, 8 * D, 9 * D
    NB = 10 * D

    def __init__(self, nc, ctx):
        def sb(name, shape, dt=F32):
            return ctx.enter_context(nc.sbuf_tensor(name, shape, dt))

        self.ident, self.ones = sb("ident", [P, P]), sb("ones", [P, P])
        self.ones3, self.minus_half = sb("ones3", [3, P], BF16), sb("minus_half", [P, 2])
        self.lin, self.whh, self.wc = sb("lin", [P, D]), sb("whh", [P, 3 * D]), sb("wc", [P, 3, 3 * D])
        self.gat = sb("gat", [P, 2, D + 8])
        self.wl, self.wr, self.wel = sb("wl", [P, 2, D]), sb("wr", [P, 2, D]), sb("wel", [ED + 1, 2, D])
        self.win, self.wf = sb("win", [P, D]), sb("wf", [P, 2, D])
        self.ffn1, self.ffn2, self.ffn1_b = sb("ffn1", [P, FFN]), sb("ffn2", [P, 4, D]), sb("ffn1_b", [P, 4])
        self.bias, self.bc = sb("bias", [3, self.NB], BF16), sb("bc", [P, len(self.BC), D])
        self.bn = [(sb(f"bn_scale{i}", [P, D]), sb(f"bn_shift{i}", [P, D])) for i in range(2)]
        self.lists, self.nat_lists = sb("lists", [P, TILES, 4]), sb("nat_lists", [P, NAT, 2])
        self.targets = sb("targets", [P, TILES * P])
        self.bias_dram = nc.dram_tensor("bias_dram", (3, self.NB), BF16).ap()
        self.pad = nc.dram_tensor("pad", (3, PAD), F32).ap()
        self.dst_row = nc.dram_tensor("dst_row", (1, TILES * P), F32).ap()
        self.bias_row = nc.dram_tensor("bias_row", (1, NAT * P), F32).ap()

    def bcast(self, name):
        return self.bc[:, self.BC.index(name), :].unsqueeze(1).to_broadcast([P, 2, D])


def graph_kernel(nc, A, out):
    with ExitStack() as ctx:
        C = Constants(nc, ctx)

        def table(name, width):
            return nc.dram_tensor(f"table_{name}", (NP, width), F32).ap()

        ha, hb, x1, x3 = (table(n, D) for n in ("ha", "hb", "x1", "x3"))
        agg, esum = table("agg", D), table("esum", ED + 1)
        gsum, gtab, gdst = table("gsum", GT), table("gtab", GT), table("gdst", HEADS)

        prepare_weights(nc, A, C)
        prepare_edges(nc, A, C)
        clear_tables(nc, C, [(agg, D, False), (esum, ED + 1, False), (gsum, GT, True)])
        sum_edges(nc, C, "Se", A["edge_attr"], ED, esum, ones=True)

        transform(nc, C, "T0", "copy", A["x"], project=(C.lin[:, :], C.B_LIN), p_out=ha, external=True)
        h, g = ha, hb
        for layer in range(3):
            sum_edges(nc, C, f"S{layer}", h, D, agg)
            gru(nc, C, f"G{layer}", layer, h, agg, g)
            h, g = g, h
        transform(nc, C, "T1", "ln", A["x"], h, x_out=x1, project=("gat", 0), p_out=(gtab, gdst), external=True)

        attend_edges(nc, C, "A1", gtab, gdst, gsum)
        merge_attention(nc, C, "M1", gsum, gtab, gdst, ha, (0, 1, 2), C.bn[0])
        transform(nc, C, "T2", "bn", ha, bn=C.bn[0], project=("gat", 1), p_out=(gtab, gdst))
        attend_edges(nc, C, "A2", gtab, gdst, gsum)
        merge_attention(nc, C, "M2", gsum, gtab, gdst, hb, (3, 4, 5), C.bn[1])
        transform(nc, C, "T3", "bn_ln", hb, x1, bn=C.bn[1], x_out=ha)

        sum_edges(nc, C, "S3", ha, D, agg)
        convolve(nc, C, "C1", 0, ha, agg, esum, hb)
        sum_edges(nc, C, "S4", hb, D, agg)
        convolve(nc, C, "C2", 1, hb, agg, esum, x1)
        transform(nc, C, "T4", "ln", ha, x1, x_out=x3, project=(C.win[:, :], C.B_IN), p_out=hb)

        max_edges(nc, C, "X5", hb, agg)
        update(nc, C, "U5", x3, hb, agg, esum, ha)
        feed_forward(nc, C, "F5", ha, x3, out)


def kernel(**inputs):
    import numpy as np
    import concourse.bacc as bacc
    from concourse.bass_utils import run_bass_kernel_spmd

    v = {name: np.asarray(a) for name, a in inputs.items()}

    def t(name):
        a = v[name]
        return np.ascontiguousarray(np.swapaxes(a, -1, -2))

    def row(name):
        return v[name].reshape(1, -1)

    host = {
        "x": v["x"], "src": v["src"], "dst": v["dst"], "edge_attr": v["edge_attr_32"],
        "lin_wT": t("L0_gnn_lin_w"), "lin_b": row("L0_gnn_lin_b"), "gru_wT": t("L0_gnn_weight"),
        "w_ihT": t("L0_gnn_w_ih"), "w_hhT": t("L0_gnn_w_hh"), "b_ih": row("L0_gnn_b_ih"), "b_hh": row("L0_gnn_b_hh"),
        "gat_W1": v["L1_gnn_W1"], "gat_W1T": t("L1_gnn_W1"), "gat_W2": v["L1_gnn_W2"], "gat_W2T": t("L1_gnn_W2"),
        "a1_src": v["L1_gnn_a1_src"], "a1_dst": v["L1_gnn_a1_dst"],
        "a2_src": v["L1_gnn_a2_src"], "a2_dst": v["L1_gnn_a2_dst"],
        "bn_b1": row("L1_gnn_b1"), "bn_g1": row("L1_gnn_g1"), "bn_be1": row("L1_gnn_beta1"),
        "bn_b2": row("L1_gnn_b2"), "bn_g2": row("L1_gnn_g2"), "bn_be2": row("L1_gnn_beta2"),
        "W_lT": t("L2_gnn_W_l"), "b_l": row("L2_gnn_b_l"), "W_rT": t("L2_gnn_W_r"),
        "W_e": v["L2_gnn_W_e"], "b_e": v["L2_gnn_b_e"],
        "W_in_w": v["L3_gnn_W_in_w"], "W_in_b": row("L3_gnn_W_in_b"),
        "W_updT": t("L3_gnn_W_upd_w"), "W_upd_b": v["L3_gnn_W_upd_b"],
        "W_out_w": v["L3_gnn_W_out_w"], "W_out_b": row("L3_gnn_W_out_b"),
        "ln1_g": row("L3_gnn_ln1_g"), "ln1_b": row("L3_gnn_ln1_b"),
        "ln2_g": row("L3_gnn_ln2_g"), "ln2_b": row("L3_gnn_ln2_b"),
        "ffn1_w": v["L3_gnn_ffn1_w"], "ffn1_b": v["L3_gnn_ffn1_b"],
        "ffn2_w": v["L3_gnn_ffn2_w"], "ffn2_b": row("L3_gnn_ffn2_b"),
    }
    nc = bacc.Bacc("TRN2", target_bir_lowering=False, num_devices=1)
    arrays, aps = {}, {}
    for name, a in host.items():
        arrays[f"in_{name}"] = np.ascontiguousarray(a)
        aps[name] = nc.dram_tensor(f"in_{name}", a.shape, mybir.dt.from_np(a.dtype), kind="ExternalInput").ap()
    out = nc.dram_tensor("out_x", (N, D), F32, kind="ExternalOutput").ap()
    graph_kernel(nc, aps, out)
    r = run_bass_kernel_spmd(nc, [arrays], core_ids=[0])
    return r.results[0]["out_x"]
```

```python
from contextlib import ExitStack

import concourse.bass as bass
from concourse import mybir

F32 = mybir.dt.float32
BF16 = mybir.dt.bfloat16
I32 = mybir.dt.int32
ALU = mybir.AluOpType
ACT = mybir.ActivationFunctionType
AX = mybir.AxisListType

P = 128
D = 128
N = 50000
E = 25000
ED = 32
HEADS = 4
FH = D // HEADS
HW = FH + 1
GW = HEADS * HW
GT = GW + HEADS
FFN = 4 * D

STEP = 2 * P
U = 14
GROUPS = -(-N // (STEP * U))
STEPS = GROUPS * U
NP = STEPS * STEP
LAST = (N - (STEPS - 1) * STEP) // 2

UE = 8
PSEUDO = 32
NEW = P - 1
TILES = -(-E // (NEW * UE)) * UE
NAT = -(-E // (P * UE)) * UE
PAD = 25728
OUTSIDE = 1.0e6
BIG = 1.0e30
EPS = 1e-5

assert STEPS * STEP >= N and (STEPS - 1) * STEP < N and N % 2 == 0


def wait(eng, sem, value):
    if isinstance(value, int) and value <= 0:
        return
    eng.wait_ge(sem, value)


def turns(eng, n):
    yield 0, False
    with eng.Fori(1, n - 1) as k:
        yield k, False
    yield n - 1, True


def pipeline(eng, n, slots, *parts):
    longest = max(lead for lead, _ in parts)
    assert longest < slots
    for j in range(longest):
        for lead, part in parts:
            if 0 <= j - (longest - lead):
                part(0, j - (longest - lead))
    for k, last in turns(eng, n):
        for j in range(slots):
            for lead, part in parts:
                if not last or j + lead < slots:
                    part(k + (j + lead) // slots, (j + lead) % slots)


class Link:

    def __init__(self, eng, sem, per_step):
        self.eng, self.sem, self.per_step, self.n, self.base = eng, sem, per_step, 0, 0

    def begin(self, step):
        assert self.n in (0, self.per_step), self.n
        self.base, self.n = step * self.per_step, 0

    def __call__(self, ins):
        ins.then_inc(self.sem, 1)
        self.n += 1
        self.eng.wait_ge(self.sem, self.base + self.n)


class Stage:

    def __init__(self, nc, name):
        self.nc, self.name, self.ctx, self.sems = nc, name, ExitStack(), []

    def __enter__(self):
        self.ctx.__enter__()
        return self

    def sb(self, name, shape, dt=F32):
        return self.ctx.enter_context(self.nc.sbuf_tensor(f"{self.name}_{name}", shape, dt))

    def bank(self, name, shape=(P, 512)):
        return self.ctx.enter_context(self.nc.psum_tensor(f"{self.name}_{name}", list(shape), F32))

    def sem(self, name):
        s = self.nc.alloc_semaphore(name=f"{self.name}_{name}")
        self.sems.append(s)
        return s

    def block(self):
        return self.ctx.enter_context(self.nc.Block())

    def __exit__(self, *exc):
        self.ctx.__exit__(*exc)
        if exc[0] is None:
            self.nc.clear_and_free_semaphores(self.sems)
            self.nc.all_engine_barrier()


def rows(table, step, width):
    return table[bass.ds(step * STEP, STEP), 0:width].rearrange("(p j) d -> p j d", j=2)




def prepare_weights(nc, A, C):
    with Stage(nc, "prep") as st:
        gw = st.sb("gw", [P, 3, D])
        wih = st.sb("wih", [P, 3 * D])
        g1 = st.sb("g1", [P, 2, D])
        a_blk = st.sb("a_blk", [P, 2, 8])
        web = st.sb("web", [P, 2, ED + 1])
        updT = st.sb("updT", [P, 2 * D])
        wout = st.sb("wout", [P, D])
        bupd = st.sb("bupd", [P, 1])
        brow = st.sb("brow", [1, C.NB])
        bmore = st.sb("bmore", [1, 2 * D])
        bout = st.sb("bout", [1, D])
        parts = st.sb("parts", [1, 3, C.NB], BF16)
        rest = st.sb("rest", [1, C.NB])
        acc = [st.bank(f"acc{i}") for i in range(8)]
        loaded, blocks_zero, placed = st.sem("loaded"), st.sem("blocks_zero"), st.sem("placed")
        ident0 = st.sem("ident0")
        ones_set = st.sem("ones_set")
        made, copied, own = st.sem("made"), st.sem("copied"), st.sem("own")
        parts_out, parts_in, split = st.sem("parts_out"), st.sem("parts_in"), st.sem("split")
        block = st.block()
        loads = [
            (gw[:, :, :], A["gru_wT"].rearrange("l m k -> m l k")),
            (wih[:, 0:D], A["w_ihT"][:, 2 * D:3 * D]), (wih[:, D:3 * D], A["w_ihT"][:, 0:2 * D]),
            (C.whh[:, :], A["w_hhT"]), (C.lin[:, :], A["lin_wT"]),
            (g1[:, 0, :], A["gat_W1T"]), (g1[:, 1, :], A["gat_W2T"]),
            (C.gat[:, 0, 0:D], A["gat_W1"]), (C.gat[:, 1, 0:D], A["gat_W2"]),
            (web[:, :, 0:ED], A["W_e"].rearrange("l h d -> h l d")),
            (web[:, :, ED:ED + 1], A["b_e"].rearrange("l (h o) -> h l o", o=1)),
            (C.wl[:, :, :], A["W_lT"].rearrange("l d h -> d l h")),
            (C.wr[:, :, :], A["W_rT"].rearrange("l d h -> d l h")),
            (C.win[:, :], A["W_in_w"]), (updT[:, :], A["W_updT"]), (wout[:, :], A["W_out_w"]),
            (bupd[:, :], A["W_upd_b"].rearrange("(p o) -> p o", o=1)),
            (C.ffn1[:, :], A["ffn1_w"]),
            (C.ffn2[:, :, :], A["ffn2_w"].rearrange("(b p) n -> p b n", p=P)),
            (C.ffn1_b[:, :], A["ffn1_b"].rearrange("(b p) -> p b", p=P)),
            (brow[:, C.B_LIN:C.B_LIN + D], A["lin_b"]),
            (brow[:, C.B_GRU:C.B_GRU + D], A["b_ih"][:, 2 * D:3 * D]),
            (brow[:, C.B_GRU + D:C.B_GRU + 3 * D], A["b_ih"][:, 0:2 * D]),
            (brow[:, C.B_GRU + 3 * D:C.B_GRU + 4 * D], A["b_hh"][:, 2 * D:3 * D]),
            (bmore[:, :], A["b_hh"][:, 0:2 * D]),
            (brow[:, C.B_L:C.B_L + 2 * D], A["b_l"]),
            (brow[:, C.B_IN:C.B_IN + D], A["W_in_b"]),
            (bout[:, :], A["W_out_b"]),
            (brow[:, C.B_F2:C.B_F2 + D], A["ffn2_b"]),
        ]
        for i, name in enumerate(C.BC):
            loads.append((C.bc[:, i, :], A[name].partition_broadcast(P)))
        n_loads = len(loads)

        @block.sync
        def _(sp):
            for out, in_ in loads:
                sp.dma_start(out, in_, allow_slow_non_contiguous=True).then_inc(loaded, 16)
            sp.wait_ge(blocks_zero, 1)
            for layer in range(2):
                for which, name in enumerate(("src", "dst")):
                    for h in range(HEADS):
                        src = A[f"a{layer + 1}_{name}"][h:h + 1, :].rearrange("o f -> f o")
                        sp.dma_start(a_blk[h * FH:(h + 1) * FH, layer, 4 * which + h:4 * which + h + 1],
                                     src, allow_slow_non_contiguous=True).then_inc(placed, 16)
            sp.wait_ge(split, 1)
            sp.dma_start(C.bias_dram.rearrange("(o a) n -> o a n", o=1), parts[:, :, :]).then_inc(parts_out, 16)
            sp.wait_ge(parts_out, 16)
            sp.dma_start(C.bias[:, :], C.bias_dram).then_inc(parts_in, 16)
            sp.wait_ge(parts_in, 16)
            sp.wait_ge(loaded, 16 * n_loads)

        @block.gpsimd
        def _(pool):
            pool.memset(C.ident[:, :], 0.0).then_inc(ident0, 1)
            pool.wait_ge(ident0, 1)
            pool.affine_select(out=C.ident[:, :], in_=C.ident[:, :], compare_op=ALU.not_equal, fill=1.0,
                               base=0, pattern=[[-1, P]], channel_multiplier=1).then_inc(ones_set, 1)
            pool.memset(C.ones[:, :], 1.0).then_inc(ones_set, 1)
            pool.memset(C.ones3[:, :], 1.0).then_inc(ones_set, 1)
            pool.memset(C.minus_half[:, :], -0.5).then_inc(ones_set, 1)

        @block.tensor
        def _(pe):
            pe.wait_ge(loaded, 16 * n_loads)
            pe.wait_ge(placed, 16 * 16)
            for i in range(3):
                pe.matmul(acc[i][:, 0:3 * D], gw[:, i, :], wih[:, :], start=True, stop=True)
            for i in range(2):
                pe.matmul(acc[3][:, 8 * i:8 * i + 8], g1[:, i, :], a_blk[:, i, :], start=True, stop=True)
            for i in range(2):
                pe.matmul(acc[4][0:ED + 1, i * D:(i + 1) * D], web[:, i, :], C.wl[:, i, :], start=True, stop=True)
            for i in range(2):
                pe.matmul(acc[5][:, i * D:(i + 1) * D], updT[:, i * D:(i + 1) * D], wout[:, :], start=True, stop=True)
            pe.matmul(acc[6][0:1, 0:D], bupd[:, :], wout[:, :], start=True, stop=True).then_inc(made, 1)

        @block.vector
        def _(dve):
            dve.memset(a_blk[:, :, :], 0.0).then_inc(blocks_zero, 1)
            dve.wait_ge(made, 1)
            for i in range(3):
                dve.tensor_copy(C.wc[:, i, :], acc[i][:, 0:3 * D]).then_inc(copied, 1)
            dve.tensor_copy(C.gat[:, :, D:D + 8], acc[3][:, 0:16].rearrange("p (l c) -> p l c", l=2)).then_inc(copied, 1)
            dve.tensor_copy(C.wel[:, :, :], acc[4][0:ED + 1, 0:2 * D].rearrange("p (l c) -> p l c", l=2)).then_inc(copied, 1)
            dve.tensor_copy(C.wf[:, :, :], acc[5][:, 0:2 * D].rearrange("p (l c) -> p l c", l=2)).then_inc(copied, 1)
            dve.tensor_tensor(brow[:, C.B_F:C.B_F + D], acc[6][0:1, 0:D], bout[:, :], ALU.add).then_inc(copied, 1)
            g = slice(C.B_GRU + D, C.B_GRU + 3 * D)
            dve.tensor_tensor(brow[:, g], brow[:, g], bmore[:, :], ALU.add).then_inc(copied, 1)
            dve.wait_ge(copied, 8)
            link = Link(dve, own, 4)
            link.begin(0)
            link(dve.tensor_copy(parts[:, 0, :], brow[:, :]))
            link(dve.tensor_tensor(rest[:, :], brow[:, :], parts[:, 0, :], ALU.subtract))
            link(dve.tensor_copy(parts[:, 1, :], rest[:, :]))
            link(dve.tensor_tensor(rest[:, :], rest[:, :], parts[:, 1, :], ALU.subtract))
            dve.tensor_copy(parts[:, 2, :], rest[:, :]).then_inc(split, 1)




def prepare_edges(nc, A, C):
    with Stage(nc, "pads") as st:
        ints = st.sb("ints", [125, 3, 200], I32)
        vals = st.sb("vals", [125, 3, 200])
        edge = st.sb("edge", [1, 3, PAD - E + 1])
        loaded, numbered, filled, turned, stored = (st.sem(n) for n in ("loaded", "numbered", "filled", "turned", "stored"))
        block = st.block()

        @block.sync
        def _(sp):
            sp.dma_start(ints[:, 0, :], A["src"].rearrange("(p c) -> p c", c=200)).then_inc(loaded, 16)
            sp.dma_start(ints[:, 1, :], A["dst"].rearrange("(p c) -> p c", c=200)).then_inc(loaded, 16)
            sp.wait_ge(filled, 4)
            for i in range(3):
                sp.dma_start(C.pad[i:i + 1, 0:1], edge[:, i, 0:1]).then_inc(stored, 16)
                sp.dma_start(C.pad[i:i + 1, E + 1:PAD], edge[:, i, 1:PAD - E]).then_inc(stored, 16)
            sp.wait_ge(turned, 1)
            for i in range(3):
                sp.dma_start(C.pad[i, 1:E + 1].rearrange("(p c) -> p c", c=200), vals[:, i, :]).then_inc(stored, 16)
            sp.wait_ge(stored, 16 * 9)

        @block.gpsimd
        def _(pool):
            pool.iota(ints[:, 2, :], pattern=[[1, 200]], base=0, channel_multiplier=200).then_inc(numbered, 1)

        @block.vector
        def _(dve):
            dve.memset(edge[:, 0, :], 0.0).then_inc(filled, 1)
            dve.memset(edge[:, 2, :], 0.0).then_inc(filled, 1)
            dve.memset(edge[:, 1, 0:1], -1.0).then_inc(filled, 1)
            dve.memset(edge[:, 1, 1:], OUTSIDE).then_inc(filled, 1)
            dve.wait_ge(loaded, 32)
            dve.wait_ge(numbered, 1)
            dve.tensor_copy(vals[:, :, :], ints[:, :, :]).then_inc(turned, 1)

    with Stage(nc, "lists") as st:
        t_src, t_dst, t_num, t_nxt, t_put = (st.sb(n, [P, 2, P]) for n in ("src", "dst", "num", "nxt", "put"))
        n_src, n_dst, n_nxt, n_prv, n_put, n_bias = (st.sb(n, [P, 2, P]) for n in ("nsrc", "ndst", "nnxt", "nprv", "nput", "nbias"))
        tps = [st.bank(f"tps{i}") for i in range(4)]
        loaded, own, ready, turned, stored, spread, done = (
            st.sem(n) for n in ("loaded", "own", "ready", "turned", "stored", "spread", "done"))
        block = st.block()
        sizes = [(0, P), (1, TILES - P)]
        nat_sizes = [(0, P), (1, NAT - P)]

        def load(sp, out, i, first, rowlen, n, b, c0, c1):
            at = 1 + first + b * P * rowlen
            src = C.pad[i, at:at + n * rowlen].rearrange("(t q) -> t q", q=rowlen)
            sp.dma_start(out[0:n, b, c0:c1], src[:, 0:c1 - c0], allow_slow_non_contiguous=True).then_inc(loaded, 16)
            return 1

        @block.sync
        def _(sp):
            n_loads = 0
            for b, n in sizes:
                for out, i, off in ((t_src, 0, 0), (t_dst, 1, 0), (t_num, 2, 0), (t_nxt, 1, 1)):
                    n_loads += load(sp, out, i, off + NEW - 1, NEW, n, b, 0, 1)
                    n_loads += load(sp, out, i, off, NEW, n, b, 1, PSEUDO)
                    n_loads += load(sp, out, i, off - 1, NEW, n, b, PSEUDO, PSEUDO + 1)
                    n_loads += load(sp, out, i, off + PSEUDO - 1, NEW, n, b, PSEUDO + 1, P)
            for b, n in nat_sizes:
                for out, i, off in ((n_src, 0, 0), (n_dst, 1, 0), (n_nxt, 1, 1), (n_prv, 1, -1)):
                    n_loads += load(sp, out, i, off, P, n, b, 0, P)
            assert n_loads == N_LIST_LOADS
            sp.wait_ge(loaded, 16 * n_loads)
            for b, n in sizes:
                sp.dma_start(C.dst_row[0, b * P * P:(b * P + n) * P].rearrange("(t q) -> t q", q=P),
                             t_dst[0:n, b, :]).then_inc(stored, 16)
            sp.wait_ge(ready, 1)
            for b, n in nat_sizes:
                sp.dma_start(C.bias_row[0, b * P * P:(b * P + n) * P].rearrange("(t q) -> t q", q=P),
                             n_bias[0:n, b, :]).then_inc(stored, 16)
            sp.wait_ge(stored, 64)
            sp.dma_start(C.targets[:, :], C.dst_row[0:1, :].partition_broadcast(P)).then_inc(spread, 16)
            sp.wait_ge(spread, 16)

        @block.vector
        def _(dve):
            link = Link(dve, own, 3 * 4 + 1 + 4)
            link.begin(0)
            dve.wait_ge(loaded, 16 * N_LIST_LOADS)
            for dst, nxt, put, sz in ((t_dst, t_nxt, t_put, sizes), (n_dst, n_nxt, n_put, nat_sizes)):
                for b, n in sz:
                    v = lambda x: x[0:n, b, :]
                    link(dve.tensor_tensor(v(nxt), v(dst), v(nxt), ALU.not_equal))
                    link(dve.scalar_tensor_tensor(out=v(put), in0=v(dst), scalar=-OUTSIDE, in1=v(nxt), op0=ALU.add, op1=ALU.mult))
                    link(dve.tensor_scalar(v(put), v(put), OUTSIDE, None, ALU.add))
            link(dve.memset(t_put[:, :, PSEUDO:PSEUDO + 1], OUTSIDE))
            for b, n in nat_sizes:
                link(dve.tensor_tensor(n_prv[0:n, b, :], n_dst[0:n, b, :], n_prv[0:n, b, :], ALU.is_equal))
                link(dve.tensor_scalar(n_bias[0:n, b, :], n_prv[0:n, b, :], BIG, -BIG, ALU.mult, ALU.add))
            dve.memset(n_prv[:, :, :], 0.0).then_inc(ready, 1)
            dve.wait_ge(turned, 1)
            for b, n in sizes:
                dve.tensor_copy(C.lists[:, b * P:b * P + n, :],
                                tps[b][:, :].rearrange("p (c t) -> p t c", c=4)[:, 0:n, :]).then_inc(done, 1)
            for b, n in nat_sizes:
                dve.tensor_copy(C.nat_lists[:, b * P:b * P + n, :],
                                tps[2 + b][:, 0:2 * P].rearrange("p (c t) -> p t c", c=2)[:, 0:n, :]).then_inc(done, 1)

        @block.tensor
        def _(pe):
            pe.wait_ge(ready, 1)
            for b, n in sizes:
                for c, x in enumerate((t_src, t_put, t_num, t_dst)):
                    pe.transpose(tps[b][:, c * P:c * P + n], x[0:n, b, :], C.ident[0:n, 0:n])
            for b, n in nat_sizes:
                for c, x in enumerate((n_src, n_put)):
                    last = pe.transpose(tps[2 + b][:, c * P:c * P + n], x[0:n, b, :], C.ident[0:n, 0:n])
            last.then_inc(turned, 1)


N_LIST_LOADS = 2 * 4 * 4 + 2 * 4


def clear_tables(nc, C, tables):
    with Stage(nc, "clear") as st:
        zeros = st.sb("zeros", [P, 8 * GT])
        lows = st.sb("lows", [P, 8, GT])
        filled, own, stored = st.sem("filled"), st.sem("own"), st.sem("stored")
        block = st.block()
        per = NP // P

        @block.sync
        def _(sp):
            sp.wait_ge(filled, 2)
            n = 0
            for table, width, low in tables:
                v = table.rearrange("(p r) d -> p r d", p=P)
                src = lows[:, :, :] if low else zeros[:, 0:8 * width].rearrange("p (r d) -> p r d", r=8)
                for r in range(0, per, 8):
                    sp.dma_start(v[:, r:r + 8, :], src).then_inc(stored, 16)
                    n += 1
            sp.wait_ge(stored, 16 * n)

        @block.vector
        def _(dve):
            dve.memset(zeros[:, :], 0.0).then_inc(filled, 1)
            dve.memset(lows[:, :, 0:GW], 0.0).then_inc(own, 1)
            dve.wait_ge(own, 1)
            dve.memset(lows[:, :, GW:GT], -BIG).then_inc(filled, 1)




def sum_edges(nc, C, name, table, width, sums, ones=False):
    total = width + ones
    first = 1 if ones else 0
    g_col, p_col = (1, 0) if ones else (0, 1)
    with Stage(nc, name) as st:
        msg = [st.sb(f"msg{j}", [P, total]) for j in range(UE)]
        sel = [st.sb(f"sel{j}", [P, P]) for j in range(UE)]
        out = [st.sb(f"out{j}", [P, total]) for j in range(UE)]
        ids = [st.sb(f"ids{j}", [P, 2], I32) for j in range(UE)]
        acc = [st.bank(f"acc{j}") for j in range(4)]
        listed, selected, carried, summed, copied, zeroed, issued = (
            st.sem(n) for n in ("listed", "selected", "carried", "summed", "copied", "zeroed", "issued"))
        gathered = [st.sem(f"gathered{j}") for j in range(UE)]
        put = [st.sem(f"put{j}") for j in range(UE)]
        block = st.block()
        n_turns = TILES // UE

        @block.vector
        def _(dve):
            for j in range(UE):
                if ones:
                    dve.memset(msg[j][:, :], 1.0).then_inc(zeroed, 1)
                dve.memset(out[j][:, :], 0.0).then_inc(zeroed, 1)
            for k, _ in turns(dve, n_turns):
                for j in range(UE):
                    t = UE * k + j
                    wait(dve, put[j], 16 * k)
                    dve.tensor_copy(ids[j][:, :], C.lists[:, bass.ds(t, 1), first:first + 2].rearrange("p o c -> p (o c)")).then_inc(listed, 1)
                    wait(dve, summed, t - UE + 1)
                    dve.tensor_scalar(sel[j][:, :], C.targets[:, bass.ds(t * P, P)],
                                      C.lists[:, bass.ds(t, 1), 3:4].rearrange("p o c -> p (o c)"), None, ALU.is_equal).then_inc(selected, 1)

        @block.gpsimd
        def _(pool):
            pool.wait_ge(zeroed, UE * (1 + ones))

            def gather(k, j):
                t = UE * k + j
                wait(pool, listed, t + 1)
                wait(pool, summed, t - UE + 1)
                pool.sem_inc(issued, 1)
                pool.indirect_dma_start(out=msg[j][:, 0:width], out_offset=None, in_=table,
                                        in_offset=bass.IndirectOffsetOnAxis(ap=ids[j][:, g_col:g_col + 1], axis=0),
                                        bounds_check=table.shape[0] - 1, oob_is_err=False).then_inc(gathered[j], 16)

            def scatter(k, j):
                wait(pool, copied, UE * k + j + 1)
                pool.sem_inc(issued, 1)
                pool.indirect_dma_start(out=sums, out_offset=bass.IndirectOffsetOnAxis(ap=ids[j][:, p_col:p_col + 1], axis=0),
                                        in_=out[j][:, :], in_offset=None,
                                        bounds_check=NP - 1, oob_is_err=False).then_inc(put[j], 16)

            pipeline(pool, n_turns, UE, (5, gather), (0, scatter))
            for j in range(UE):
                pool.wait_ge(put[j], 16 * n_turns)

        @block.scalar
        def _(act):
            act.wait_ge(zeroed, UE * (1 + ones))
            for k, _ in turns(act, n_turns):
                for j in range(UE):
                    t = UE * k + j
                    act.wait_ge(gathered[j], 16 * (k + 1))
                    wait(act, copied, t)
                    act.activation(msg[j][PSEUDO:PSEUDO + 1, :], out[(j - 1) % UE][0:1, :], ACT.Copy).then_inc(carried, 1)
                    act.wait_ge(summed, t + 1)
                    wait(act, put[j], 16 * k)
                    act.activation(out[j][:, :], acc[j % 4][:, 0:total], ACT.Copy).then_inc(copied, 1)

        @block.tensor
        def _(pe):
            for k, _ in turns(pe, n_turns):
                for j in range(UE):
                    t = UE * k + j
                    pe.wait_ge(selected, t + 1)
                    pe.wait_ge(carried, t + 1)
                    wait(pe, copied, t - 3)
                    pe.matmul(acc[j % 4][:, 0:total], sel[j][:, :], msg[j][:, :], start=True, stop=True).then_inc(summed, 1)


def max_edges(nc, C, name, table, maxima):
    with Stage(nc, name) as st:
        msg = [st.sb(f"msg{j}", [P, D]) for j in range(UE)]
        run = [st.sb(f"run{j}", [P, P]) for j in range(UE)]
        out = [st.sb(f"out{j}", [P, D]) for j in range(UE)]
        ids = [st.sb(f"ids{j}", [P, 2], I32) for j in range(UE)]
        turned_ps = [st.bank(f"turned{i}") for i in range(2)]
        back_ps = [st.bank(f"back{i}") for i in range(2)]
        biased, listed, turned, scanned, back, copied, issued, low = (
            st.sem(n) for n in ("biased", "listed", "turned_", "scanned", "back_", "copied", "issued", "low"))
        gathered = [st.sem(f"gathered{j}") for j in range(UE)]
        put = [st.sem(f"put{j}") for j in range(UE)]
        block = st.block()
        n_turns = NAT // UE
        bias = C.targets

        @block.sync
        def _(sp):
            sp.dma_start(bias[:, 0:NAT * P], C.bias_row[0:1, :].partition_broadcast(P)).then_inc(biased, 16)

        @block.gpsimd
        def _(pool):
            def gather(k, j):
                t = UE * k + j
                wait(pool, listed, t + 1)
                wait(pool, turned, t - UE + 1)
                pool.sem_inc(issued, 1)
                pool.indirect_dma_start(out=msg[j][:, :], out_offset=None, in_=table,
                                        in_offset=bass.IndirectOffsetOnAxis(ap=ids[j][:, 0:1], axis=0),
                                        bounds_check=NP - 1, oob_is_err=False).then_inc(gathered[j], 16)

            def scatter(k, j):
                wait(pool, copied, UE * k + j + 1)
                pool.sem_inc(issued, 1)
                pool.indirect_dma_start(out=maxima, out_offset=bass.IndirectOffsetOnAxis(ap=ids[j][:, 1:2], axis=0),
                                        in_=out[j][:, :], in_offset=None,
                                        bounds_check=NP - 1, oob_is_err=False).then_inc(put[j], 16)

            pipeline(pool, n_turns, UE, (5, gather), (0, scatter))
            for j in range(UE):
                pool.wait_ge(put[j], 16 * n_turns)

        @block.vector
        def _(dve):
            dve.memset(run[UE - 1][:, :], -BIG).then_inc(low, 1)
            dve.wait_ge(low, 1)
            dve.wait_ge(biased, 16)

            def indices(k, j):
                wait(dve, put[j], 16 * k)
                dve.tensor_copy(ids[j][:, :], C.nat_lists[:, bass.ds(UE * k + j, 1), :].rearrange("p o c -> p (o c)")).then_inc(listed, 1)

            def scan(k, j):
                t = UE * k + j
                dve.wait_ge(turned, t + 1)
                wait(dve, scanned, t)
                wait(dve, back, t - UE + 1)
                dve.tensor_tensor_scan(run[j][:, :], bias[:, bass.ds(t * P, P)], turned_ps[j % 2][:, 0:P],
                                       run[(j - 1) % UE][:, P - 1:P], ALU.add, ALU.max).then_inc(scanned, 1)

            pipeline(dve, n_turns, UE, (6, indices), (0, scan))

        @block.tensor
        def _(pe):
            def turn(k, j):
                t = UE * k + j
                pe.wait_ge(gathered[j], 16 * (k + 1))
                wait(pe, scanned, t - 1)
                pe.transpose(turned_ps[j % 2][:, 0:P], msg[j][:, :], C.ident[:, :]).then_inc(turned, 1)

            def turn_back(k, j):
                t = UE * k + j
                pe.wait_ge(scanned, t + 1)
                wait(pe, copied, t - 1)
                pe.transpose(back_ps[j % 2][:, 0:D], run[j][:, :], C.ident[:, :]).then_inc(back, 1)

            pipeline(pe, n_turns, UE, (1, turn), (0, turn_back))

        @block.scalar
        def _(act):
            for k, _ in turns(act, n_turns):
                for j in range(UE):
                    act.wait_ge(back, UE * k + j + 1)
                    wait(act, put[j], 16 * k)
                    act.activation(out[j][:, :], back_ps[j % 2][:, 0:D], ACT.Copy).then_inc(copied, 1)


def attend_edges(nc, C, name, table, dst_logits, result):
    with Stage(nc, name) as st:
        msg = [st.sb(f"msg{j}", [P, GT]) for j in range(UE)]
        ald = [st.sb(f"ald{j}", [P, HEADS]) for j in range(UE)]
        sel = [st.sb(f"sel{j}", [P, P]) for j in range(UE)]
        low = [st.sb(f"low{j}", [P, P]) for j in range(UE)]
        logit = [st.sb(f"logit{j}", [P, HEADS]) for j in range(UE)]
        masked = [st.sb(f"masked{i}", [P, HEADS, P]) for i in range(2)]
        inner = [st.sb(f"inner{j}", [P, HEADS]) for j in range(UE)]
        wgt = [st.sb(f"wgt{j}", [P, HEADS]) for j in range(UE)]
        out = [st.sb(f"out{j}", [P, GT]) for j in range(UE)]
        ids = [st.sb(f"ids{j}", [P, 2], I32) for j in range(UE)]
        idd = [st.sb(f"idd{j}", [P, 1], I32) for j in range(UE)]
        spread_ps = [st.bank(f"spread{i}") for i in range(2)]
        prev_ps = [st.bank(f"prev{i}") for i in range(2)]
        acc = [st.bank(f"acc{i}") for i in range(2)]
        zeroed, listed, selected, lowered, issued = (st.sem(n) for n in ("zeroed", "listed", "selected", "lowered", "issued"))
        joined, rectified, logits, blend, spread, inner_done, shared, peak, placed, weight, weighed, carried, message, summed, copied = (
            st.sem(n) for n in ("joined", "rectified", "logits", "blend", "spread_", "inner_", "shared", "peak", "placed", "weight",
                                "weighed", "carried", "message", "summed", "copied"))
        gathered = [st.sem(f"gathered{j}") for j in range(UE)]
        put = [st.sem(f"put{j}") for j in range(UE)]
        block = st.block()
        n_turns = TILES // UE

        @block.gpsimd
        def _(pool):
            def gather(k, j):
                t = UE * k + j
                wait(pool, listed, t + 1)
                wait(pool, summed, t - UE + 1)
                pool.sem_inc(issued, 1)
                pool.indirect_dma_start(out=msg[j][:, :], out_offset=None, in_=table,
                                        in_offset=bass.IndirectOffsetOnAxis(ap=ids[j][:, 0:1], axis=0),
                                        bounds_check=NP - 1, oob_is_err=False).then_inc(gathered[j], 16)
                pool.indirect_dma_start(out=ald[j][:, :], out_offset=None, in_=dst_logits,
                                        in_offset=bass.IndirectOffsetOnAxis(ap=idd[j][:, 0:1], axis=0),
                                        bounds_check=NP - 1, oob_is_err=False).then_inc(gathered[j], 16)

            def scatter(k, j):
                wait(pool, copied, UE * k + j + 1)
                pool.sem_inc(issued, 1)
                pool.indirect_dma_start(out=result, out_offset=bass.IndirectOffsetOnAxis(ap=ids[j][:, 1:2], axis=0),
                                        in_=out[j][:, :], in_offset=None,
                                        bounds_check=NP - 1, oob_is_err=False).then_inc(put[j], 16)

            pool.wait_ge(zeroed, 2 * UE)
            pipeline(pool, n_turns, UE, (5, gather), (0, scatter))
            for j in range(UE):
                pool.wait_ge(put[j], 16 * n_turns)

        @block.vector
        def _(dve):
            for j in range(UE):
                dve.memset(out[j][:, :], 0.0).then_inc(zeroed, 1)
                dve.memset(ald[j][:, :], 0.0).then_inc(zeroed, 1)
            dve.wait_ge(zeroed, 2 * UE)

            def select(k, j):
                t = UE * k + j
                wait(dve, put[j], 16 * k)
                dve.tensor_copy(ids[j][:, :], C.lists[:, bass.ds(t, 1), 0:2].rearrange("p o c -> p (o c)"))
                dve.tensor_scalar(idd[j][:, :], C.lists[:, bass.ds(t, 1), 3:4].rearrange("p o c -> p (o c)"),
                                  0.0, None, ALU.max).then_inc(listed, 1)
                wait(dve, summed, t - UE + 1)
                dve.tensor_scalar(sel[j][:, :], C.targets[:, bass.ds(t * P, P)],
                                  C.lists[:, bass.ds(t, 1), 3:4].rearrange("p o c -> p (o c)"), None, ALU.is_equal).then_inc(selected, 1)

            def add_logits(k, j):
                dve.wait_ge(gathered[j], 32 * (k + 1))
                dve.tensor_tensor(logit[j][:, :], msg[j][:, GW:GT], ald[j][:, :], ALU.add).then_inc(joined, 1)

            def mask(k, j):
                t = UE * k + j
                dve.wait_ge(logits, t + 1)
                dve.wait_ge(lowered, t + 1)
                wait(dve, spread, t - 1)
                dve.tensor_tensor(masked[j % 2][:, :, :],
                                  low[j][:, :].unsqueeze(1).to_broadcast([P, HEADS, P]),
                                  logit[j][:, :].unsqueeze(2).to_broadcast([P, HEADS, P]), ALU.add).then_inc(blend, 1)

            def reduce(k, j):
                t = UE * k + j
                dve.wait_ge(spread, t + 1)
                dve.tensor_reduce(inner[j][:, :], spread_ps[j % 2][:, :].rearrange("p (h e) -> p h e", h=HEADS),
                                  AX.X, ALU.max).then_inc(inner_done, 1)

            def fold(k, j):
                t = UE * k + j
                dve.wait_ge(shared, t + 1)
                wait(dve, put[j], 16 * k)
                dve.wait_ge(inner_done, t + 1)
                dve.scalar_tensor_tensor(out=out[j][:, GW:GT], in0=prev_ps[j % 2][:, 0:HEADS], scalar=low[j][:, PSEUDO:PSEUDO + 1],
                                         in1=inner[j][:, :], op0=ALU.add, op1=ALU.max).then_inc(peak, 1)
                dve.tensor_copy(logit[j][PSEUDO:PSEUDO + 1, :], prev_ps[j % 2][PSEUDO:PSEUDO + 1, 0:HEADS]).then_inc(placed, 1)

            def rectify(k, j):
                t = UE * k + j
                dve.wait_ge(joined, t + 1)
                dve.scalar_tensor_tensor(out=logit[j][:, :], in0=logit[j][:, :], scalar=0.2, in1=logit[j][:, :],
                                         op0=ALU.mult, op1=ALU.max).then_inc(rectified, 1)

            def silence(k, j):
                t = UE * k + j
                dve.wait_ge(rectified, t + 1)
                dve.memset(logit[j][PSEUDO:PSEUDO + 1, :], -BIG).then_inc(logits, 1)

            def subtract(k, j):
                t = UE * k + j
                dve.wait_ge(placed, t + 1)
                dve.tensor_tensor(wgt[j][:, :], logit[j][:, :], out[j][:, GW:GT], ALU.subtract).then_inc(weight, 1)

            def weigh(k, j):
                t = UE * k + j
                dve.wait_ge(weighed, t + 1)
                dve.wait_ge(carried, t + 1)
                dve.tensor_tensor(msg[j][:, 0:GW].rearrange("p (h f) -> p h f", h=HEADS),
                                  msg[j][:, 0:GW].rearrange("p (h f) -> p h f", h=HEADS),
                                  wgt[j][:, :].unsqueeze(2).to_broadcast([P, HEADS, HW]), ALU.mult).then_inc(message, 1)

            pipeline(dve, n_turns, UE, (6, select), (3, add_logits), (1, fold), (3, rectify), (2, reduce), (3, silence),
                     (1, subtract), (3, mask), (0, weigh))

        @block.scalar
        def _(act):
            act.wait_ge(zeroed, 2 * UE)

            def lower(k, j):
                t = UE * k + j
                wait(act, summed, t - UE + 1)
                act.wait_ge(selected, t + 1)
                act.activation(low[j][:, :], sel[j][:, :], ACT.Copy, bias=-BIG, scale=BIG).then_inc(lowered, 1)

            def exponent(k, j):
                act.wait_ge(weight, UE * k + j + 1)
                act.activation(wgt[j][:, :], wgt[j][:, :], ACT.Exp).then_inc(weighed, 1)

            def carry(k, j):
                t = UE * k + j
                act.wait_ge(gathered[j], 32 * (k + 1))
                wait(act, copied, t)
                act.activation(msg[j][PSEUDO:PSEUDO + 1, 0:GW], out[(j - 1) % UE][0:1, 0:GW], ACT.Copy).then_inc(carried, 1)

            def copy(k, j):
                t = UE * k + j
                act.wait_ge(summed, t + 1)
                wait(act, put[j], 16 * k)
                act.activation(out[j][:, 0:GW], acc[j % 2][:, 0:GW], ACT.Copy).then_inc(copied, 1)

            pipeline(act, n_turns, UE, (4, lower), (1, exponent), (0, carry), (0, copy))

        @block.tensor
        def _(pe):
            def turn(k, j):
                t = UE * k + j
                pe.wait_ge(blend, t + 1)
                wait(pe, inner_done, t - 1)
                for h in range(HEADS):
                    last = pe.transpose(spread_ps[j % 2][:, h * P:(h + 1) * P], masked[j % 2][:, h, :], C.ident[:, :])
                last.then_inc(spread, 1)

            def share(k, j):
                t = UE * k + j
                wait(pe, peak, t)
                wait(pe, placed, t - 1)
                pe.wait_ge(zeroed, 2 * UE)
                pe.matmul(prev_ps[j % 2][:, 0:HEADS], C.ones[0:1, :], out[(j - 1) % UE][0:1, GW:GT], start=True, stop=True).then_inc(shared, 1)

            def multiply(k, j):
                t = UE * k + j
                pe.wait_ge(message, t + 1)
                wait(pe, copied, t - 1)
                pe.matmul(acc[j % 2][:, 0:GW], sel[j][:, :], msg[j][:, 0:GW], start=True, stop=True).then_inc(summed, 1)

            pipeline(pe, n_turns, UE, (1, share), (3, turn), (0, multiply))




def load_rows(sp, buf, table, k, j, loaded, external):
    s = U * k + j
    width = buf.shape[-1]
    if external and isinstance(s, int) and s == STEPS - 1:
        src = table[s * STEP:N, 0:width].rearrange("(p j) d -> p j d", j=2)
        sp.dma_start(buf[0:LAST, :, :], src).then_inc(loaded[j], 16)
    else:
        sp.dma_start(buf[:, :, :], rows(table, s, width)).then_inc(loaded[j], 16)


def store_rows(sp, table, buf, k, j, stored, external=False):
    s = U * k + j
    width = buf.shape[-1]
    if external and isinstance(s, int) and s == STEPS - 1:
        dst = table[s * STEP:N, 0:width].rearrange("(p j) d -> p j d", j=2)
        sp.dma_start(dst, buf[0:LAST, :, :]).then_inc(stored[j], 16)
    else:
        sp.dma_start(rows(table, s, width), buf[:, :, :]).then_inc(stored[j], 16)


def sync_program(sp, n_in, loads, n_out, stores, loaded, used, stored, ready):
    def load(k, j):
        wait(sp, used, U * k + j - U + 1)
        loads(k, j)

    def store(k, j):
        wait(sp, ready, U * k + j + 1)
        stores(k, j)

    pipeline(sp, GROUPS, U, (U - 1, load), (0, store))
    for j in range(U):
        sp.wait_ge(stored[j], 16 * n_out * GROUPS)


def gru(nc, C, name, layer, h_in, sums, h_out):
    with Stage(nc, name) as st:
        h = [st.sb(f"h{j}", [P, 2, D]) for j in range(U)]
        agg = [st.sb(f"agg{j}", [P, 2, D]) for j in range(U)]
        out = [st.sb(f"out{j}", [P, 2, D]) for j in range(U)]
        hT = [st.sb(f"hT{i}", [P, 4, P]) for i in range(2)]
        rz = [st.sb(f"rz{i}", [P, 2, 2 * D]) for i in range(2)]
        cand = [st.sb(f"cand{i}", [P, 2, D]) for i in range(2)]
        t_ps = [st.bank(f"t{i}") for i in range(2)]
        g_ps = [st.bank(f"g{i}", (P, 2, 512)) for i in range(2)]
        loaded = [st.sem(f"loaded{j}") for j in range(U)]
        stored = [st.sem(f"stored{j}") for j in range(U)]
        turned, copied, gates, squashed, before, cands, own, done = (
            st.sem(n) for n in ("turned", "copied", "gates", "squashed", "before", "cands", "own", "done"))
        block = st.block()

        @block.sync
        def _(sp):
            def loads(k, j):
                load_rows(sp, h[j], h_in, k, j, loaded, False)
                load_rows(sp, agg[j], sums, k, j, loaded, False)

            sync_program(sp, 2, loads, 1, lambda k, j: store_rows(sp, h_out, out[j], k, j, stored),
                         loaded, done, stored, done)

        @block.tensor
        def _(pe):
            def turn(k, j):
                s = U * k + j
                pe.wait_ge(loaded[j], 32 * (k + 1))
                wait(pe, copied, s - 1)
                for i in range(2):
                    pe.transpose(t_ps[j % 2][:, i * P:(i + 1) * P], agg[j][:, i, :], C.ident[:, :])
                for i in range(2):
                    last = pe.transpose(t_ps[j % 2][:, (2 + i) * P:(3 + i) * P], h[j][:, i, :], C.ident[:, :])
                last.then_inc(turned, 1)

            def multiply(k, j):
                s = U * k + j
                pe.wait_ge(copied, s + 1)
                wait(pe, before, s - 1)
                for i in range(2):
                    g = g_ps[j % 2][:, i, :]
                    pe.matmul(g, C.ones3[:, :], C.bias[:, C.B_GRU:C.B_GRU + 4 * D], start=True, stop=False)
                    pe.matmul(g[:, 0:3 * D], hT[j % 2][:, i, :], C.wc[:, layer, :], start=False, stop=False)
                    last = pe.matmul(g[:, D:4 * D], hT[j % 2][:, 2 + i, :], C.whh[:, :], start=False, stop=True)
                last.then_inc(gates, 1)

            pipeline(pe, GROUPS, U, (1, turn), (0, multiply))

        @block.scalar
        def _(act):
            def copy(k, j):
                s = U * k + j
                act.wait_ge(turned, s + 1)
                wait(act, gates, s - 1)
                act.activation(hT[j % 2][:, :, :], t_ps[j % 2][:, :].rearrange("p (a b) -> p a b", a=4), ACT.Copy).then_inc(copied, 1)

            def squash(k, j):
                s = U * k + j
                act.wait_ge(gates, s + 1)
                wait(act, done, s - 1)
                act.activation(rz[j % 2][:, :, :], g_ps[j % 2][:, :, D:3 * D], ACT.Sigmoid).then_inc(squashed, 1)
                act.wait_ge(before, s + 1)
                act.activation(cand[j % 2][:, :, :], cand[j % 2][:, :, :], ACT.Tanh).then_inc(cands, 1)

            pipeline(act, GROUPS, U, (1, copy), (0, squash))

        @block.vector
        def _(dve):
            link = Link(dve, own, 3)
            for k, _ in turns(dve, GROUPS):
                for j in range(U):
                    s = U * k + j
                    link.begin(s)
                    c, r, z = cand[j % 2][:, :, :], rz[j % 2][:, :, 0:D], rz[j % 2][:, :, D:2 * D]
                    dve.wait_ge(squashed, s + 1)
                    link(dve.tensor_tensor(c, g_ps[j % 2][:, :, 3 * D:4 * D], r, ALU.mult))
                    dve.tensor_tensor(c, g_ps[j % 2][:, :, 0:D], c, ALU.add).then_inc(before, 1)
                    dve.wait_ge(cands, s + 1)
                    wait(dve, stored[j], 16 * k)
                    link(dve.tensor_tensor(out[j][:, :, :], h[j][:, :, :], c, ALU.subtract))
                    link(dve.tensor_tensor(out[j][:, :, :], out[j][:, :, :], z, ALU.mult))
                    dve.tensor_tensor(out[j][:, :, :], out[j][:, :, :], c, ALU.add).then_inc(done, 1)


class Norm:

    def __init__(self, st, name):
        self.stats = [st.sb(f"{name}_stats{j}", [P, 2, 6]) for j in range(U)]
        self.mv = [st.sb(f"{name}_mv{j}", [P, 2, 2]) for j in range(U)]
        self.rstd = [st.sb(f"{name}_rstd{j}", [P, 2]) for j in range(U)]
        self.counted, self.carrier = st.sem(f"{name}_counted"), st.sem(f"{name}_carrier")
        self.varied, self.begun, self.raised, self.rooted = (st.sem(f"{name}_{n}") for n in ("varied", "begun", "raised", "rooted"))

    def count(self, dve, x, j):
        for i in range(2):
            ins = dve.bn_stats(self.stats[j][:, i, :], x[:, i, :])
        ins.then_inc(self.counted, 1)

    def aggregate(self, dve, s, j):
        dve.wait_ge(self.counted, s + 1)
        dve.sem_inc(self.carrier, 1)
        for i in range(2):
            ins = dve.bn_aggr(self.mv[j][:, i, :], self.stats[j][:, i, :])
        ins.then_inc(self.varied, 1)

    def power(self, pool, C, s, j):
        pool.wait_ge(self.varied, s + 1)
        pool.sem_inc(self.begun, 1)
        var, rstd = self.mv[j][:, :, 1:2].rearrange("p j o -> p (j o)"), self.rstd[j][:, :]
        pool.tensor_scalar(rstd, var, EPS, None, ALU.add).then_inc(self.raised, 1)
        pool.wait_ge(self.raised, s + 1)
        pool.tensor_tensor(rstd, rstd, C.minus_half[:, :], ALU.pow).then_inc(self.rooted, 1)

    def scale(self, dve, out, x, s, j):
        dve.wait_ge(self.rooted, s + 1)
        for i in range(2):
            ins = dve.tensor_scalar(out[:, i, :], x[:, i, :], self.mv[j][:, i, 0:1], self.rstd[j][:, i:i + 1],
                                    ALU.subtract, ALU.mult)
        return ins


def transform(nc, C, name, front, a, b=None, bn=None, x_out=None, project=None, p_out=None, external=False):
    gat = project is not None and project[0] == "gat"
    with Stage(nc, name) as st:
        has_b = b is not None
        xa = [st.sb(f"xa{j}", [P, 2, D]) for j in range(U)]
        xb = [st.sb(f"xb{j}", [P, 2, D]) for j in range(U)] if has_b else None
        x = [st.sb(f"x{j}", [P, 2, D]) for j in range(U)]
        ex = [st.sb(f"ex{j}", [P, 2, D]) for j in range(U)] if bn is not None else None
        width = D + 8 if gat else D
        if project is not None:
            xT = [st.sb(f"xT{i}", [P, 2, P]) for i in range(2)]
            t_ps = [st.bank(f"t{i}") for i in range(2)]
            p_ps = [st.bank(f"p{i}") for i in range(2)]
            po = [st.sb(f"po{j}", [P, 2, GT if gat else D]) for j in range(U)]
            pd = [st.sb(f"pd{j}", [P, 2, HEADS]) for j in range(U)] if gat else None
        ln = Norm(st, "ln") if front in ("ln", "bn_ln") else None
        loaded = [st.sem(f"loaded{j}") for j in range(U)]
        stored = [st.sem(f"stored{j}") for j in range(U)]
        joined, scaled, shifted, lifted, fronted, turned, copied, multiplied, projected, low, exps, ones_set = (
            st.sem(n) for n in ("joined", "scaled", "shifted", "lifted", "fronted", "turned", "copied", "multiplied", "projected",
                                "low", "exps", "ones_set"))
        n_in = 1 + has_b
        n_out = (x_out is not None) + (project is not None) + gat
        ready = projected if project is not None else fronted
        block = st.block()

        @block.sync
        def _(sp):
            def loads(k, j):
                load_rows(sp, xa[j], a, k, j, loaded, external)
                if has_b:
                    load_rows(sp, xb[j], b, k, j, loaded, False)

            def stores(k, j):
                if x_out is not None:
                    store_rows(sp, x_out, x[j], k, j, stored)
                if project is not None:
                    store_rows(sp, p_out[0] if gat else p_out, po[j], k, j, stored)
                if gat:
                    store_rows(sp, p_out[1], pd[j], k, j, stored)

            sync_program(sp, n_in, loads, n_out, stores, loaded, ready, stored, ready)

        def put(eng, copy, k, j):
            s = U * k + j
            eng.wait_ge(multiplied, s + 1)
            wait(eng, stored[j], 16 * n_out * k)
            v = p_ps[j % 2][:, 0:2 * width].rearrange("p (a c) -> p a c", a=2)
            if gat:
                for i in range(2):
                    copy(po[j][:, i, 0:GW].rearrange("p (h f) -> p h f", h=HEADS)[:, :, 0:FH],
                         v[:, i, 0:D].rearrange("p (h f) -> p h f", h=HEADS))
                copy(po[j][:, :, GW:GT], v[:, :, D:D + 4])
                copy(pd[j][:, :, :], v[:, :, D + 4:D + 8]).then_inc(projected, 1)
            else:
                copy(po[j][:, :, :], v).then_inc(projected, 1)

        put_on_act = project is not None and front == "ln"

        @block.vector
        def _(dve):
            if gat:
                for j in range(U):
                    dve.memset(po[j][:, :, :], 1.0).then_inc(ones_set, 1)
                dve.wait_ge(ones_set, U)

            def take(k, j):
                dve.wait_ge(loaded[j], 16 * n_in * (k + 1))
                wait(dve, stored[j], 16 * n_out * k)

            def join(k, j):
                take(k, j)
                dve.tensor_tensor(x[j][:, :, :], xa[j][:, :, :], xb[j][:, :, :], ALU.add).then_inc(joined, 1)

            def multiply(k, j):
                take(k, j)
                dve.tensor_tensor(x[j][:, :, :], xa[j][:, :, :], bn[0][:, :].unsqueeze(1).to_broadcast([P, 2, D]), ALU.mult).then_inc(scaled, 1)

            def shift(k, j):
                dve.wait_ge(scaled, U * k + j + 1)
                dve.tensor_tensor(x[j][:, :, :], x[j][:, :, :], bn[1][:, :].unsqueeze(1).to_broadcast([P, 2, D]), ALU.add).then_inc(shifted, 1)

            def elu(k, j):
                dve.wait_ge(exps, U * k + j + 1)
                dve.scalar_tensor_tensor(out=x[j][:, :, :], in0=ex[j][:, :, :], scalar=-1.0, in1=x[j][:, :, :],
                                         op0=ALU.add, op1=ALU.max).then_inc(fronted if front == "bn" else lifted, 1)

            def join_elu(k, j):
                dve.wait_ge(lifted, U * k + j + 1)
                dve.tensor_tensor(x[j][:, :, :], x[j][:, :, :], xb[j][:, :, :], ALU.add).then_inc(joined, 1)

            def count(k, j):
                dve.wait_ge(joined, U * k + j + 1)
                ln.count(dve, x[j], j)

            def aggregate(k, j):
                ln.aggregate(dve, U * k + j, j)

            def scale(k, j):
                ln.scale(dve, x[j], x[j], U * k + j, j).then_inc(fronted, 1)

            def put_(k, j):
                put(dve, dve.tensor_copy, k, j)

            if front == "copy":
                parts = [(0, put_)]
            elif front == "ln":
                parts = [(4, join), (3, count), (2, aggregate), (0, scale)]
            elif front == "bn":
                parts = [(5, multiply), (4, shift), (2, elu), (0, put_)]
            else:
                parts = [(9, multiply), (8, shift), (6, elu), (5, join_elu), (4, count), (3, aggregate), (0, scale)]
            pipeline(dve, GROUPS, U, *parts)

        if ln is not None:
            @block.gpsimd
            def _(pool):
                for k, _ in turns(pool, GROUPS):
                    for j in range(U):
                        ln.power(pool, C, U * k + j, j)

        if project is not None:
            @block.tensor
            def _(pe):
                if gat:
                    w = C.gat[:, project[1], :]
                else:
                    w = project[0]

                def turn(k, j):
                    s = U * k + j
                    src = xa[j] if front == "copy" else x[j]
                    if front == "copy":
                        pe.wait_ge(loaded[j], 16 * (k + 1))
                    else:
                        pe.wait_ge(fronted, s + 1)
                    wait(pe, copied, s - 1)
                    for i in range(2):
                        last = pe.transpose(t_ps[j % 2][:, i * P:(i + 1) * P], src[:, i, :], C.ident[:, :])
                    last.then_inc(turned, 1)

                def multiply(k, j):
                    s = U * k + j
                    pe.wait_ge(copied, s + 1)
                    wait(pe, projected, s - 1)
                    for i in range(2):
                        g = p_ps[j % 2][:, i * width:(i + 1) * width]
                        if not gat:
                            pe.matmul(g, C.ones3[:, :], C.bias[:, project[1]:project[1] + D], start=True, stop=False)
                        last = pe.matmul(g, xT[j % 2][:, i, :], w, start=gat, stop=True)
                    last.then_inc(multiplied, 1)

                pipeline(pe, GROUPS, U, (1, turn), (0, multiply))

        if project is not None or bn is not None:
            @block.scalar
            def _(act):
                def lower(k, j):
                    act.wait_ge(shifted, U * k + j + 1)
                    wait(act, lifted if front == "bn_ln" else fronted, U * k + j - U + 1)
                    act.activation(ex[j][:, :, :], x[j][:, :, :], ACT.Relu, scale=-1.0).then_inc(low, 1)

                def lift(k, j):
                    act.wait_ge(low, U * k + j + 1)
                    act.activation(ex[j][:, :, :], ex[j][:, :, :], ACT.Exp, scale=-1.0).then_inc(exps, 1)

                def copy(k, j):
                    s = U * k + j
                    act.wait_ge(turned, s + 1)
                    wait(act, multiplied, s - 1)
                    act.activation(xT[j % 2][:, :, :], t_ps[j % 2][:, 0:2 * P].rearrange("p (a b) -> p a b", a=2), ACT.Copy).then_inc(copied, 1)

                def put_(k, j):
                    put(act, lambda out, in_: act.activation(out, in_, ACT.Copy), k, j)

                parts = []
                if bn is not None:
                    parts += [(4, lower), (3, lift)]
                if project is not None:
                    parts += [(1, copy)]
                if put_on_act:
                    parts += [(0, put_)]
                if not put_on_act:
                    parts = [(lead - parts[-1][0], part) for lead, part in parts]
                if put_on_act and gat:
                    act.wait_ge(ones_set, U)
                pipeline(act, GROUPS, U, *parts)


def merge_attention(nc, C, name, sums, table, dst_logits, out_table, gb, bn):
    with Stage(nc, name) as st:
        sm = [st.sb(f"sm{j}", [P, 2, GT]) for j in range(U)]
        tb = [st.sb(f"tb{j}", [P, 2, GT]) for j in range(U)]
        ad = [st.sb(f"ad{j}", [P, 2, HEADS]) for j in range(U)]
        lg = [st.sb(f"lg{j}", [P, 2, HEADS]) for j in range(U)]
        mx = [st.sb(f"mx{j}", [P, 2, HEADS]) for j in range(U)]
        df = [st.sb(f"df{j}", [P, 2, 2, HEADS]) for j in range(U)]
        rc = [st.sb(f"rc{j}", [P, 2, HEADS]) for j in range(U)]
        sq = [st.sb(f"sq{j}", [P, 2, D]) for j in range(2)]
        out = [st.sb(f"out{j}", [P, 2, D]) for j in range(U)]
        st1 = st.sb("st1", [P, 8, D])
        acc, acc2 = st.bank("acc"), st.bank("acc2")
        loaded = [st.sem(f"loaded{j}") for j in range(U)]
        stored = [st.sem(f"stored{j}") for j in range(U)]
        summed, leaked, highest, apart, factors, weighed, merged, inverted, done, squared, counted, own2, varied, rooted = (
            st.sem(n) for n in ("summed", "leaked", "highest", "apart", "factors", "weighed", "merged", "inverted", "done",
                                "squared", "counted", "own2", "varied", "rooted"))
        block = st.block()

        @block.sync
        def _(sp):
            def loads(k, j):
                load_rows(sp, sm[j], sums, k, j, loaded, False)
                load_rows(sp, tb[j], table, k, j, loaded, False)
                load_rows(sp, ad[j], dst_logits, k, j, loaded, False)

            sync_program(sp, 3, loads, 1, lambda k, j: store_rows(sp, out_table, out[j], k, j, stored),
                         loaded, done, stored, done)

        @block.vector
        def _(dve):
            heads = lambda v: v[:, :, 0:GW].rearrange("p j (h f) -> p j h f", h=HEADS)

            def add(k, j):
                dve.wait_ge(loaded[j], 48 * (k + 1))
                dve.tensor_tensor(lg[j][:, :, :], tb[j][:, :, GW:GT], ad[j][:, :, :], ALU.add).then_inc(summed, 1)

            def leak(k, j):
                dve.wait_ge(summed, U * k + j + 1)
                dve.scalar_tensor_tensor(out=lg[j][:, :, :], in0=lg[j][:, :, :], scalar=0.2, in1=lg[j][:, :, :],
                                         op0=ALU.mult, op1=ALU.max).then_inc(leaked, 1)

            def top(k, j):
                dve.wait_ge(leaked, U * k + j + 1)
                dve.tensor_tensor(mx[j][:, :, :], lg[j][:, :, :], sm[j][:, :, GW:GT], ALU.max).then_inc(highest, 1)

            def subtract(k, j):
                dve.wait_ge(highest, U * k + j + 1)
                dve.tensor_tensor(df[j][:, 0, :, :], sm[j][:, :, GW:GT], mx[j][:, :, :], ALU.subtract)
                dve.tensor_tensor(df[j][:, 1, :, :], lg[j][:, :, :], mx[j][:, :, :], ALU.subtract).then_inc(apart, 1)

            def weigh(k, j):
                dve.wait_ge(factors, U * k + j + 1)
                for i, v in enumerate((sm[j], tb[j])):
                    ins = dve.tensor_tensor(heads(v), heads(v), df[j][:, i, :, :].unsqueeze(3).to_broadcast([P, 2, HEADS, HW]), ALU.mult)
                ins.then_inc(weighed, 1)

            def merge(k, j):
                dve.wait_ge(weighed, U * k + j + 1)
                dve.tensor_tensor(heads(sm[j]), heads(sm[j]), heads(tb[j]), ALU.add).then_inc(merged, 1)

            def invert(k, j):
                dve.wait_ge(merged, U * k + j + 1)
                dve.reciprocal(rc[j][:, :, :].unsqueeze(3), heads(sm[j])[:, :, :, FH:HW]).then_inc(inverted, 1)

            def divide(k, j):
                s = U * k + j
                dve.wait_ge(inverted, s + 1)
                wait(dve, stored[j], 16 * k)
                wait(dve, counted, s - U + 1)
                dve.tensor_tensor(out[j][:, :, :].rearrange("p j (h f) -> p j h f", h=HEADS), heads(sm[j])[:, :, :, 0:FH],
                                  rc[j][:, :, :].unsqueeze(3).to_broadcast([P, 2, HEADS, FH]), ALU.mult).then_inc(done, 1)

            pipeline(dve, GROUPS, U, (9, add), (8, leak), (7, top), (6, subtract), (3, weigh), (2, merge), (1, invert), (0, divide))
            dve.wait_ge(counted, STEPS)
            g, be, bb = (C.bc[:, i, :] for i in gb)
            w = lambda i: st1[:, i, :]
            fin = Link(dve, own2, 8)
            fin.begin(0)
            fin(dve.tensor_copy(st1[:, 0:4, :], acc[:, :].rearrange("p (a d) -> p a d", a=4)))
            fin(dve.tensor_tensor(st1[:, 4:5, :], st1[:, 0:1, :], st1[:, 1:2, :], ALU.add))
            fin(dve.tensor_tensor(st1[:, 5:6, :], st1[:, 2:3, :], st1[:, 3:4, :], ALU.add))
            fin(dve.tensor_scalar(st1[:, 4:6, :], st1[:, 4:6, :], 1.0 / N, None, ALU.mult))
            fin(dve.tensor_tensor(w(0), w(4), w(4), ALU.mult))
            fin(dve.tensor_tensor(w(0), w(5), w(0), ALU.subtract))
            dve.tensor_scalar(w(0), w(0), EPS, None, ALU.add).then_inc(varied, 1)
            dve.memset(w(1), -0.5).then_inc(varied, 1)
            dve.wait_ge(rooted, 1)
            sc, sh = bn
            fin(dve.tensor_tensor(sc[:, :], w(2), g, ALU.mult))
            fin(dve.tensor_tensor(w(4), w(4), bb, ALU.add))
            dve.tensor_tensor(w(6), bb, w(4), ALU.subtract).then_inc(varied, 1)
            dve.wait_ge(varied, 3)
            dve.tensor_tensor(w(6), w(6), sc[:, :], ALU.mult).then_inc(varied, 1)
            dve.wait_ge(varied, 4)
            dve.tensor_tensor(sh[:, :], w(6), be, ALU.add).then_inc(varied, 1)

        @block.gpsimd
        def _(pool):
            pool.wait_ge(varied, 2)
            pool.tensor_tensor(st1[:, 2, :], st1[:, 0, :], st1[:, 1, :], ALU.pow).then_inc(rooted, 1)

        @block.scalar
        def _(act):
            def exponent(k, j):
                act.wait_ge(apart, U * k + j + 1)
                act.activation(df[j][:, :, :, :], df[j][:, :, :, :], ACT.Exp).then_inc(factors, 1)

            def square(k, j):
                s = U * k + j
                act.wait_ge(done, s + 1)
                wait(act, counted, s - 1)
                act.activation(sq[j % 2][:, :, :], out[j][:, :, :], ACT.Square).then_inc(squared, 1)

            pipeline(act, GROUPS, U, (5, exponent), (0, square))

        @block.tensor
        def _(pe):
            for k, last in turns(pe, GROUPS):
                for j in range(U):
                    s = U * k + j
                    pe.wait_ge(squared, s + 1)
                    end = last and j == U - 1
                    n = LAST if end else P
                    start = isinstance(k, int) and k == 0 and j == 0
                    pe.matmul(acc[:, 0:2 * D], C.ones[0:n, :], out[j][0:n, :, :].rearrange("p j d -> p (j d)"),
                              start=start, stop=False, skip_group_check=True)
                    pe.matmul(acc[:, 2 * D:4 * D], C.ones[0:n, :], sq[j % 2][0:n, :, :].rearrange("p j d -> p (j d)"),
                              start=False, stop=end, skip_group_check=True).then_inc(counted, 1)


def convolve(nc, C, name, layer, x_in, sums, edge_sums, y_out):
    with Stage(nc, name) as st:
        x = [st.sb(f"x{j}", [P, 2, D]) for j in range(U)]
        agg = [st.sb(f"agg{j}", [P, 2, D]) for j in range(U)]
        ea = [st.sb(f"ea{j}", [P, 2, ED + 1]) for j in range(U)]
        inv = [st.sb(f"inv{j}", [P, 2]) for j in range(U)]
        out = [st.sb(f"out{j}", [P, 2, D]) for j in range(U)]
        xT = [st.sb(f"xT{i}", [P, 4, P]) for i in range(2)]
        eT = [st.sb(f"eT{i}", [ED + 1, 2, P]) for i in range(2)]
        t_ps = [st.bank(f"t{i}") for i in range(2)]
        e_ps = [st.bank(f"e{i}") for i in range(2)]
        p_ps = [st.bank(f"p{i}") for i in range(2)]
        loaded = [st.sem(f"loaded{j}") for j in range(U)]
        stored = [st.sem(f"stored{j}") for j in range(U)]
        counted, inverted, scaled, turned, copied, e_copied, multiplied, done = (
            st.sem(n) for n in ("counted", "inverted", "scaled", "turned", "copied", "e_copied", "multiplied", "done"))
        block = st.block()

        @block.sync
        def _(sp):
            def loads(k, j):
                load_rows(sp, x[j], x_in, k, j, loaded, False)
                load_rows(sp, agg[j], sums, k, j, loaded, False)
                load_rows(sp, ea[j], edge_sums, k, j, loaded, False)

            sync_program(sp, 3, loads, 1, lambda k, j: store_rows(sp, y_out, out[j], k, j, stored),
                         loaded, done, stored, done)

        @block.vector
        def _(dve):
            def count(k, j):
                dve.wait_ge(loaded[j], 48 * (k + 1))
                dve.tensor_scalar(inv[j][:, :].unsqueeze(2), ea[j][:, :, ED:ED + 1], 1.0, None, ALU.max).then_inc(counted, 1)

            def invert(k, j):
                dve.wait_ge(counted, U * k + j + 1)
                dve.reciprocal(inv[j][:, :], inv[j][:, :]).then_inc(inverted, 1)

            def scale(k, j):
                dve.wait_ge(inverted, U * k + j + 1)
                dve.tensor_tensor(agg[j][:, :, :], agg[j][:, :, :], inv[j][:, :].unsqueeze(2).to_broadcast([P, 2, D]), ALU.mult)
                dve.tensor_tensor(ea[j][:, :, :], ea[j][:, :, :], inv[j][:, :].unsqueeze(2).to_broadcast([P, 2, ED + 1]),
                                  ALU.mult).then_inc(scaled, 1)

            def copy_e(k, j):
                s = U * k + j
                dve.wait_ge(turned, s + 1)
                wait(dve, multiplied, s - 1)
                dve.tensor_copy(eT[j % 2][:, :, :], e_ps[j % 2][0:ED + 1, 0:2 * P].rearrange("p (a b) -> p a b", a=2)).then_inc(e_copied, 1)

            pipeline(dve, GROUPS, U, (5, count), (4, invert), (3, scale), (0, copy_e))

        @block.tensor
        def _(pe):
            def turn(k, j):
                s = U * k + j
                pe.wait_ge(scaled, s + 1)
                wait(pe, copied, s - 1)
                wait(pe, e_copied, s - 1)
                for i in range(2):
                    pe.transpose(t_ps[j % 2][:, i * P:(i + 1) * P], agg[j][:, i, :], C.ident[:, :])
                    pe.transpose(t_ps[j % 2][:, (2 + i) * P:(3 + i) * P], x[j][:, i, :], C.ident[:, :])
                    last = pe.transpose(e_ps[j % 2][0:ED + 1, i * P:(i + 1) * P], ea[j][:, i, :], C.ident[:, :])
                last.then_inc(turned, 1)

            def multiply(k, j):
                s = U * k + j
                pe.wait_ge(copied, s + 1)
                pe.wait_ge(e_copied, s + 1)
                wait(pe, done, s - 1)
                for i in range(2):
                    g = p_ps[j % 2][:, i * D:(i + 1) * D]
                    pe.matmul(g, C.ones3[:, :], C.bias[:, C.B_L + layer * D:C.B_L + (layer + 1) * D], start=True, stop=False)
                    pe.matmul(g, xT[j % 2][:, i, :], C.wl[:, layer, :], start=False, stop=False)
                    pe.matmul(g, eT[j % 2][:, i, :], C.wel[:, layer, :], start=False, stop=False)
                    last = pe.matmul(g, xT[j % 2][:, 2 + i, :], C.wr[:, layer, :], start=False, stop=True)
                last.then_inc(multiplied, 1)

            pipeline(pe, GROUPS, U, (1, turn), (0, multiply))

        @block.scalar
        def _(act):
            def copy(k, j):
                s = U * k + j
                act.wait_ge(turned, s + 1)
                wait(act, multiplied, s - 1)
                act.activation(xT[j % 2][:, :, :], t_ps[j % 2][:, :].rearrange("p (a b) -> p a b", a=4), ACT.Copy).then_inc(copied, 1)

            def rectify(k, j):
                s = U * k + j
                act.wait_ge(multiplied, s + 1)
                wait(act, stored[j], 16 * k)
                act.activation(out[j][:, :, :], p_ps[j % 2][:, 0:2 * D].rearrange("p (a b) -> p a b", a=2), ACT.Relu).then_inc(done, 1)

            pipeline(act, GROUPS, U, (1, copy), (0, rectify))


def update(nc, C, name, x_in, h_in, maxima, edge_sums, x_out):
    with Stage(nc, name) as st:
        x = [st.sb(f"x{j}", [P, 2, D]) for j in range(U)]
        h = [st.sb(f"h{j}", [P, 2, D]) for j in range(U)]
        mx = [st.sb(f"mx{j}", [P, 2, D]) for j in range(U)]
        ea = [st.sb(f"ea{j}", [P, 2, ED + 1]) for j in range(U)]
        has = [st.sb(f"has{j}", [P, 2]) for j in range(U)]
        out = [st.sb(f"out{j}", [P, 2, D]) for j in range(U)]
        xT = [st.sb(f"xT{i}", [P, 4, P]) for i in range(2)]
        t_ps = [st.bank(f"t{i}") for i in range(2)]
        p_ps = [st.bank(f"p{i}") for i in range(2)]
        ln = Norm(st, "ln")
        loaded = [st.sem(f"loaded{j}") for j in range(U)]
        stored = [st.sem(f"stored{j}") for j in range(U)]
        known, parted, turned, copied, multiplied, added, normed, gained, done = (
            st.sem(n) for n in ("known", "parted", "turned", "copied", "multiplied", "added", "normed", "gained", "done"))
        block = st.block()

        @block.sync
        def _(sp):
            def loads(k, j):
                load_rows(sp, x[j], x_in, k, j, loaded, False)
                load_rows(sp, h[j], h_in, k, j, loaded, False)
                load_rows(sp, mx[j], maxima, k, j, loaded, False)
                load_rows(sp, ea[j], edge_sums, k, j, loaded, False)

            sync_program(sp, 4, loads, 1, lambda k, j: store_rows(sp, x_out, out[j], k, j, stored),
                         loaded, done, stored, done)

        @block.vector
        def _(dve):
            def subtract(k, j):
                dve.wait_ge(loaded[j], 64 * (k + 1))
                dve.tensor_scalar(has[j][:, :].unsqueeze(2), ea[j][:, :, ED:ED + 1], 1.0, None, ALU.min)
                dve.tensor_tensor(mx[j][:, :, :], mx[j][:, :, :], h[j][:, :, :], ALU.subtract).then_inc(known, 1)

            def part(k, j):
                dve.wait_ge(known, U * k + j + 1)
                dve.tensor_tensor(mx[j][:, :, :], mx[j][:, :, :], has[j][:, :].unsqueeze(2).to_broadcast([P, 2, D]),
                                  ALU.mult).then_inc(parted, 1)

            def add(k, j):
                s = U * k + j
                dve.wait_ge(multiplied, s + 1)
                wait(dve, stored[j], 16 * k)
                dve.tensor_tensor(out[j][:, :, :], p_ps[j % 2][:, 0:2 * D].rearrange("p (a b) -> p a b", a=2), x[j][:, :, :],
                                  ALU.add).then_inc(added, 1)

            def count(k, j):
                dve.wait_ge(added, U * k + j + 1)
                ln.count(dve, out[j], j)

            def aggregate(k, j):
                ln.aggregate(dve, U * k + j, j)

            def scale(k, j):
                ln.scale(dve, out[j], out[j], U * k + j, j).then_inc(normed, 1)

            def gain(k, j):
                dve.wait_ge(normed, U * k + j + 1)
                dve.tensor_tensor(out[j][:, :, :], out[j][:, :, :], C.bcast("ln1_g"), ALU.mult).then_inc(gained, 1)

            def shift(k, j):
                dve.wait_ge(gained, U * k + j + 1)
                dve.tensor_tensor(out[j][:, :, :], out[j][:, :, :], C.bcast("ln1_b"), ALU.add).then_inc(done, 1)

            pipeline(dve, GROUPS, U, (10, subtract), (9, part), (6, add), (5, count), (4, aggregate), (2, scale), (1, gain), (0, shift))

        @block.gpsimd
        def _(pool):
            for k, _ in turns(pool, GROUPS):
                for j in range(U):
                    ln.power(pool, C, U * k + j, j)

        @block.tensor
        def _(pe):
            def turn(k, j):
                s = U * k + j
                pe.wait_ge(parted, s + 1)
                wait(pe, copied, s - 1)
                for i in range(2):
                    pe.transpose(t_ps[j % 2][:, i * P:(i + 1) * P], h[j][:, i, :], C.ident[:, :])
                    last = pe.transpose(t_ps[j % 2][:, (2 + i) * P:(3 + i) * P], mx[j][:, i, :], C.ident[:, :])
                last.then_inc(turned, 1)

            def multiply(k, j):
                s = U * k + j
                pe.wait_ge(copied, s + 1)
                wait(pe, added, s - 1)
                for i in range(2):
                    g = p_ps[j % 2][:, i * D:(i + 1) * D]
                    pe.matmul(g, C.ones3[:, :], C.bias[:, C.B_F:C.B_F + D], start=True, stop=False)
                    pe.matmul(g, xT[j % 2][:, i, :], C.wf[:, 0, :], start=False, stop=False)
                    last = pe.matmul(g, xT[j % 2][:, 2 + i, :], C.wf[:, 1, :], start=False, stop=True)
                last.then_inc(multiplied, 1)

            pipeline(pe, GROUPS, U, (1, turn), (0, multiply))

        @block.scalar
        def _(act):
            for k, _ in turns(act, GROUPS):
                for j in range(U):
                    s = U * k + j
                    act.wait_ge(turned, s + 1)
                    wait(act, multiplied, s - 1)
                    act.activation(xT[j % 2][:, :, :], t_ps[j % 2][:, :].rearrange("p (a b) -> p a b", a=4), ACT.Copy).then_inc(copied, 1)


def feed_forward(nc, C, name, x4_in, x3_in, y_out):
    HB = FFN // P
    with Stage(nc, name) as st:
        x4 = [st.sb(f"x4{j}", [P, 2, D]) for j in range(U)]
        x3 = [st.sb(f"x3{j}", [P, 2, D]) for j in range(U)]
        out = [st.sb(f"out{j}", [P, 2, D]) for j in range(U)]
        xT = [st.sb(f"xT{i}", [P, 2 * P]) for i in range(2)]
        hid = [st.sb(f"hid{i}", [P, HB, 2 * P]) for i in range(2)]
        t_ps = [st.bank(f"t{i}") for i in range(2)]
        h_ps = [st.bank(f"h{i}") for i in range(HB)]
        p_ps = [st.bank(f"p{i}") for i in range(2)]
        ln2, ln = Norm(st, "lnb"), Norm(st, "ln")
        loaded = [st.sem(f"loaded{j}") for j in range(U)]
        stored = [st.sem(f"stored{j}") for j in range(U)]
        turned, copied, hidden, active, multiplied, added, normed, gained, shifted, joined, done = (
            st.sem(n) for n in ("turned", "copied", "hidden", "active", "multiplied", "added", "normed", "gained", "shifted",
                                "joined", "done"))
        block = st.block()

        @block.sync
        def _(sp):
            def loads(k, j):
                load_rows(sp, x4[j], x4_in, k, j, loaded, False)
                load_rows(sp, x3[j], x3_in, k, j, loaded, False)

            sync_program(sp, 2, loads, 1, lambda k, j: store_rows(sp, y_out, out[j], k, j, stored, external=True),
                         loaded, done, stored, done)

        @block.tensor
        def _(pe):
            def grow(k, j):
                s = U * k + j
                pe.wait_ge(loaded[j], 32 * (k + 1))
                wait(pe, copied, s - 1)
                for i in range(2):
                    last = pe.transpose(t_ps[j % 2][:, i * P:(i + 1) * P], x4[j][:, i, :], C.ident[:, :])
                last.then_inc(turned, 1)
                pe.wait_ge(copied, s + 1)
                for q in range(HB // 2):
                    wait(pe, active, (HB // 2) * (s - 2) + q + 1)
                    for b in range(2 * q, 2 * q + 2):
                        last = pe.matmul(h_ps[2 * (j % 2) + q][:, (b % 2) * 2 * P:(b % 2 + 1) * 2 * P],
                                         C.ffn1[:, b * P:(b + 1) * P], xT[j % 2][:, :], start=True, stop=True)
                    last.then_inc(hidden, 1)

            def shrink(k, j):
                s = U * k + j
                pe.wait_ge(active, (HB // 2) * (s + 1))
                wait(pe, added, s - 1)
                for i in range(2):
                    g = p_ps[j % 2][:, i * D:(i + 1) * D]
                    pe.matmul(g, C.ones3[:, :], C.bias[:, C.B_F2:C.B_F2 + D], start=True, stop=False)
                    for b in range(HB):
                        last = pe.matmul(g, hid[j % 2][:, b, i * P:(i + 1) * P], C.ffn2[:, b, :],
                                         start=False, stop=(b == HB - 1))
                last.then_inc(multiplied, 1)

            pipeline(pe, GROUPS, U, (1, grow), (0, shrink))

        @block.scalar
        def _(act):
            for k, _ in turns(act, GROUPS):
                for j in range(U):
                    s = U * k + j
                    act.wait_ge(turned, s + 1)
                    wait(act, hidden, (HB // 2) * (s - 1))
                    act.activation(xT[j % 2][:, :], t_ps[j % 2][:, 0:2 * P], ACT.Copy).then_inc(copied, 1)
                    wait(act, multiplied, s - 1)
                    for q in range(HB // 2):
                        act.wait_ge(hidden, (HB // 2) * s + q + 1)
                        for b in range(2 * q, 2 * q + 2):
                            last = act.activation(hid[j % 2][:, b, :], h_ps[2 * (j % 2) + q][:, (b % 2) * 2 * P:(b % 2 + 1) * 2 * P],
                                                  ACT.Gelu, bias=C.ffn1_b[:, b:b + 1])
                        last.then_inc(active, 1)

        @block.vector
        def _(dve):
            def add(k, j):
                s = U * k + j
                dve.wait_ge(multiplied, s + 1)
                wait(dve, stored[j], 16 * k)
                dve.tensor_tensor(out[j][:, :, :], p_ps[j % 2][:, 0:2 * D].rearrange("p (a b) -> p a b", a=2), x4[j][:, :, :],
                                  ALU.add).then_inc(added, 1)

            def count2(k, j):
                dve.wait_ge(added, U * k + j + 1)
                ln2.count(dve, out[j], j)

            def aggregate2(k, j):
                ln2.aggregate(dve, U * k + j, j)

            def scale2(k, j):
                ln2.scale(dve, out[j], out[j], U * k + j, j).then_inc(normed, 1)

            def gain(k, j):
                dve.wait_ge(normed, U * k + j + 1)
                dve.tensor_tensor(out[j][:, :, :], out[j][:, :, :], C.bcast("ln2_g"), ALU.mult).then_inc(gained, 1)

            def shift(k, j):
                dve.wait_ge(gained, U * k + j + 1)
                dve.tensor_tensor(out[j][:, :, :], out[j][:, :, :], C.bcast("ln2_b"), ALU.add).then_inc(shifted, 1)

            def join(k, j):
                dve.wait_ge(shifted, U * k + j + 1)
                dve.tensor_tensor(out[j][:, :, :], out[j][:, :, :], x3[j][:, :, :], ALU.add).then_inc(joined, 1)

            def count(k, j):
                dve.wait_ge(joined, U * k + j + 1)
                ln.count(dve, out[j], j)

            def aggregate(k, j):
                ln.aggregate(dve, U * k + j, j)

            def scale(k, j):
                ln.scale(dve, out[j], out[j], U * k + j, j).then_inc(done, 1)

            pipeline(dve, GROUPS, U, (11, add), (10, count2), (9, aggregate2), (7, scale2), (6, gain), (5, shift), (4, join),
                     (3, count), (2, aggregate), (0, scale))

        @block.gpsimd
        def _(pool):
            pipeline(pool, GROUPS, U, (8, lambda k, j: ln2.power(pool, C, U * k + j, j)), (0, lambda k, j: ln.power(pool, C, U * k + j, j)))




class Constants:
    BC = ["bn_g1", "bn_be1", "bn_b1", "bn_g2", "bn_be2", "bn_b2", "ln1_g", "ln1_b", "ln2_g", "ln2_b"]
    B_LIN, B_GRU, B_L, B_IN, B_F, B_F2 = 0, D, 5 * D, 7 * D, 8 * D, 9 * D
    NB = 10 * D

    def __init__(self, nc, ctx):
        def sb(name, shape, dt=F32):
            return ctx.enter_context(nc.sbuf_tensor(name, shape, dt))

        self.ident, self.ones = sb("ident", [P, P]), sb("ones", [P, P])
        self.ones3, self.minus_half = sb("ones3", [3, P], BF16), sb("minus_half", [P, 2])
        self.lin, self.whh, self.wc = sb("lin", [P, D]), sb("whh", [P, 3 * D]), sb("wc", [P, 3, 3 * D])
        self.gat = sb("gat", [P, 2, D + 8])
        self.wl, self.wr, self.wel = sb("wl", [P, 2, D]), sb("wr", [P, 2, D]), sb("wel", [ED + 1, 2, D])
        self.win, self.wf = sb("win", [P, D]), sb("wf", [P, 2, D])
        self.ffn1, self.ffn2, self.ffn1_b = sb("ffn1", [P, FFN]), sb("ffn2", [P, 4, D]), sb("ffn1_b", [P, 4])
        self.bias, self.bc = sb("bias", [3, self.NB], BF16), sb("bc", [P, len(self.BC), D])
        self.bn = [(sb(f"bn_scale{i}", [P, D]), sb(f"bn_shift{i}", [P, D])) for i in range(2)]
        self.lists, self.nat_lists = sb("lists", [P, TILES, 4]), sb("nat_lists", [P, NAT, 2])
        self.targets = sb("targets", [P, TILES * P])
        self.bias_dram = nc.dram_tensor("bias_dram", (3, self.NB), BF16).ap()
        self.pad = nc.dram_tensor("pad", (3, PAD), F32).ap()
        self.dst_row = nc.dram_tensor("dst_row", (1, TILES * P), F32).ap()
        self.bias_row = nc.dram_tensor("bias_row", (1, NAT * P), F32).ap()

    def bcast(self, name):
        return self.bc[:, self.BC.index(name), :].unsqueeze(1).to_broadcast([P, 2, D])


def graph_kernel(nc, A, out):
    with ExitStack() as ctx:
        C = Constants(nc, ctx)

        def table(name, width):
            return nc.dram_tensor(f"table_{name}", (NP, width), F32).ap()

        ha, hb, x1, x3 = (table(n, D) for n in ("ha", "hb", "x1", "x3"))
        agg, esum = table("agg", D), table("esum", ED + 1)
        gsum, gtab, gdst = table("gsum", GT), table("gtab", GT), table("gdst", HEADS)

        prepare_weights(nc, A, C)
        prepare_edges(nc, A, C)
        clear_tables(nc, C, [(agg, D, False), (esum, ED + 1, False), (gsum, GT, True)])
        sum_edges(nc, C, "Se", A["edge_attr"], ED, esum, ones=True)

        transform(nc, C, "T0", "copy", A["x"], project=(C.lin[:, :], C.B_LIN), p_out=ha, external=True)
        h, g = ha, hb
        for layer in range(3):
            sum_edges(nc, C, f"S{layer}", h, D, agg)
            gru(nc, C, f"G{layer}", layer, h, agg, g)
            h, g = g, h
        transform(nc, C, "T1", "ln", A["x"], h, x_out=x1, project=("gat", 0), p_out=(gtab, gdst), external=True)

        attend_edges(nc, C, "A1", gtab, gdst, gsum)
        merge_attention(nc, C, "M1", gsum, gtab, gdst, ha, (0, 1, 2), C.bn[0])
        transform(nc, C, "T2", "bn", ha, bn=C.bn[0], project=("gat", 1), p_out=(gtab, gdst))
        attend_edges(nc, C, "A2", gtab, gdst, gsum)
        merge_attention(nc, C, "M2", gsum, gtab, gdst, hb, (3, 4, 5), C.bn[1])
        transform(nc, C, "T3", "bn_ln", hb, x1, bn=C.bn[1], x_out=ha)

        sum_edges(nc, C, "S3", ha, D, agg)
        convolve(nc, C, "C1", 0, ha, agg, esum, hb)
        sum_edges(nc, C, "S4", hb, D, agg)
        convolve(nc, C, "C2", 1, hb, agg, esum, x1)
        transform(nc, C, "T4", "ln", ha, x1, x_out=x3, project=(C.win[:, :], C.B_IN), p_out=hb)

        max_edges(nc, C, "X5", hb, agg)
        update(nc, C, "U5", x3, hb, agg, esum, ha)
        feed_forward(nc, C, "F5", ha, x3, out)


def kernel(**inputs):
    import numpy as np
    import concourse.bacc as bacc
    from concourse.bass_utils import run_bass_kernel_spmd

    v = {name: np.asarray(a) for name, a in inputs.items()}

    def t(name):
        a = v[name]
        return np.ascontiguousarray(np.swapaxes(a, -1, -2))

    def row(name):
        return v[name].reshape(1, -1)

    host = {
        "x": v["x"], "src": v["src"], "dst": v["dst"], "edge_attr": v["edge_attr_32"],
        "lin_wT": t("L0_gnn_lin_w"), "lin_b": row("L0_gnn_lin_b"), "gru_wT": t("L0_gnn_weight"),
        "w_ihT": t("L0_gnn_w_ih"), "w_hhT": t("L0_gnn_w_hh"), "b_ih": row("L0_gnn_b_ih"), "b_hh": row("L0_gnn_b_hh"),
        "gat_W1": v["L1_gnn_W1"], "gat_W1T": t("L1_gnn_W1"), "gat_W2": v["L1_gnn_W2"], "gat_W2T": t("L1_gnn_W2"),
        "a1_src": v["L1_gnn_a1_src"], "a1_dst": v["L1_gnn_a1_dst"],
        "a2_src": v["L1_gnn_a2_src"], "a2_dst": v["L1_gnn_a2_dst"],
        "bn_b1": row("L1_gnn_b1"), "bn_g1": row("L1_gnn_g1"), "bn_be1": row("L1_gnn_beta1"),
        "bn_b2": row("L1_gnn_b2"), "bn_g2": row("L1_gnn_g2"), "bn_be2": row("L1_gnn_beta2"),
        "W_lT": t("L2_gnn_W_l"), "b_l": row("L2_gnn_b_l"), "W_rT": t("L2_gnn_W_r"),
        "W_e": v["L2_gnn_W_e"], "b_e": v["L2_gnn_b_e"],
        "W_in_w": v["L3_gnn_W_in_w"], "W_in_b": row("L3_gnn_W_in_b"),
        "W_updT": t("L3_gnn_W_upd_w"), "W_upd_b": v["L3_gnn_W_upd_b"],
        "W_out_w": v["L3_gnn_W_out_w"], "W_out_b": row("L3_gnn_W_out_b"),
        "ln1_g": row("L3_gnn_ln1_g"), "ln1_b": row("L3_gnn_ln1_b"),
        "ln2_g": row("L3_gnn_ln2_g"), "ln2_b": row("L3_gnn_ln2_b"),
        "ffn1_w": v["L3_gnn_ffn1_w"], "ffn1_b": v["L3_gnn_ffn1_b"],
        "ffn2_w": v["L3_gnn_ffn2_w"], "ffn2_b": row("L3_gnn_ffn2_b"),
    }
    nc = bacc.Bacc("TRN2", target_bir_lowering=False, num_devices=1)
    arrays, aps = {}, {}
    for name, a in host.items():
        arrays[f"in_{name}"] = np.ascontiguousarray(a)
        aps[name] = nc.dram_tensor(f"in_{name}", a.shape, mybir.dt.from_np(a.dtype), kind="ExternalInput").ap()
    out = nc.dram_tensor("out_x", (N, D), F32, kind="ExternalOutput").ap()
    graph_kernel(nc, aps, out)
    r = run_bass_kernel_spmd(nc, [arrays], core_ids=[0])
    return r.results[0]["out_x"]
```

```python
from contextlib import ExitStack

import concourse.bass as bass
from concourse import mybir

F32 = mybir.dt.float32
BF16 = mybir.dt.bfloat16
I32 = mybir.dt.int32
ALU = mybir.AluOpType
ACT = mybir.ActivationFunctionType
AX = mybir.AxisListType

P = 128
D = 128
N = 50000
E = 25000
ED = 32
HEADS = 4
FH = D // HEADS
HW = FH + 1
GW = HEADS * HW
GT = GW + HEADS
GX = GT + HEADS
FFN = 4 * D

STEP = 2 * P
U = 14
GROUPS = -(-N // (STEP * U))
STEPS = GROUPS * U
NP = STEPS * STEP
LAST = (N - (STEPS - 1) * STEP) // 2

UE = 8
PSEUDO = 32
NEW = P - 1
TILES = -(-E // (NEW * UE)) * UE
NAT = -(-E // (P * UE)) * UE
PAD = 25728
EW = ED + 3
OUTSIDE = 1.0e6
BIG = 1.0e30
EPS = 1e-5

assert STEPS * STEP >= N and (STEPS - 1) * STEP < N and N % 2 == 0


def wait(eng, sem, value):
    if isinstance(value, int) and value <= 0:
        return
    eng.wait_ge(sem, value)


def turns(eng, n):
    yield 0, False
    with eng.Fori(1, n - 1) as k:
        yield k, False
    yield n - 1, True


def pipeline(eng, n, slots, *parts):
    longest = max(lead for lead, _ in parts)
    assert longest < slots
    for j in range(longest):
        for lead, part in parts:
            if 0 <= j - (longest - lead):
                part(0, j - (longest - lead))
    for k, last in turns(eng, n):
        for j in range(slots):
            for lead, part in parts:
                if not last or j + lead < slots:
                    part(k + (j + lead) // slots, (j + lead) % slots)


class Link:

    def __init__(self, eng, sem, per_step):
        self.eng, self.sem, self.per_step, self.n, self.base = eng, sem, per_step, 0, 0

    def begin(self, step):
        assert self.n in (0, self.per_step), self.n
        self.base, self.n = step * self.per_step, 0

    def __call__(self, ins):
        ins.then_inc(self.sem, 1)
        self.n += 1
        self.eng.wait_ge(self.sem, self.base + self.n)


class Stage:

    def __init__(self, nc, name):
        self.nc, self.name, self.ctx, self.sems = nc, name, ExitStack(), []

    def __enter__(self):
        self.ctx.__enter__()
        return self

    def sb(self, name, shape, dt=F32):
        return self.ctx.enter_context(self.nc.sbuf_tensor(f"{self.name}_{name}", shape, dt))

    def bank(self, name, shape=(P, 512)):
        return self.ctx.enter_context(self.nc.psum_tensor(f"{self.name}_{name}", list(shape), F32))

    def sem(self, name):
        s = self.nc.alloc_semaphore(name=f"{self.name}_{name}")
        self.sems.append(s)
        return s

    def block(self):
        return self.ctx.enter_context(self.nc.Block())

    def __exit__(self, *exc):
        self.ctx.__exit__(*exc)
        if exc[0] is None:
            self.nc.clear_and_free_semaphores(self.sems)
            self.nc.all_engine_barrier()


def rows(table, step, width):
    return table[bass.ds(step * STEP, STEP), 0:width].rearrange("(p j) d -> p j d", j=2)




def prepare_weights(nc, A, C):
    with Stage(nc, "prep") as st:
        gw = st.sb("gw", [P, 3, D])
        wih = st.sb("wih", [P, 3 * D])
        g1 = st.sb("g1", [P, 2, D])
        a_blk = st.sb("a_blk", [P, 2, 8])
        web = st.sb("web", [P, 2, ED + 1])
        updT = st.sb("updT", [P, 2 * D])
        wout = st.sb("wout", [P, D])
        bupd = st.sb("bupd", [P, 1])
        brow = st.sb("brow", [1, C.NB])
        bmore = st.sb("bmore", [1, 2 * D])
        bout = st.sb("bout", [1, D])
        parts = st.sb("parts", [1, 3, C.NB], BF16)
        rest = st.sb("rest", [1, C.NB])
        acc = [st.bank(f"acc{i}") for i in range(8)]
        loaded, blocks_zero, placed = st.sem("loaded"), st.sem("blocks_zero"), st.sem("placed")
        ident0 = st.sem("ident0")
        ones_set = st.sem("ones_set")
        made, copied, own = st.sem("made"), st.sem("copied"), st.sem("own")
        parts_out, parts_in, split = st.sem("parts_out"), st.sem("parts_in"), st.sem("split")
        block = st.block()
        loads = [
            (gw[:, :, :], A["gru_wT"].rearrange("l m k -> m l k")),
            (wih[:, 0:D], A["w_ihT"][:, 2 * D:3 * D]), (wih[:, D:3 * D], A["w_ihT"][:, 0:2 * D]),
            (C.whh[:, :], A["w_hhT"]), (C.lin[:, :], A["lin_wT"]),
            (g1[:, 0, :], A["gat_W1T"]), (g1[:, 1, :], A["gat_W2T"]),
            (C.gat[:, 0, 0:D], A["gat_W1"]), (C.gat[:, 1, 0:D], A["gat_W2"]),
            (web[:, :, 0:ED], A["W_e"].rearrange("l h d -> h l d")),
            (web[:, :, ED:ED + 1], A["b_e"].rearrange("l (h o) -> h l o", o=1)),
            (C.wl[:, :, :], A["W_lT"].rearrange("l d h -> d l h")),
            (C.wr[:, :, :], A["W_rT"].rearrange("l d h -> d l h")),
            (C.win[:, :], A["W_in_w"]), (updT[:, :], A["W_updT"]), (wout[:, :], A["W_out_w"]),
            (bupd[:, :], A["W_upd_b"].rearrange("(p o) -> p o", o=1)),
            (C.ffn1[:, :], A["ffn1_w"]),
            (C.ffn2[:, :, :], A["ffn2_w"].rearrange("(b p) n -> p b n", p=P)),
            (C.ffn1_b[:, :], A["ffn1_b"].rearrange("(b p) -> p b", p=P)),
            (brow[:, C.B_LIN:C.B_LIN + D], A["lin_b"]),
            (brow[:, C.B_GRU:C.B_GRU + D], A["b_ih"][:, 2 * D:3 * D]),
            (brow[:, C.B_GRU + D:C.B_GRU + 3 * D], A["b_ih"][:, 0:2 * D]),
            (brow[:, C.B_GRU + 3 * D:C.B_GRU + 4 * D], A["b_hh"][:, 2 * D:3 * D]),
            (bmore[:, :], A["b_hh"][:, 0:2 * D]),
            (brow[:, C.B_L:C.B_L + 2 * D], A["b_l"]),
            (brow[:, C.B_IN:C.B_IN + D], A["W_in_b"]),
            (bout[:, :], A["W_out_b"]),
            (brow[:, C.B_F2:C.B_F2 + D], A["ffn2_b"]),
        ]
        for i, name in enumerate(C.BC):
            loads.append((C.bc[:, i, :], A[name].partition_broadcast(P)))
        n_loads = len(loads)

        @block.sync
        def _(sp):
            for out, in_ in loads:
                sp.dma_start(out, in_, allow_slow_non_contiguous=True).then_inc(loaded, 16)
            sp.wait_ge(blocks_zero, 1)
            for layer in range(2):
                for which, name in enumerate(("src", "dst")):
                    for h in range(HEADS):
                        src = A[f"a{layer + 1}_{name}"][h:h + 1, :].rearrange("o f -> f o")
                        sp.dma_start(a_blk[h * FH:(h + 1) * FH, layer, 4 * which + h:4 * which + h + 1],
                                     src, allow_slow_non_contiguous=True).then_inc(placed, 16)
            sp.wait_ge(split, 1)
            sp.dma_start(C.bias_dram.rearrange("(o a) n -> o a n", o=1), parts[:, :, :]).then_inc(parts_out, 16)
            sp.wait_ge(parts_out, 16)
            sp.dma_start(C.bias[:, :], C.bias_dram).then_inc(parts_in, 16)
            sp.wait_ge(parts_in, 16)
            sp.wait_ge(loaded, 16 * n_loads)

        @block.gpsimd
        def _(pool):
            pool.memset(C.ident[:, :], 0.0).then_inc(ident0, 1)
            pool.wait_ge(ident0, 1)
            pool.affine_select(out=C.ident[:, :], in_=C.ident[:, :], compare_op=ALU.not_equal, fill=1.0,
                               base=0, pattern=[[-1, P]], channel_multiplier=1).then_inc(ones_set, 1)
            pool.memset(C.ones[:, :], 1.0).then_inc(ones_set, 1)
            pool.memset(C.ones3[:, :], 1.0).then_inc(ones_set, 1)
            pool.memset(C.minus_half[:, :], -0.5).then_inc(ones_set, 1)

        @block.tensor
        def _(pe):
            pe.wait_ge(loaded, 16 * n_loads)
            pe.wait_ge(placed, 16 * 16)
            for i in range(3):
                pe.matmul(acc[i][:, 0:3 * D], gw[:, i, :], wih[:, :], start=True, stop=True)
            for i in range(2):
                pe.matmul(acc[3][:, 8 * i:8 * i + 8], g1[:, i, :], a_blk[:, i, :], start=True, stop=True)
            for i in range(2):
                pe.matmul(acc[4][0:ED + 1, i * D:(i + 1) * D], web[:, i, :], C.wl[:, i, :], start=True, stop=True)
            for i in range(2):
                pe.matmul(acc[5][:, i * D:(i + 1) * D], updT[:, i * D:(i + 1) * D], wout[:, :], start=True, stop=True)
            pe.matmul(acc[6][0:1, 0:D], bupd[:, :], wout[:, :], start=True, stop=True).then_inc(made, 1)

        @block.vector
        def _(dve):
            dve.memset(a_blk[:, :, :], 0.0).then_inc(blocks_zero, 1)
            dve.wait_ge(made, 1)
            for i in range(3):
                dve.tensor_copy(C.wc[:, i, :], acc[i][:, 0:3 * D]).then_inc(copied, 1)
            dve.tensor_copy(C.gat[:, :, D:D + 8], acc[3][:, 0:16].rearrange("p (l c) -> p l c", l=2)).then_inc(copied, 1)
            dve.tensor_copy(C.wel[:, :, :], acc[4][0:ED + 1, 0:2 * D].rearrange("p (l c) -> p l c", l=2)).then_inc(copied, 1)
            dve.tensor_copy(C.wf[:, :, :], acc[5][:, 0:2 * D].rearrange("p (l c) -> p l c", l=2)).then_inc(copied, 1)
            dve.tensor_tensor(brow[:, C.B_F:C.B_F + D], acc[6][0:1, 0:D], bout[:, :], ALU.add).then_inc(copied, 1)
            g = slice(C.B_GRU + D, C.B_GRU + 3 * D)
            dve.tensor_tensor(brow[:, g], brow[:, g], bmore[:, :], ALU.add).then_inc(copied, 1)
            dve.wait_ge(copied, 8)
            link = Link(dve, own, 4)
            link.begin(0)
            link(dve.tensor_copy(parts[:, 0, :], brow[:, :]))
            link(dve.tensor_tensor(rest[:, :], brow[:, :], parts[:, 0, :], ALU.subtract))
            link(dve.tensor_copy(parts[:, 1, :], rest[:, :]))
            link(dve.tensor_tensor(rest[:, :], rest[:, :], parts[:, 1, :], ALU.subtract))
            dve.tensor_copy(parts[:, 2, :], rest[:, :]).then_inc(split, 1)




def prepare_edges(nc, A, C):
    with Stage(nc, "pads") as st:
        ints = st.sb("ints", [125, 3, 200], I32)
        vals = st.sb("vals", [125, 3, 200])
        edge = st.sb("edge", [1, 3, PAD - E + 1])
        loaded, numbered, filled, turned, stored = (st.sem(n) for n in ("loaded", "numbered", "filled", "turned", "stored"))
        block = st.block()

        @block.sync
        def _(sp):
            sp.dma_start(ints[:, 0, :], A["src"].rearrange("(p c) -> p c", c=200)).then_inc(loaded, 16)
            sp.dma_start(ints[:, 1, :], A["dst"].rearrange("(p c) -> p c", c=200)).then_inc(loaded, 16)
            sp.wait_ge(filled, 4)
            for i in range(3):
                sp.dma_start(C.pad[i:i + 1, 0:1], edge[:, i, 0:1]).then_inc(stored, 16)
                sp.dma_start(C.pad[i:i + 1, E + 1:PAD], edge[:, i, 1:PAD - E]).then_inc(stored, 16)
            sp.wait_ge(turned, 1)
            for i in range(3):
                sp.dma_start(C.pad[i, 1:E + 1].rearrange("(p c) -> p c", c=200), vals[:, i, :]).then_inc(stored, 16)
            sp.wait_ge(stored, 16 * 9)

        @block.gpsimd
        def _(pool):
            pool.iota(ints[:, 2, :], pattern=[[1, 200]], base=0, channel_multiplier=200).then_inc(numbered, 1)

        @block.vector
        def _(dve):
            dve.memset(edge[:, 0, :], 0.0).then_inc(filled, 1)
            dve.memset(edge[:, 2, :], 0.0).then_inc(filled, 1)
            dve.memset(edge[:, 1, 0:1], -1.0).then_inc(filled, 1)
            dve.memset(edge[:, 1, 1:], OUTSIDE).then_inc(filled, 1)
            dve.wait_ge(loaded, 32)
            dve.wait_ge(numbered, 1)
            dve.tensor_copy(vals[:, :, :], ints[:, :, :]).then_inc(turned, 1)

    with Stage(nc, "lists") as st:
        rows_i = st.sb("rows_i", [P, TILES], I32)
        t_src, t_dst, t_num, t_nxt, t_put = (st.sb(n, [P, 2, P]) for n in ("src", "dst", "num", "nxt", "put"))
        t_seq = st.sb("seq", [P, 2, P])
        n_src, n_dst, n_prv, n_bias = (st.sb(n, [P, 2, P]) for n in ("nsrc", "ndst", "nprv", "nbias"))
        tps = [st.bank(f"tps{i}") for i in range(4)]
        loaded, own, ready, turned, stored, spread, done, numbered = (
            st.sem(n) for n in ("loaded", "own", "ready", "turned", "stored", "spread", "done", "numbered"))
        block = st.block()
        sizes = [(0, P), (1, TILES - P)]
        nat_sizes = [(0, P), (1, NAT - P)]

        def load(sp, out, i, first, rowlen, n, b, c0, c1):
            at = 1 + first + b * P * rowlen
            src = C.pad[i, at:at + n * rowlen].rearrange("(t q) -> t q", q=rowlen)
            sp.dma_start(out[0:n, b, c0:c1], src[:, 0:c1 - c0], allow_slow_non_contiguous=True).then_inc(loaded, 16)
            return 1

        @block.sync
        def _(sp):
            n_loads = 0
            for b, n in sizes:
                for out, i, off in ((t_src, 0, 0), (t_dst, 1, 0), (t_num, 2, 0), (t_nxt, 1, 1)):
                    n_loads += load(sp, out, i, off + NEW - 1, NEW, n, b, 0, 1)
                    n_loads += load(sp, out, i, off, NEW, n, b, 1, PSEUDO)
                    n_loads += load(sp, out, i, off - 1, NEW, n, b, PSEUDO, PSEUDO + 1)
                    n_loads += load(sp, out, i, off + PSEUDO - 1, NEW, n, b, PSEUDO + 1, P)
                n_loads += load(sp, t_seq, 1, -1, NEW, n, b, 0, 1)
                n_loads += load(sp, t_seq, 1, 0, NEW, n, b, 1, P)
            for b, n in nat_sizes:
                for out, i, off in ((n_src, 0, 0), (n_dst, 1, 0), (n_prv, 1, -1)):
                    n_loads += load(sp, out, i, off, P, n, b, 0, P)
            assert n_loads == N_LIST_LOADS
            sp.wait_ge(loaded, 16 * n_loads)
            for b, n in sizes:
                sp.dma_start(C.dst_row[0, b * P * P:(b * P + n) * P].rearrange("(t q) -> t q", q=P),
                             t_dst[0:n, b, :]).then_inc(stored, 16)
            sp.wait_ge(ready, 1)
            for b, n in nat_sizes:
                sp.dma_start(C.bias_row[0, b * P * P:(b * P + n) * P].rearrange("(t q) -> t q", q=P),
                             n_bias[0:n, b, :]).then_inc(stored, 16)
            sp.wait_ge(stored, 64)
            sp.dma_start(C.targets[:, :], C.dst_row[0:1, :].partition_broadcast(P)).then_inc(spread, 16)
            sp.wait_ge(spread, 16)

        @block.vector
        def _(dve):
            link = Link(dve, own, 3 * 2 + 2 + 4)
            link.begin(0)
            dve.wait_ge(loaded, 16 * N_LIST_LOADS)
            for b, n in sizes:
                dst, nxt, put = (x[0:n, b, :] for x in (t_dst, t_nxt, t_put))
                link(dve.tensor_tensor(nxt, dst, nxt, ALU.not_equal))
                link(dve.scalar_tensor_tensor(out=put, in0=dst, scalar=-OUTSIDE, in1=nxt, op0=ALU.add, op1=ALU.mult))
                link(dve.tensor_scalar(put, put, OUTSIDE, None, ALU.add))
            link(dve.memset(t_put[:, :, PSEUDO:PSEUDO + 1], OUTSIDE))
            link(dve.memset(t_src[:, :, PSEUDO:PSEUDO + 1], OUTSIDE))
            for b, n in nat_sizes:
                link(dve.tensor_tensor(n_prv[0:n, b, :], n_dst[0:n, b, :], n_prv[0:n, b, :], ALU.is_equal))
                link(dve.tensor_scalar(n_bias[0:n, b, :], n_prv[0:n, b, :], BIG, -BIG, ALU.mult, ALU.add))
            dve.memset(n_prv[:, :, :], 0.0).then_inc(ready, 1)
            dve.wait_ge(turned, 1)
            for b, n in sizes:
                dve.tensor_copy(C.lists[:, b * P:b * P + n, 0:4],
                                tps[b][:, :].rearrange("p (c t) -> p t c", c=4)[:, 0:n, :]).then_inc(done, 1)
            for b, n in nat_sizes:
                dve.tensor_copy(C.nat_lists[:, b * P:b * P + n, :],
                                tps[2 + b][:, 0:P].rearrange("p (c t) -> p t c", c=1)[:, 0:n, :]).then_inc(done, 1)
            for b, n in sizes:
                dve.tensor_copy(C.lists[:, b * P:b * P + n, 5:6],
                                tps[2 + b][:, P:2 * P].rearrange("p (c t) -> p t c", c=1)[:, 0:n, :]).then_inc(done, 1)
            dve.wait_ge(numbered, 1)
            dve.tensor_copy(C.lists[:, :, 4:5].rearrange("p t o -> p (t o)"), rows_i[:, :]).then_inc(done, 1)
            dve.wait_ge(done, 2)
            dve.tensor_scalar(C.lists[:, :, 3:4], C.lists[:, :, 3:4], float(P), None, ALU.add).then_inc(done, 1)

        @block.gpsimd
        def _(pool):
            pool.iota(rows_i[:, :], pattern=[[P, TILES]], base=P, channel_multiplier=1).then_inc(numbered, 1)

        @block.tensor
        def _(pe):
            pe.wait_ge(ready, 1)
            for b, n in sizes:
                for c, x in enumerate((t_src, t_put, t_dst, t_num)):
                    pe.transpose(tps[b][:, c * P:c * P + n], x[0:n, b, :], C.ident[0:n, 0:n])
                pe.transpose(tps[2 + b][:, P:P + n], t_seq[0:n, b, :], C.ident[0:n, 0:n])
            for b, n in nat_sizes:
                last = pe.transpose(tps[2 + b][:, 0:n], n_src[0:n, b, :], C.ident[0:n, 0:n])
            last.then_inc(turned, 1)


N_LIST_LOADS = 2 * 4 * 4 + 2 * 2 + 2 * 3


def clear_tables(nc, C, edge_sums, firsts):
    per = NP // P
    chunk = 56
    with Stage(nc, "clear") as st:
        zeros = st.sb("zeros", [P, chunk * EW])
        low = st.sb("low", [P, GT])
        filled, own, stored = st.sem("filled"), st.sem("own"), st.sem("stored")
        block = st.block()

        @block.sync
        def _(sp):
            sp.wait_ge(filled, 2)
            n = 0
            v = edge_sums.rearrange("(p r) d -> p r d", p=P)
            for r in range(0, per, chunk):
                sp.dma_start(v[:, r:r + chunk, :], zeros[:, :].rearrange("p (r d) -> p r d", d=EW)).then_inc(stored, 16)
                n += 1
            for table, width in firsts:
                sp.dma_start(table[0:P, :], low[:, :] if width == GT else zeros[:, 0:width]).then_inc(stored, 16)
                n += 1
            sp.wait_ge(stored, 16 * n)

        @block.vector
        def _(dve):
            dve.memset(zeros[:, :], 0.0).then_inc(filled, 1)
            dve.memset(low[:, 0:GW], 0.0).then_inc(own, 1)
            dve.wait_ge(own, 1)
            dve.memset(low[:, GW:GT], -BIG).then_inc(filled, 1)




def block_rows(table, t):
    return table[bass.ds((t + 1) * P, P), :]


def store_tiles(sp, n_turns, table, out, copied, put):
    for k, _ in turns(sp, n_turns):
        for j in range(UE):
            sp.wait_ge(copied, UE * k + j + 1)
            sp.dma_start(block_rows(table, UE * k + j), out[j][:, :]).then_inc(put[j], 16)
    for j in range(UE):
        sp.wait_ge(put[j], 16 * n_turns)


def sum_edges(nc, C, name, table, sums, attributes=False, places=False):
    width = ED if attributes else D
    total = width + attributes
    with Stage(nc, name) as st:
        msg = [st.sb(f"msg{j}", [P, total]) for j in range(UE)]
        sel = [st.sb(f"sel{j}", [P, P]) for j in range(UE)]
        goes_on = [st.sb(f"goes_on{j}", [1, P]) for j in range(UE)]
        out = [st.sb(f"out{j}", [P, EW if attributes else D]) for j in range(UE)]
        ids = [st.sb(f"ids{j}", [P, 1], I32) for j in range(UE)]
        acc = [st.bank(f"acc{j}") for j in range(4)]
        listed, selected, summed, copied, zeroed, own, issued = (
            st.sem(n) for n in ("listed", "selected", "summed", "copied", "zeroed", "own", "issued"))
        gathered = [st.sem(f"gathered{j}") for j in range(UE)]
        put = [st.sem(f"put{j}") for j in range(UE)]
        placed = st.sem("placed")
        block = st.block()
        n_turns = TILES // UE
        n_zeroed = 2 * UE
        empty = 0 if attributes else PSEUDO
        targets = 5 if attributes else 2
        column = 1 if attributes else 0

        @block.vector
        def _(dve):
            for j in range(UE):
                if attributes:
                    dve.memset(msg[j][:, :], 1.0).then_inc(own, 1)
                    dve.wait_ge(own, j + 1)
                    dve.memset(msg[j][empty:empty + 1, :], 0.0).then_inc(zeroed, 1)
                else:
                    dve.memset(msg[j][:, :], 0.0).then_inc(zeroed, 1)
                dve.memset(out[j][:, :], 0.0).then_inc(zeroed, 1)
            dve.wait_ge(zeroed, n_zeroed)
            for k, _ in turns(dve, n_turns):
                for j in range(UE):
                    t = UE * k + j
                    if attributes:
                        wait(dve, put[j], 16 * k)
                        dve.tensor_copy(out[j][:, ED + 1:EW], C.lists[:, bass.ds(t, 1), 3:5].rearrange("p o c -> p (o c)")).then_inc(placed, 1)
                    else:
                        wait(dve, gathered[j], 16 * k)
                    dve.tensor_copy(ids[j][:, :], C.lists[:, bass.ds(t, 1), column:column + 1].rearrange("p o c -> p (o c)")).then_inc(listed, 1)
                    wait(dve, summed, t - UE + 1)
                    dve.tensor_scalar(sel[j][:, :], C.targets[:, bass.ds(t * P, P)],
                                      C.lists[:, bass.ds(t, 1), targets:targets + 1].rearrange("p o c -> p (o c)"), None, ALU.is_equal)
                    dve.tensor_scalar(goes_on[j][:, :], C.targets[0:1, bass.ds(t * P, P)],
                                      C.targets[0:1, bass.ds(t * P + PSEUDO, 1)], None, ALU.is_equal).then_inc(selected, 1)

        @block.gpsimd
        def _(pool):
            pool.wait_ge(zeroed, n_zeroed)

            def gather(k, j):
                t = UE * k + j
                pool.wait_ge(listed, t + 1)
                wait(pool, summed, t - UE + 1)
                pool.sem_inc(issued, 1)
                pool.indirect_dma_start(out=msg[j][:, :], out_offset=None, in_=table,
                                        in_offset=bass.IndirectOffsetOnAxis(ap=ids[j][:, 0:1], axis=0),
                                        bounds_check=NP - 1, oob_is_err=False).then_inc(gathered[j], 16)

            def scatter(k, j):
                t = UE * k + j
                pool.wait_ge(listed, t + 1)
                pool.wait_ge(placed, t + 1)
                pool.wait_ge(copied, t + 1)
                pool.sem_inc(issued, 1)
                pool.indirect_dma_start(out=sums, out_offset=bass.IndirectOffsetOnAxis(ap=ids[j][:, 0:1], axis=0),
                                        in_=out[j][:, :], in_offset=None,
                                        bounds_check=NP - 1, oob_is_err=False).then_inc(put[j], 16)

            for k, _ in turns(pool, n_turns):
                for j in range(UE):
                    (scatter if attributes else gather)(k, j)
            if attributes:
                for j in range(UE):
                    pool.wait_ge(put[j], 16 * n_turns)

        @block.sync
        def _(sp):
            if not attributes:
                if places:
                    for i in range(2):
                        sp.dma_start(C.place_f[:, :, i, :],
                                     C.edge_sums.rearrange("(s p j) d -> p s j d", p=P, j=2)[:, :, i, ED + 1:EW],
                                     allow_slow_non_contiguous=True).then_inc(placed, 16)
                store_tiles(sp, n_turns, sums, out, copied, put)
                if places:
                    sp.wait_ge(placed, 32)
                return
            sp.wait_ge(zeroed, n_zeroed)
            for k, _ in turns(sp, n_turns):
                for j in range(UE):
                    t = UE * k + j
                    wait(sp, summed, t - UE + 1)
                    n = max(0, min(NEW, E - NEW * t)) if isinstance(t, int) else NEW
                    if n:
                        sp.dma_start(msg[j][1:1 + n, 0:ED], table[bass.ds(NEW * t, n), :]).then_inc(gathered[j], 16)
                    else:
                        sp.sem_inc(gathered[j], 16)

        @block.scalar
        def _(act):
            act.wait_ge(zeroed, n_zeroed)
            for k, _ in turns(act, n_turns):
                for j in range(UE):
                    t = UE * k + j
                    act.wait_ge(summed, t + 1)
                    wait(act, put[j], 16 * k)
                    act.activation(out[j][:, 0:total], acc[j % 4][:, 0:total], ACT.Copy).then_inc(copied, 1)

        @block.tensor
        def _(pe):
            pe.wait_ge(zeroed, n_zeroed)

            def gather_sums(k, j):
                t = UE * k + j
                pe.wait_ge(selected, t + 1)
                pe.wait_ge(gathered[j], 16 * (k + 1))
                wait(pe, copied, t - 3)
                pe.matmul(acc[j % 4][:, 0:total], sel[j][:, :], msg[j][:, :], start=True, stop=False)

            def carry(k, j):
                t = UE * k + j
                wait(pe, copied, t)
                pe.matmul(acc[j % 4][:, 0:total], goes_on[j][:, :], out[(j - 1) % UE][0:1, 0:total],
                          start=False, stop=True).then_inc(summed, 1)

            pipeline(pe, n_turns, UE, (2, gather_sums), (0, carry))


def max_edges(nc, C, name, table, maxima):
    with Stage(nc, name) as st:
        msg = [st.sb(f"msg{j}", [P, D]) for j in range(UE)]
        run = [st.sb(f"run{j}", [P, P]) for j in range(UE)]
        out = [st.sb(f"out{j}", [P, D]) for j in range(UE)]
        ids = [st.sb(f"ids{j}", [P, 1], I32) for j in range(UE)]
        turned_ps = [st.bank(f"turned{i}") for i in range(2)]
        back_ps = [st.bank(f"back{i}") for i in range(2)]
        biased, listed, turned, scanned, back, copied, issued, low = (
            st.sem(n) for n in ("biased", "listed", "turned_", "scanned", "back_", "copied", "issued", "low"))
        gathered = [st.sem(f"gathered{j}") for j in range(UE)]
        put = [st.sem(f"put{j}") for j in range(UE)]
        block = st.block()
        n_turns = NAT // UE
        bias = C.targets

        @block.sync
        def _(sp):
            sp.dma_start(bias[:, 0:NAT * P], C.bias_row[0:1, :].partition_broadcast(P)).then_inc(biased, 16)
            store_tiles(sp, n_turns, maxima, out, copied, put)

        @block.gpsimd
        def _(pool):
            for k, _ in turns(pool, n_turns):
                for j in range(UE):
                    t = UE * k + j
                    pool.wait_ge(listed, t + 1)
                    wait(pool, turned, t - UE + 1)
                    pool.sem_inc(issued, 1)
                    pool.indirect_dma_start(out=msg[j][:, :], out_offset=None, in_=table,
                                            in_offset=bass.IndirectOffsetOnAxis(ap=ids[j][:, 0:1], axis=0),
                                            bounds_check=NP - 1, oob_is_err=False).then_inc(gathered[j], 16)

        @block.vector
        def _(dve):
            dve.memset(run[UE - 1][:, :], -BIG).then_inc(low, 1)
            dve.wait_ge(low, 1)
            dve.wait_ge(biased, 16)

            def indices(k, j):
                wait(dve, gathered[j], 16 * k)
                dve.tensor_copy(ids[j][:, :], C.nat_lists[:, bass.ds(UE * k + j, 1), :].rearrange("p o c -> p (o c)")).then_inc(listed, 1)

            def scan(k, j):
                t = UE * k + j
                dve.wait_ge(turned, t + 1)
                wait(dve, scanned, t)
                wait(dve, back, t - UE + 1)
                dve.tensor_tensor_scan(run[j][:, :], bias[:, bass.ds(t * P, P)], turned_ps[j % 2][:, 0:P],
                                       run[(j - 1) % UE][:, P - 1:P], ALU.add, ALU.max).then_inc(scanned, 1)

            pipeline(dve, n_turns, UE, (7, indices), (0, scan))

        @block.tensor
        def _(pe):
            def turn(k, j):
                t = UE * k + j
                pe.wait_ge(gathered[j], 16 * (k + 1))
                wait(pe, scanned, t - 1)
                pe.transpose(turned_ps[j % 2][:, 0:P], msg[j][:, :], C.ident[:, :]).then_inc(turned, 1)

            def turn_back(k, j):
                t = UE * k + j
                pe.wait_ge(scanned, t + 1)
                wait(pe, copied, t - 1)
                pe.transpose(back_ps[j % 2][:, 0:D], run[j][:, :], C.ident[:, :]).then_inc(back, 1)

            pipeline(pe, n_turns, UE, (1, turn), (0, turn_back))

        @block.scalar
        def _(act):
            for k, _ in turns(act, n_turns):
                for j in range(UE):
                    act.wait_ge(back, UE * k + j + 1)
                    wait(act, put[j], 16 * k)
                    act.activation(out[j][:, :], back_ps[j % 2][:, 0:D], ACT.Copy).then_inc(copied, 1)


def attend_edges(nc, C, name, table, result):
    with Stage(nc, name) as st:
        msg = [st.sb(f"msg{j}", [P, GX]) for j in range(UE)]
        ald = [st.sb(f"ald{j}", [P, HEADS]) for j in range(UE)]
        sel = [st.sb(f"sel{j}", [P, P]) for j in range(UE)]
        low = [st.sb(f"low{j}", [P, P]) for j in range(UE)]
        logit = [st.sb(f"logit{j}", [P, HEADS]) for j in range(UE)]
        masked = [st.sb(f"masked{i}", [P, HEADS, P]) for i in range(2)]
        inner = [st.sb(f"inner{j}", [P, HEADS]) for j in range(UE)]
        wgt = [st.sb(f"wgt{j}", [P, HEADS]) for j in range(UE)]
        out = [st.sb(f"out{j}", [P, GT]) for j in range(UE)]
        ids = [st.sb(f"ids{j}", [P, 1], I32) for j in range(UE)]
        idd = [st.sb(f"idd{j}", [P, 1], I32) for j in range(UE)]
        spread_ps = [st.bank(f"spread{i}") for i in range(2)]
        prev_ps = [st.bank(f"prev{i}") for i in range(2)]
        acc = [st.bank(f"acc{i}") for i in range(2)]
        zeroed, listed, selected, lowered, issued = (st.sem(n) for n in ("zeroed", "listed", "selected", "lowered", "issued"))
        joined, rectified, logits, blend, spread, inner_done, shared, peak, placed, weight, weighed, carried, message, summed, copied = (
            st.sem(n) for n in ("joined", "rectified", "logits", "blend", "spread_", "inner_", "shared", "peak", "placed", "weight",
                                "weighed", "carried", "message", "summed", "copied"))
        gathered = [st.sem(f"gathered{j}") for j in range(UE)]
        put = [st.sem(f"put{j}") for j in range(UE)]
        block = st.block()
        n_turns = TILES // UE

        @block.gpsimd
        def _(pool):
            def gather(k, j):
                t = UE * k + j
                wait(pool, listed, t + 1)
                wait(pool, summed, t - UE + 1)
                pool.sem_inc(issued, 1)
                pool.indirect_dma_start(out=msg[j][:, :], out_offset=None, in_=table,
                                        in_offset=bass.IndirectOffsetOnAxis(ap=ids[j][:, 0:1], axis=0),
                                        bounds_check=NP - 1, oob_is_err=False).then_inc(gathered[j], 16)
                pool.indirect_dma_start(out=ald[j][:, :], out_offset=None, in_=table.rearrange("n (g h) -> (n g) h", h=HEADS),
                                        in_offset=bass.IndirectOffsetOnAxis(ap=idd[j][:, 0:1], axis=0),
                                        bounds_check=NP * (GX // HEADS) - 1, oob_is_err=False).then_inc(gathered[j], 16)

            pool.wait_ge(zeroed, 3 * UE)
            for k, _ in turns(pool, n_turns):
                for j in range(UE):
                    gather(k, j)

        @block.sync
        def _(sp):
            store_tiles(sp, n_turns, result, out, copied, put)

        @block.vector
        def _(dve):
            for j in range(UE):
                dve.memset(out[j][:, :], 0.0).then_inc(zeroed, 1)
                dve.memset(ald[j][:, :], 0.0).then_inc(zeroed, 1)
                dve.memset(msg[j][:, :], 0.0).then_inc(zeroed, 1)
            dve.wait_ge(zeroed, 3 * UE)

            def select(k, j):
                t = UE * k + j
                wait(dve, gathered[j], 32 * k)
                dve.tensor_copy(ids[j][:, :], C.lists[:, bass.ds(t, 1), 0:1].rearrange("p o c -> p (o c)"))
                dve.tensor_scalar(idd[j][:, :], C.lists[:, bass.ds(t, 1), 2:3].rearrange("p o c -> p (o c)"),
                                  0.0, float(GX // HEADS), ALU.max, ALU.mult).then_inc(listed, 1)
                wait(dve, summed, t - UE + 1)
                dve.tensor_scalar(sel[j][:, :], C.targets[:, bass.ds(t * P, P)],
                                  C.lists[:, bass.ds(t, 1), 2:3].rearrange("p o c -> p (o c)"), None, ALU.is_equal).then_inc(selected, 1)

            def add_logits(k, j):
                dve.wait_ge(gathered[j], 32 * (k + 1))
                dve.tensor_tensor(logit[j][:, :], msg[j][:, GT:GX], ald[j][:, :], ALU.add).then_inc(joined, 1)

            def mask(k, j):
                t = UE * k + j
                dve.wait_ge(logits, t + 1)
                dve.wait_ge(lowered, t + 1)
                wait(dve, spread, t - 1)
                dve.tensor_tensor(masked[j % 2][:, :, :],
                                  low[j][:, :].unsqueeze(1).to_broadcast([P, HEADS, P]),
                                  logit[j][:, :].unsqueeze(2).to_broadcast([P, HEADS, P]), ALU.add).then_inc(blend, 1)

            def reduce(k, j):
                t = UE * k + j
                dve.wait_ge(spread, t + 1)
                dve.tensor_reduce(inner[j][:, :], spread_ps[j % 2][:, :].rearrange("p (h e) -> p h e", h=HEADS),
                                  AX.X, ALU.max).then_inc(inner_done, 1)

            def fold(k, j):
                t = UE * k + j
                dve.wait_ge(shared, t + 1)
                wait(dve, put[j], 16 * k)
                dve.wait_ge(inner_done, t + 1)
                dve.scalar_tensor_tensor(out=out[j][:, GW:GT], in0=prev_ps[j % 2][:, 0:HEADS], scalar=low[j][:, PSEUDO:PSEUDO + 1],
                                         in1=inner[j][:, :], op0=ALU.add, op1=ALU.max).then_inc(peak, 1)
                dve.tensor_copy(logit[j][PSEUDO:PSEUDO + 1, :], prev_ps[j % 2][PSEUDO:PSEUDO + 1, 0:HEADS]).then_inc(placed, 1)

            def rectify(k, j):
                t = UE * k + j
                dve.wait_ge(joined, t + 1)
                dve.scalar_tensor_tensor(out=logit[j][:, :], in0=logit[j][:, :], scalar=0.2, in1=logit[j][:, :],
                                         op0=ALU.mult, op1=ALU.max).then_inc(rectified, 1)

            def silence(k, j):
                t = UE * k + j
                dve.wait_ge(rectified, t + 1)
                dve.memset(logit[j][PSEUDO:PSEUDO + 1, :], -BIG).then_inc(logits, 1)

            def subtract(k, j):
                t = UE * k + j
                dve.wait_ge(placed, t + 1)
                dve.tensor_tensor(wgt[j][:, :], logit[j][:, :], out[j][:, GW:GT], ALU.subtract).then_inc(weight, 1)

            def weigh(k, j):
                t = UE * k + j
                dve.wait_ge(weighed, t + 1)
                dve.wait_ge(carried, t + 1)
                dve.tensor_tensor(msg[j][:, HEADS:GT].rearrange("p (h f) -> p h f", h=HEADS),
                                  msg[j][:, HEADS:GT].rearrange("p (h f) -> p h f", h=HEADS),
                                  wgt[j][:, :].unsqueeze(2).to_broadcast([P, HEADS, HW]), ALU.mult).then_inc(message, 1)

            pipeline(dve, n_turns, UE, (4, add_logits), (6, select), (4, rectify), (2, reduce), (4, silence), (1, fold),
                     (4, mask), (1, subtract), (0, weigh))

        @block.scalar
        def _(act):
            act.wait_ge(zeroed, 3 * UE)

            def lower(k, j):
                t = UE * k + j
                wait(act, summed, t - UE + 1)
                act.wait_ge(selected, t + 1)
                act.activation(low[j][:, :], sel[j][:, :], ACT.Copy, bias=-BIG, scale=BIG).then_inc(lowered, 1)

            def exponent(k, j):
                act.wait_ge(weight, UE * k + j + 1)
                act.activation(wgt[j][:, :], wgt[j][:, :], ACT.Exp).then_inc(weighed, 1)

            def carry(k, j):
                t = UE * k + j
                act.wait_ge(gathered[j], 32 * (k + 1))
                wait(act, copied, t)
                act.activation(msg[j][PSEUDO:PSEUDO + 1, HEADS:GT], out[(j - 1) % UE][0:1, 0:GW], ACT.Copy).then_inc(carried, 1)

            def copy(k, j):
                t = UE * k + j
                act.wait_ge(summed, t + 1)
                wait(act, put[j], 16 * k)
                act.activation(out[j][:, 0:GW], acc[j % 2][:, 0:GW], ACT.Copy).then_inc(copied, 1)

            pipeline(act, n_turns, UE, (0, carry), (5, lower), (1, exponent), (0, copy))

        @block.tensor
        def _(pe):
            def turn(k, j):
                t = UE * k + j
                pe.wait_ge(blend, t + 1)
                wait(pe, inner_done, t - 1)
                for h in range(HEADS):
                    last = pe.transpose(spread_ps[j % 2][:, h * P:(h + 1) * P], masked[j % 2][:, h, :], C.ident[:, :])
                last.then_inc(spread, 1)

            def share(k, j):
                t = UE * k + j
                wait(pe, peak, t)
                wait(pe, placed, t - 1)
                pe.wait_ge(zeroed, 3 * UE)
                pe.matmul(prev_ps[j % 2][:, 0:HEADS], C.ones[0:1, :], out[(j - 1) % UE][0:1, GW:GT], start=True, stop=True).then_inc(shared, 1)

            def multiply(k, j):
                t = UE * k + j
                pe.wait_ge(message, t + 1)
                wait(pe, copied, t - 1)
                pe.matmul(acc[j % 2][:, 0:GW], sel[j][:, :], msg[j][:, HEADS:GT], start=True, stop=True).then_inc(summed, 1)

            pipeline(pe, n_turns, UE, (0, multiply), (2, share), (4, turn))




def load_rows(sp, buf, table, k, j, loaded, external):
    s = U * k + j
    width = buf.shape[-1]
    if external and isinstance(s, int) and s == STEPS - 1:
        src = table[s * STEP:N, 0:width].rearrange("(p j) d -> p j d", j=2)
        sp.dma_start(buf[0:LAST, :, :], src).then_inc(loaded[j], 16)
    else:
        sp.dma_start(buf[:, :, :], rows(table, s, width)).then_inc(loaded[j], 16)


def store_rows(sp, table, buf, k, j, stored, external=False):
    s = U * k + j
    width = buf.shape[-1]
    if external and isinstance(s, int) and s == STEPS - 1:
        dst = table[s * STEP:N, 0:width].rearrange("(p j) d -> p j d", j=2)
        sp.dma_start(dst, buf[0:LAST, :, :]).then_inc(stored[j], 16)
    else:
        sp.dma_start(rows(table, s, width), buf[:, :, :]).then_inc(stored[j], 16)


def sync_program(sp, n_in, loads, n_out, stores, loaded, used, stored, ready):
    def load(k, j):
        wait(sp, used, U * k + j - U + 1)
        loads(k, j)

    def store(k, j):
        if ready is not None:
            sp.wait_ge(ready, U * k + j + 1)
            stores(k, j)

    pipeline(sp, GROUPS, U, (U - 1, load), (0, store))
    for j in range(U):
        sp.wait_ge(stored[j], 16 * n_out * GROUPS)


class Fetch:

    def __init__(self, st, C, buf, table, column):
        self.C, self.buf, self.table, self.column = C, buf, table, column
        self.ids = [st.sb(f"ids{j}", [P, 2], I32) for j in range(U)]
        self.listed, self.issued = st.sem("listed"), st.sem("issued")
        self.fetched = [st.sem(f"fetched{j}") for j in range(U)]

    def number(self, dve, k, j):
        wait(dve, self.fetched[j], 32 * k)
        dve.tensor_copy(self.ids[j][:, :], self.C.place_f[:, bass.ds(U * k + j, 1), :, self.column:self.column + 1]
                        .rearrange("p o j c -> p (o j c)")).then_inc(self.listed, 1)

    def gather(self, pool, k, j, used):
        s = U * k + j
        pool.wait_ge(self.listed, s + 1)
        wait(pool, used, s - U + 1)
        pool.sem_inc(self.issued, 1)
        for i in range(2):
            pool.indirect_dma_start(out=self.buf[j][:, i, :], out_offset=None, in_=self.table,
                                    in_offset=bass.IndirectOffsetOnAxis(ap=self.ids[j][:, i:i + 1], axis=0),
                                    bounds_check=self.table.shape[0] - 1, oob_is_err=False).then_inc(self.fetched[j], 16)

    def ready(self, eng, k, j):
        eng.wait_ge(self.fetched[j], 32 * (k + 1))


class Norm:

    def __init__(self, st, name, slots=U):
        self.slots = slots
        self.stats = [st.sb(f"{name}_stats{j}", [P, 2, 6]) for j in range(self.slots)]
        self.mv = [st.sb(f"{name}_mv{j}", [P, 2, 2]) for j in range(self.slots)]
        self.rstd = [st.sb(f"{name}_rstd{j}", [P, 2]) for j in range(self.slots)]
        self.counted, self.carrier = st.sem(f"{name}_counted"), st.sem(f"{name}_carrier")
        self.varied, self.begun, self.raised, self.rooted, self.offsets = (
            st.sem(f"{name}_{n}") for n in ("varied", "begun", "raised", "rooted", "offsets"))

    def count(self, dve, x, j):
        for i in range(2):
            ins = dve.bn_stats(self.stats[j % self.slots][:, i, :], x[:, i, :])
        ins.then_inc(self.counted, 1)

    def aggregate(self, dve, s, j):
        dve.wait_ge(self.counted, s + 1)
        dve.sem_inc(self.carrier, 1)
        for i in range(2):
            ins = dve.bn_aggr(self.mv[j % self.slots][:, i, :], self.stats[j % self.slots][:, i, :])
        ins.then_inc(self.varied, 1)

    def power(self, pool, C, s, j):
        pool.wait_ge(self.varied, s + 1)
        pool.sem_inc(self.begun, 1)
        var, rstd = self.mv[j % self.slots][:, :, 1:2].rearrange("p j o -> p (j o)"), self.rstd[j % self.slots][:, :]
        pool.tensor_scalar(rstd, var, EPS, None, ALU.add).then_inc(self.raised, 1)
        pool.wait_ge(self.raised, s + 1)
        pool.tensor_tensor(rstd, rstd, C.minus_half[:, :], ALU.pow).then_inc(self.rooted, 1)

    def offset(self, dve, s, j):
        dve.wait_ge(self.rooted, s + 1)
        mean = self.mv[j % self.slots][:, :, 0:1].rearrange("p j o -> p (j o)")
        dve.scalar_tensor_tensor(out=mean, in0=mean, scalar=-1.0, in1=self.rstd[j % self.slots][:, :],
                                 op0=ALU.mult, op1=ALU.mult).then_inc(self.offsets, 1)

    def scale_act(self, act, out, x, s, j):
        act.wait_ge(self.offsets, s + 1)
        for i in range(2):
            ins = act.activation(out[:, i, :], x[:, i, :], ACT.Identity, bias=self.mv[j % self.slots][:, i, 0:1],
                                 scale=self.rstd[j % self.slots][:, i:i + 1])
        return ins

    def scale(self, dve, out, x, s, j):
        dve.wait_ge(self.rooted, s + 1)
        for i in range(2):
            ins = dve.tensor_scalar(out[:, i, :], x[:, i, :], self.mv[j % self.slots][:, i, 0:1], self.rstd[j % self.slots][:, i:i + 1],
                                    ALU.subtract, ALU.mult)
        return ins


class Tail:

    def __init__(self, st, C, out, written, a, project, p_out, external=False):
        self.C, self.out, self.written, self.a, self.project, self.p_out, self.external = C, out, written, a, project, p_out, external
        self.gat = project[0] == "gat"
        self.width = D + 8 if self.gat else D
        self.xa = [st.sb(f"xa{j}", [P, 2, D]) for j in range(U)]
        self.xT = [st.sb(f"tail_xT{i}", [P, 2, P]) for i in range(2)]
        self.po = [st.sb(f"po{i}", [P, 2, GX if self.gat else D]) for i in range(2)]
        self.t_ps, self.p_ps = st.bank("tail_t"), st.bank("tail_p")
        self.ln = Norm(st, "ln", U // 2)
        self.a_loaded = [st.sem(f"a_loaded{j}") for j in range(U)]
        self.p_stored = [st.sem(f"p_stored{i}") for i in range(2)]
        self.joined, self.fronted, self.turned, self.copied, self.multiplied, self.projected, self.ones_set = (
            st.sem(f"tail_{n}") for n in ("joined", "fronted", "turned", "copied", "multiplied", "projected", "ones_set"))

    def load(self, sp, k, j):
        wait(sp, self.joined, U * k + j - U + 1)
        load_rows(sp, self.xa[j], self.a, k, j, self.a_loaded, self.external)

    def free(self, eng, k, j):
        wait(eng, self.turned, U * k + j - U + 1)

    def prepare(self, dve):
        if self.gat:
            for i in range(2):
                dve.memset(self.po[i][:, :, :], 1.0).then_inc(self.ones_set, 1)

    def join(self, dve, k, j):
        dve.wait_ge(self.written, U * k + j + 1)
        dve.wait_ge(self.a_loaded[j], 16 * (k + 1))
        dve.tensor_tensor(self.out[j][:, :, :], self.out[j][:, :, :], self.xa[j][:, :, :], ALU.add).then_inc(self.joined, 1)

    def count(self, dve, k, j):
        dve.wait_ge(self.joined, U * k + j + 1)
        self.ln.count(dve, self.out[j], j)

    def aggregate(self, dve, k, j):
        self.ln.aggregate(dve, U * k + j, j)

    def scale(self, dve, k, j):
        self.ln.scale(dve, self.out[j], self.out[j], U * k + j, j).then_inc(self.fronted, 1)

    def power(self, pool, k, j):
        self.ln.power(pool, self.C, U * k + j, j)

    def turn(self, pe, k, j):
        s = U * k + j
        pe.wait_ge(self.fronted, s + 1)
        wait(pe, self.copied, s)
        for i in range(2):
            last = pe.transpose(self.t_ps[:, i * P:(i + 1) * P], self.out[j][:, i, :], self.C.ident[:, :])
        last.then_inc(self.turned, 1)

    def copy(self, act, k, j):
        s = U * k + j
        act.wait_ge(self.turned, s + 1)
        wait(act, self.multiplied, s - 1)
        act.activation(self.xT[j % 2][:, :, :], self.t_ps[:, 0:2 * P].rearrange("p (a b) -> p a b", a=2),
                       ACT.Copy).then_inc(self.copied, 1)

    def multiply(self, pe, k, j):
        s, C, width = U * k + j, self.C, self.width
        pe.wait_ge(self.copied, s + 1)
        wait(pe, self.projected, s)
        for i in range(2):
            g = self.p_ps[:, i * width:(i + 1) * width]
            if self.gat:
                last = pe.matmul(g, self.xT[j % 2][:, i, :], C.gat[:, self.project[1], :], start=True, stop=True)
            else:
                pe.matmul(g, C.ones3[:, :], C.bias[:, self.project[1]:self.project[1] + D], start=True, stop=False)
                last = pe.matmul(g, self.xT[j % 2][:, i, :], self.project[0], start=False, stop=True)
        last.then_inc(self.multiplied, 1)

    def put(self, act, k, j):
        s, po = U * k + j, self.po[j % 2]
        act.wait_ge(self.multiplied, s + 1)
        wait(act, self.p_stored[j % 2], 16 * (U // 2 * k + j // 2))
        v = self.p_ps[:, 0:2 * self.width].rearrange("p (a c) -> p a c", a=2)
        if self.gat:
            for i in range(2):
                act.activation(po[:, i, HEADS:GT].rearrange("p (h f) -> p h f", h=HEADS)[:, :, 0:FH],
                               v[:, i, 0:D].rearrange("p (h f) -> p h f", h=HEADS), ACT.Copy)
            act.activation(po[:, :, GT:GX], v[:, :, D:D + 4], ACT.Copy)
            act.activation(po[:, :, 0:HEADS], v[:, :, D + 4:D + 8], ACT.Copy).then_inc(self.projected, 1)
        else:
            act.activation(po[:, :, :], v, ACT.Copy).then_inc(self.projected, 1)

    def store(self, act, k, j):
        act.wait_ge(self.projected, U * k + j + 1)
        act.dma_start(rows(self.p_out, U * k + j, self.po[j % 2].shape[-1]), self.po[j % 2][:, :, :]).then_inc(self.p_stored[j % 2], 16)

    def finish(self, act):
        for i in range(2):
            act.wait_ge(self.p_stored[i], 16 * (U // 2) * GROUPS)

    def parts(self, eng, *leads):
        return [(lead, lambda k, j, part=part: part(eng, k, j)) for lead, part in leads]


def gru(nc, C, name, layer, h_in, sums, h_out, tail=None):
    with Stage(nc, name) as st:
        h = [st.sb(f"h{j}", [P, 2, D]) for j in range(U)]
        agg = [st.sb(f"agg{j}", [P, 2, D]) for j in range(U)]
        out = [st.sb(f"out{j}", [P, 2, D]) for j in range(U)]
        hT = [st.sb(f"hT{i}", [P, 4, P]) for i in range(2)]
        rz = [st.sb(f"rz{i}", [P, 2, 2 * D]) for i in range(2)]
        cand = [st.sb(f"cand{i}", [P, 2, D]) for i in range(2)]
        t_ps = [st.bank(f"t{i}") for i in range(2)]
        g_ps = [st.bank(f"g{i}", (P, 2, 512)) for i in range(2)]
        loaded = [st.sem(f"loaded{j}") for j in range(U)]
        stored = [st.sem(f"stored{j}") for j in range(U)]
        turned, copied, gates, squashed, before, cands, own, done = (
            st.sem(n) for n in ("turned", "copied", "gates", "squashed", "before", "cands", "own", "done"))
        fetch = Fetch(st, C, agg, sums, 1)
        tail = tail and Tail(st, C, out, done, **tail)
        block = st.block()

        @block.sync
        def _(sp):
            def loads(k, j):
                load_rows(sp, h[j], h_in, k, j, loaded, False)
                if tail:
                    tail.load(sp, k, j)

            sync_program(sp, 1, loads, 1, lambda k, j: store_rows(sp, h_out, out[j], k, j, stored),
                         loaded, done, stored, tail.fronted if tail else done)

        @block.tensor
        def _(pe):
            def turn(k, j):
                s = U * k + j
                pe.wait_ge(loaded[j], 16 * (k + 1))
                fetch.ready(pe, k, j)
                wait(pe, copied, s - 1)
                for i in range(2):
                    pe.transpose(t_ps[j % 2][:, i * P:(i + 1) * P], agg[j][:, i, :], C.ident[:, :])
                for i in range(2):
                    last = pe.transpose(t_ps[j % 2][:, (2 + i) * P:(3 + i) * P], h[j][:, i, :], C.ident[:, :])
                last.then_inc(turned, 1)

            def multiply(k, j):
                s = U * k + j
                pe.wait_ge(copied, s + 1)
                wait(pe, before, s - 1)
                for i in range(2):
                    g = g_ps[j % 2][:, i, :]
                    pe.matmul(g, C.ones3[:, :], C.bias[:, C.B_GRU:C.B_GRU + 4 * D], start=True, stop=False)
                    pe.matmul(g[:, 0:3 * D], hT[j % 2][:, i, :], C.wc[:, layer, :], start=False, stop=False)
                    last = pe.matmul(g[:, D:4 * D], hT[j % 2][:, 2 + i, :], C.whh[:, :], start=False, stop=True)
                last.then_inc(gates, 1)

            if tail:
                pipeline(pe, GROUPS, U, (8, turn), (7, multiply), *tail.parts(pe, (1, tail.turn), (0, tail.multiply)))
            else:
                pipeline(pe, GROUPS, U, (1, turn), (0, multiply))

        @block.scalar
        def _(act):
            def copy(k, j):
                s = U * k + j
                act.wait_ge(turned, s + 1)
                wait(act, gates, s - 1)
                act.activation(hT[j % 2][:, :, :], t_ps[j % 2][:, :].rearrange("p (a b) -> p a b", a=4), ACT.Copy).then_inc(copied, 1)

            def squash(k, j):
                s = U * k + j
                act.wait_ge(gates, s + 1)
                wait(act, done, s - 1)
                act.activation(rz[j % 2][:, :, :], g_ps[j % 2][:, :, D:3 * D], ACT.Sigmoid).then_inc(squashed, 1)
                act.wait_ge(before, s + 1)
                act.activation(cand[j % 2][:, :, :], cand[j % 2][:, :, :], ACT.Tanh).then_inc(cands, 1)

            if tail:
                if tail.gat:
                    act.wait_ge(tail.ones_set, 2)
                pipeline(act, GROUPS, U, (8, copy), (7, squash), *tail.parts(act, (1, tail.copy), (0, tail.put), (0, tail.store)))
                tail.finish(act)
            else:
                pipeline(act, GROUPS, U, (1, copy), (0, squash))

        @block.gpsimd
        def _(pool):
            if tail:
                pipeline(pool, GROUPS, U, (10, lambda k, j: fetch.gather(pool, k, j, turned)), *tail.parts(pool, (0, tail.power)))
            else:
                for k, _ in turns(pool, GROUPS):
                    for j in range(U):
                        fetch.gather(pool, k, j, turned)

        @block.vector
        def _(dve):
            link = Link(dve, own, 3)

            def number(k, j):
                fetch.number(dve, k, j)

            def update(k, j):
                s = U * k + j
                link.begin(s)
                c, r, z = cand[j % 2][:, :, :], rz[j % 2][:, :, 0:D], rz[j % 2][:, :, D:2 * D]
                dve.wait_ge(squashed, s + 1)
                link(dve.tensor_tensor(c, g_ps[j % 2][:, :, 3 * D:4 * D], r, ALU.mult))
                dve.tensor_tensor(c, g_ps[j % 2][:, :, 0:D], c, ALU.add).then_inc(before, 1)
                dve.wait_ge(cands, s + 1)
                wait(dve, stored[j], 16 * k)
                if tail:
                    tail.free(dve, k, j)
                link(dve.tensor_tensor(out[j][:, :, :], h[j][:, :, :], c, ALU.subtract))
                link(dve.tensor_tensor(out[j][:, :, :], out[j][:, :, :], z, ALU.mult))
                dve.tensor_tensor(out[j][:, :, :], out[j][:, :, :], c, ALU.add).then_inc(done, 1)

            if tail:
                tail.prepare(dve)
                t_join, t_count, t_aggregate, t_scale = tail.parts(dve, (3, tail.join), (2, tail.count), (2, tail.aggregate), (0, tail.scale))
                pipeline(dve, GROUPS, U, (13, number), (4, update), t_count, t_join, t_aggregate, t_scale)
            else:
                pipeline(dve, GROUPS, U, (10, number), (0, update))


def transform(nc, C, name, front, a, b=None, bn=None, x_out=None, project=None, p_out=None, external=False):
    gat = project is not None and project[0] == "gat"
    with Stage(nc, name) as st:
        has_b = b is not None
        xa = [st.sb(f"xa{j}", [P, 2, D]) for j in range(U)]
        xb = [st.sb(f"xb{j}", [P, 2, D]) for j in range(U)] if has_b else None
        x = [st.sb(f"x{j}", [P, 2, D]) for j in range(U)]
        ex = [st.sb(f"ex{j}", [P, 2, D]) for j in range(U)] if bn is not None else None
        width = D + 8 if gat else D
        if project is not None:
            xT = [st.sb(f"xT{i}", [P, 2, P]) for i in range(2)]
            t_ps = [st.bank(f"t{i}") for i in range(2)]
            p_ps = [st.bank(f"p{i}") for i in range(2)]
            po = [st.sb(f"po{j}", [P, 2, GX if gat else D]) for j in range(U)]
        ln = Norm(st, "ln") if front in ("ln", "bn_ln") else None
        loaded = [st.sem(f"loaded{j}") for j in range(U)]
        stored = [st.sem(f"stored{j}") for j in range(U)]
        joined, scaled, shifted, lifted, fronted, turned, copied, multiplied, projected, low, exps, ones_set = (
            st.sem(n) for n in ("joined", "scaled", "shifted", "lifted", "fronted", "turned", "copied", "multiplied", "projected",
                                "low", "exps", "ones_set"))
        n_in = 1 + has_b
        n_out = (x_out is not None) + (project is not None)
        block = st.block()

        @block.sync
        def _(sp):
            def loads(k, j):
                load_rows(sp, xa[j], a, k, j, loaded, external)
                if has_b:
                    load_rows(sp, xb[j], b, k, j, loaded, False)

            def stores(k, j):
                if x_out is not None:
                    store_rows(sp, x_out, x[j], k, j, stored)

            used = {"copy": turned, "bn": scaled}.get(front, joined)
            sync_program(sp, n_in, loads, n_out, stores, loaded, used, stored, fronted if x_out is not None else None)

        def put(eng, copy, k, j):
            s = U * k + j
            eng.wait_ge(multiplied, s + 1)
            wait(eng, stored[j], 16 * n_out * k)
            v = p_ps[j % 2][:, 0:2 * width].rearrange("p (a c) -> p a c", a=2)
            if gat:
                for i in range(2):
                    copy(po[j][:, i, HEADS:GT].rearrange("p (h f) -> p h f", h=HEADS)[:, :, 0:FH],
                         v[:, i, 0:D].rearrange("p (h f) -> p h f", h=HEADS))
                copy(po[j][:, :, GT:GX], v[:, :, D:D + 4])
                copy(po[j][:, :, 0:HEADS], v[:, :, D + 4:D + 8]).then_inc(projected, 1)
            else:
                copy(po[j][:, :, :], v).then_inc(projected, 1)

        put_on_act = project is not None and front == "ln"

        @block.vector
        def _(dve):
            if gat:
                for j in range(U):
                    dve.memset(po[j][:, :, :], 1.0).then_inc(ones_set, 1)
                dve.wait_ge(ones_set, U)

            def take(k, j):
                dve.wait_ge(loaded[j], 16 * n_in * (k + 1))
                wait(dve, stored[j], 16 * n_out * k)

            def join(k, j):
                take(k, j)
                dve.tensor_tensor(x[j][:, :, :], xa[j][:, :, :], xb[j][:, :, :], ALU.add).then_inc(joined, 1)

            def multiply(k, j):
                take(k, j)
                dve.tensor_tensor(x[j][:, :, :], xa[j][:, :, :], bn[0][:, :].unsqueeze(1).to_broadcast([P, 2, D]), ALU.mult).then_inc(scaled, 1)

            def shift(k, j):
                dve.wait_ge(scaled, U * k + j + 1)
                dve.tensor_tensor(x[j][:, :, :], x[j][:, :, :], bn[1][:, :].unsqueeze(1).to_broadcast([P, 2, D]), ALU.add).then_inc(shifted, 1)

            def elu(k, j):
                dve.wait_ge(exps, U * k + j + 1)
                dve.scalar_tensor_tensor(out=x[j][:, :, :], in0=ex[j][:, :, :], scalar=-1.0, in1=x[j][:, :, :],
                                         op0=ALU.add, op1=ALU.max).then_inc(fronted if front == "bn" else lifted, 1)

            def join_elu(k, j):
                dve.wait_ge(lifted, U * k + j + 1)
                dve.tensor_tensor(x[j][:, :, :], x[j][:, :, :], xb[j][:, :, :], ALU.add).then_inc(joined, 1)

            def count(k, j):
                dve.wait_ge(joined, U * k + j + 1)
                ln.count(dve, x[j], j)

            def aggregate(k, j):
                ln.aggregate(dve, U * k + j, j)

            def offset(k, j):
                ln.offset(dve, U * k + j, j)

            def scale(k, j):
                ln.scale(dve, x[j], x[j], U * k + j, j).then_inc(fronted, 1)

            def put_(k, j):
                put(dve, dve.tensor_copy, k, j)

            if front == "copy":
                parts = [(0, put_)]
            elif front == "ln":
                parts = [(4, join), (3, count), (2, aggregate), (0, scale)]
            elif front == "bn":
                parts = [(5, multiply), (4, shift), (2, elu), (0, put_)]
            else:
                parts = [(3, elu), (6, multiply), (2, count), (3, join_elu), (6, shift), (2, aggregate), (0, offset)]
            pipeline(dve, GROUPS, U, *parts)

        if ln is not None:
            @block.gpsimd
            def _(pool):
                for k, _ in turns(pool, GROUPS):
                    for j in range(U):
                        ln.power(pool, C, U * k + j, j)

        if project is not None:
            @block.tensor
            def _(pe):
                if gat:
                    w = C.gat[:, project[1], :]
                else:
                    w = project[0]

                def turn(k, j):
                    s = U * k + j
                    src = xa[j] if front == "copy" else x[j]
                    if front == "copy":
                        pe.wait_ge(loaded[j], 16 * (k + 1))
                    else:
                        pe.wait_ge(fronted, s + 1)
                    wait(pe, copied, s - 1)
                    for i in range(2):
                        last = pe.transpose(t_ps[j % 2][:, i * P:(i + 1) * P], src[:, i, :], C.ident[:, :])
                    last.then_inc(turned, 1)

                def multiply(k, j):
                    s = U * k + j
                    pe.wait_ge(copied, s + 1)
                    wait(pe, projected, s - 1)
                    for i in range(2):
                        g = p_ps[j % 2][:, i * width:(i + 1) * width]
                        if not gat:
                            pe.matmul(g, C.ones3[:, :], C.bias[:, project[1]:project[1] + D], start=True, stop=False)
                        last = pe.matmul(g, xT[j % 2][:, i, :], w, start=gat, stop=True)
                    last.then_inc(multiplied, 1)

                pipeline(pe, GROUPS, U, (1, turn), (0, multiply))

        if project is not None or bn is not None:
            @block.scalar
            def _(act):
                def lower(k, j):
                    act.wait_ge(shifted, U * k + j + 1)
                    wait(act, lifted if front == "bn_ln" else fronted, U * k + j - U + 1)
                    act.activation(ex[j][:, :, :], x[j][:, :, :], ACT.Relu, scale=-1.0).then_inc(low, 1)

                def lift(k, j):
                    act.wait_ge(low, U * k + j + 1)
                    act.activation(ex[j][:, :, :], ex[j][:, :, :], ACT.Exp, scale=-1.0).then_inc(exps, 1)

                def copy(k, j):
                    s = U * k + j
                    act.wait_ge(turned, s + 1)
                    wait(act, multiplied, s - 1)
                    act.activation(xT[j % 2][:, :, :], t_ps[j % 2][:, 0:2 * P].rearrange("p (a b) -> p a b", a=2), ACT.Copy).then_inc(copied, 1)

                def put_(k, j):
                    put(act, lambda out, in_: act.activation(out, in_, ACT.Copy), k, j)

                def scale(k, j):
                    ln.scale_act(act, x[j], x[j], U * k + j, j).then_inc(fronted, 1)

                def store(k, j):
                    act.wait_ge(projected, U * k + j + 1)
                    store_rows(act, p_out, po[j], k, j, stored)

                parts = []
                if bn is not None:
                    parts += [(4, lower), (3, lift)]
                if project is not None:
                    parts += [(2, copy)]
                if put_on_act:
                    parts += [(1, put_)]
                if project is not None:
                    parts += [(0, store)]
                elif front == "bn_ln":
                    parts = [(6, lower), (5, lift), (0, scale)]
                if gat:
                    act.wait_ge(ones_set, U)
                pipeline(act, GROUPS, U, *parts)


def merge_attention(nc, C, name, sums, table, out_table, gb, bn):
    with Stage(nc, name) as st:
        sm = [st.sb(f"sm{j}", [P, 2, GT]) for j in range(U)]
        tb = [st.sb(f"tb{j}", [P, 2, GX]) for j in range(U)]
        lg = [st.sb(f"lg{j}", [P, 2, HEADS]) for j in range(U)]
        mx = [st.sb(f"mx{j}", [P, 2, HEADS]) for j in range(U)]
        df = [st.sb(f"df{j}", [P, 2, 2, HEADS]) for j in range(U)]
        rc = [st.sb(f"rc{j}", [P, 2, HEADS]) for j in range(U)]
        sq = [st.sb(f"sq{j}", [P, 2, D]) for j in range(2)]
        out = [st.sb(f"out{j}", [P, 2, D]) for j in range(U)]
        st1 = st.sb("st1", [P, 8, D])
        acc, acc2 = st.bank("acc"), st.bank("acc2")
        loaded = [st.sem(f"loaded{j}") for j in range(U)]
        stored = [st.sem(f"stored{j}") for j in range(U)]
        summed, leaked, highest, apart, factors, weighed, merged, inverted, done, squared, counted, own2, varied, rooted = (
            st.sem(n) for n in ("summed", "leaked", "highest", "apart", "factors", "weighed", "merged", "inverted", "done",
                                "squared", "counted", "own2", "varied", "rooted"))
        fetch = Fetch(st, C, sm, sums, 1)
        block = st.block()

        @block.sync
        def _(sp):
            def loads(k, j):
                load_rows(sp, tb[j], table, k, j, loaded, False)

            sync_program(sp, 1, loads, 1, lambda k, j: store_rows(sp, out_table, out[j], k, j, stored),
                         loaded, merged, stored, done)

        @block.vector
        def _(dve):
            def heads(v):
                first = HEADS if v.shape[-1] == GX else 0
                return v[:, :, first:first + GW].rearrange("p j (h f) -> p j h f", h=HEADS)

            def number(k, j):
                fetch.number(dve, k, j)

            def add(k, j):
                dve.wait_ge(loaded[j], 16 * (k + 1))
                dve.tensor_tensor(lg[j][:, :, :], tb[j][:, :, GT:GX], tb[j][:, :, 0:HEADS], ALU.add).then_inc(summed, 1)

            def leak(k, j):
                dve.wait_ge(summed, U * k + j + 1)
                dve.scalar_tensor_tensor(out=lg[j][:, :, :], in0=lg[j][:, :, :], scalar=0.2, in1=lg[j][:, :, :],
                                         op0=ALU.mult, op1=ALU.max).then_inc(leaked, 1)

            def top(k, j):
                dve.wait_ge(leaked, U * k + j + 1)
                fetch.ready(dve, k, j)
                dve.tensor_tensor(mx[j][:, :, :], lg[j][:, :, :], sm[j][:, :, GW:GT], ALU.max).then_inc(highest, 1)

            def subtract(k, j):
                dve.wait_ge(highest, U * k + j + 1)
                dve.tensor_tensor(df[j][:, 0, :, :], sm[j][:, :, GW:GT], mx[j][:, :, :], ALU.subtract)
                dve.tensor_tensor(df[j][:, 1, :, :], lg[j][:, :, :], mx[j][:, :, :], ALU.subtract).then_inc(apart, 1)

            def weigh(k, j):
                dve.wait_ge(factors, U * k + j + 1)
                for i, v in enumerate((sm[j], tb[j])):
                    ins = dve.tensor_tensor(heads(v), heads(v), df[j][:, i, :, :].unsqueeze(3).to_broadcast([P, 2, HEADS, HW]), ALU.mult)
                ins.then_inc(weighed, 1)

            def merge(k, j):
                dve.wait_ge(weighed, U * k + j + 1)
                dve.tensor_tensor(heads(sm[j]), heads(sm[j]), heads(tb[j]), ALU.add).then_inc(merged, 1)

            def invert(k, j):
                dve.wait_ge(merged, U * k + j + 1)
                dve.reciprocal(rc[j][:, :, :].unsqueeze(3), heads(sm[j])[:, :, :, FH:HW]).then_inc(inverted, 1)

            def divide(k, j):
                s = U * k + j
                dve.wait_ge(inverted, s + 1)
                wait(dve, stored[j], 16 * k)
                wait(dve, counted, s - U + 1)
                dve.tensor_tensor(out[j][:, :, :].rearrange("p j (h f) -> p j h f", h=HEADS), heads(sm[j])[:, :, :, 0:FH],
                                  rc[j][:, :, :].unsqueeze(3).to_broadcast([P, 2, HEADS, FH]), ALU.mult).then_inc(done, 1)

            pipeline(dve, GROUPS, U, (13, number), (9, add), (8, leak), (7, top), (6, subtract), (3, weigh), (2, merge), (1, invert), (0, divide))
            dve.wait_ge(counted, STEPS)
            g, be, bb = (C.bc[:, i, :] for i in gb)
            w = lambda i: st1[:, i, :]
            fin = Link(dve, own2, 8)
            fin.begin(0)
            fin(dve.tensor_copy(st1[:, 0:4, :], acc[:, :].rearrange("p (a d) -> p a d", a=4)))
            fin(dve.tensor_tensor(st1[:, 4:5, :], st1[:, 0:1, :], st1[:, 1:2, :], ALU.add))
            fin(dve.tensor_tensor(st1[:, 5:6, :], st1[:, 2:3, :], st1[:, 3:4, :], ALU.add))
            fin(dve.tensor_scalar(st1[:, 4:6, :], st1[:, 4:6, :], 1.0 / N, None, ALU.mult))
            fin(dve.tensor_tensor(w(0), w(4), w(4), ALU.mult))
            fin(dve.tensor_tensor(w(0), w(5), w(0), ALU.subtract))
            dve.tensor_scalar(w(0), w(0), EPS, None, ALU.add).then_inc(varied, 1)
            dve.memset(w(1), -0.5).then_inc(varied, 1)
            dve.wait_ge(rooted, 1)
            sc, sh = bn
            fin(dve.tensor_tensor(sc[:, :], w(2), g, ALU.mult))
            fin(dve.tensor_tensor(w(4), w(4), bb, ALU.add))
            dve.tensor_tensor(w(6), bb, w(4), ALU.subtract).then_inc(varied, 1)
            dve.wait_ge(varied, 3)
            dve.tensor_tensor(w(6), w(6), sc[:, :], ALU.mult).then_inc(varied, 1)
            dve.wait_ge(varied, 4)
            dve.tensor_tensor(sh[:, :], w(6), be, ALU.add).then_inc(varied, 1)

        @block.gpsimd
        def _(pool):
            for k, _ in turns(pool, GROUPS):
                for j in range(U):
                    fetch.gather(pool, k, j, done)
            pool.wait_ge(varied, 2)
            pool.tensor_tensor(st1[:, 2, :], st1[:, 0, :], st1[:, 1, :], ALU.pow).then_inc(rooted, 1)

        @block.scalar
        def _(act):
            def exponent(k, j):
                act.wait_ge(apart, U * k + j + 1)
                act.activation(df[j][:, :, :, :], df[j][:, :, :, :], ACT.Exp).then_inc(factors, 1)

            def square(k, j):
                s = U * k + j
                act.wait_ge(done, s + 1)
                wait(act, counted, s - 1)
                act.activation(sq[j % 2][:, :, :], out[j][:, :, :], ACT.Square).then_inc(squared, 1)

            pipeline(act, GROUPS, U, (5, exponent), (0, square))

        @block.tensor
        def _(pe):
            for k, last in turns(pe, GROUPS):
                for j in range(U):
                    s = U * k + j
                    pe.wait_ge(squared, s + 1)
                    end = last and j == U - 1
                    n = LAST if end else P
                    start = isinstance(k, int) and k == 0 and j == 0
                    pe.matmul(acc[:, 0:2 * D], C.ones[0:n, :], out[j][0:n, :, :].rearrange("p j d -> p (j d)"),
                              start=start, stop=False, skip_group_check=True)
                    pe.matmul(acc[:, 2 * D:4 * D], C.ones[0:n, :], sq[j % 2][0:n, :, :].rearrange("p j d -> p (j d)"),
                              start=False, stop=end, skip_group_check=True).then_inc(counted, 1)


def convolve(nc, C, name, layer, x_in, sums, edge_sums, y_out, tail=None):
    with Stage(nc, name) as st:
        x = [st.sb(f"x{j}", [P, 2, D]) for j in range(U)]
        agg = [st.sb(f"agg{j}", [P, 2, D]) for j in range(U)]
        ea = [st.sb(f"ea{j}", [P, 2, ED + 1]) for j in range(U)]
        inv = [st.sb(f"inv{j}", [P, 2]) for j in range(U)]
        out = [st.sb(f"out{j}", [P, 2, D]) for j in range(U)]
        xT = [st.sb(f"xT{i}", [P, 4, P]) for i in range(2)]
        eT = [st.sb(f"eT{i}", [ED + 1, 2, P]) for i in range(2)]
        t_ps = [st.bank(f"t{i}") for i in range(2)]
        e_ps = [st.bank(f"e{i}") for i in range(2)]
        p_ps = [st.bank(f"p{i}") for i in range(2)]
        loaded = [st.sem(f"loaded{j}") for j in range(U)]
        stored = [st.sem(f"stored{j}") for j in range(U)]
        counted, inverted, scaled, turned, copied, e_copied, multiplied, done = (
            st.sem(n) for n in ("counted", "inverted", "scaled", "turned", "copied", "e_copied", "multiplied", "done"))
        fetch = Fetch(st, C, agg, sums, 1)
        tail = tail and Tail(st, C, out, done, **tail)
        block = st.block()

        @block.sync
        def _(sp):
            def loads(k, j):
                load_rows(sp, x[j], x_in, k, j, loaded, False)
                load_rows(sp, ea[j], edge_sums, k, j, loaded, False)
                if tail:
                    tail.load(sp, k, j)

            sync_program(sp, 2, loads, 1, lambda k, j: store_rows(sp, y_out, out[j], k, j, stored),
                         loaded, done, stored, tail.fronted if tail else done)

        @block.gpsimd
        def _(pool):
            if tail:
                pipeline(pool, GROUPS, U, (11, lambda k, j: fetch.gather(pool, k, j, turned)), *tail.parts(pool, (0, tail.power)))
            else:
                for k, _ in turns(pool, GROUPS):
                    for j in range(U):
                        fetch.gather(pool, k, j, turned)

        @block.vector
        def _(dve):
            def number(k, j):
                fetch.number(dve, k, j)

            def count(k, j):
                dve.wait_ge(loaded[j], 32 * (k + 1))
                dve.tensor_scalar(inv[j][:, :].unsqueeze(2), ea[j][:, :, ED:ED + 1], 1.0, None, ALU.max).then_inc(counted, 1)

            def invert(k, j):
                dve.wait_ge(counted, U * k + j + 1)
                dve.reciprocal(inv[j][:, :], inv[j][:, :]).then_inc(inverted, 1)

            def scale(k, j):
                dve.wait_ge(inverted, U * k + j + 1)
                fetch.ready(dve, k, j)
                dve.tensor_tensor(agg[j][:, :, :], agg[j][:, :, :], inv[j][:, :].unsqueeze(2).to_broadcast([P, 2, D]), ALU.mult)
                dve.tensor_tensor(ea[j][:, :, :], ea[j][:, :, :], inv[j][:, :].unsqueeze(2).to_broadcast([P, 2, ED + 1]),
                                  ALU.mult).then_inc(scaled, 1)

            def copy_e(k, j):
                s = U * k + j
                dve.wait_ge(turned, s + 1)
                wait(dve, multiplied, s - 1)
                dve.tensor_copy(eT[j % 2][:, :, :], e_ps[j % 2][0:ED + 1, 0:2 * P].rearrange("p (a b) -> p a b", a=2)).then_inc(e_copied, 1)

            if tail:
                tail.prepare(dve)
                t_join, t_count, t_aggregate, t_scale = tail.parts(dve, (3, tail.join), (2, tail.count), (2, tail.aggregate), (0, tail.scale))
                pipeline(dve, GROUPS, U, (13, number), (10, count), (9, invert), (8, scale), (5, copy_e), t_count, t_join, t_aggregate, t_scale)
            else:
                pipeline(dve, GROUPS, U, (11, number), (5, count), (4, invert), (3, scale), (0, copy_e))

        @block.tensor
        def _(pe):
            def turn(k, j):
                s = U * k + j
                pe.wait_ge(scaled, s + 1)
                wait(pe, copied, s - 1)
                wait(pe, e_copied, s - 1)
                for i in range(2):
                    pe.transpose(t_ps[j % 2][:, i * P:(i + 1) * P], agg[j][:, i, :], C.ident[:, :])
                    pe.transpose(t_ps[j % 2][:, (2 + i) * P:(3 + i) * P], x[j][:, i, :], C.ident[:, :])
                    last = pe.transpose(e_ps[j % 2][0:ED + 1, i * P:(i + 1) * P], ea[j][:, i, :], C.ident[:, :])
                last.then_inc(turned, 1)

            def multiply(k, j):
                s = U * k + j
                pe.wait_ge(copied, s + 1)
                pe.wait_ge(e_copied, s + 1)
                wait(pe, done, s - 1)
                for i in range(2):
                    g = p_ps[j % 2][:, i * D:(i + 1) * D]
                    pe.matmul(g, C.ones3[:, :], C.bias[:, C.B_L + layer * D:C.B_L + (layer + 1) * D], start=True, stop=False)
                    pe.matmul(g, xT[j % 2][:, i, :], C.wl[:, layer, :], start=False, stop=False)
                    pe.matmul(g, eT[j % 2][:, i, :], C.wel[:, layer, :], start=False, stop=False)
                    last = pe.matmul(g, xT[j % 2][:, 2 + i, :], C.wr[:, layer, :], start=False, stop=True)
                last.then_inc(multiplied, 1)

            if tail:
                pipeline(pe, GROUPS, U, (8, turn), (7, multiply), *tail.parts(pe, (1, tail.turn), (0, tail.multiply)))
            else:
                pipeline(pe, GROUPS, U, (1, turn), (0, multiply))

        @block.scalar
        def _(act):
            def copy(k, j):
                s = U * k + j
                act.wait_ge(turned, s + 1)
                wait(act, multiplied, s - 1)
                act.activation(xT[j % 2][:, :, :], t_ps[j % 2][:, :].rearrange("p (a b) -> p a b", a=4), ACT.Copy).then_inc(copied, 1)

            def rectify(k, j):
                s = U * k + j
                act.wait_ge(multiplied, s + 1)
                wait(act, stored[j], 16 * k)
                if tail:
                    tail.free(act, k, j)
                act.activation(out[j][:, :, :], p_ps[j % 2][:, 0:2 * D].rearrange("p (a b) -> p a b", a=2), ACT.Relu).then_inc(done, 1)

            if tail:
                pipeline(act, GROUPS, U, (8, copy), (7, rectify), *tail.parts(act, (1, tail.copy), (0, tail.put), (0, tail.store)))
                tail.finish(act)
            else:
                pipeline(act, GROUPS, U, (1, copy), (0, rectify))


def update(nc, C, name, x_in, h_in, maxima, edge_sums, x_out):
    with Stage(nc, name) as st:
        x = [st.sb(f"x{j}", [P, 2, D]) for j in range(U)]
        h = [st.sb(f"h{j}", [P, 2, D]) for j in range(U)]
        mx = [st.sb(f"mx{j}", [P, 2, D]) for j in range(U)]
        ea = [st.sb(f"ea{j}", [P, 2, ED + 1]) for j in range(U)]
        has = [st.sb(f"has{j}", [P, 2]) for j in range(U)]
        out = [st.sb(f"out{j}", [P, 2, D]) for j in range(U)]
        xT = [st.sb(f"xT{i}", [P, 4, P]) for i in range(2)]
        t_ps = [st.bank(f"t{i}") for i in range(2)]
        p_ps = [st.bank(f"p{i}") for i in range(2)]
        ln = Norm(st, "ln")
        loaded = [st.sem(f"loaded{j}") for j in range(U)]
        stored = [st.sem(f"stored{j}") for j in range(U)]
        known, parted, turned, copied, multiplied, added, normed, gained, done = (
            st.sem(n) for n in ("known", "parted", "turned", "copied", "multiplied", "added", "normed", "gained", "done"))
        fetch = Fetch(st, C, mx, maxima, 0)
        block = st.block()

        @block.sync
        def _(sp):
            def loads(k, j):
                load_rows(sp, x[j], x_in, k, j, loaded, False)
                load_rows(sp, h[j], h_in, k, j, loaded, False)
                load_rows(sp, ea[j], edge_sums, k, j, loaded, False)

            sync_program(sp, 3, loads, 1, lambda k, j: store_rows(sp, x_out, out[j], k, j, stored),
                         loaded, added, stored, done)

        @block.vector
        def _(dve):
            def number(k, j):
                fetch.number(dve, k, j)

            def subtract(k, j):
                dve.wait_ge(loaded[j], 48 * (k + 1))
                fetch.ready(dve, k, j)
                dve.tensor_scalar(has[j][:, :].unsqueeze(2), ea[j][:, :, ED:ED + 1], 1.0, None, ALU.min)
                dve.tensor_tensor(mx[j][:, :, :], mx[j][:, :, :], h[j][:, :, :], ALU.subtract).then_inc(known, 1)

            def part(k, j):
                dve.wait_ge(known, U * k + j + 1)
                dve.tensor_tensor(mx[j][:, :, :], mx[j][:, :, :], has[j][:, :].unsqueeze(2).to_broadcast([P, 2, D]),
                                  ALU.mult).then_inc(parted, 1)

            def add(k, j):
                s = U * k + j
                dve.wait_ge(multiplied, s + 1)
                wait(dve, stored[j], 16 * k)
                dve.tensor_tensor(out[j][:, :, :], p_ps[j % 2][:, 0:2 * D].rearrange("p (a b) -> p a b", a=2), x[j][:, :, :],
                                  ALU.add).then_inc(added, 1)

            def count(k, j):
                dve.wait_ge(added, U * k + j + 1)
                ln.count(dve, out[j], j)

            def aggregate(k, j):
                ln.aggregate(dve, U * k + j, j)

            def offset(k, j):
                ln.offset(dve, U * k + j, j)

            def gain(k, j):
                dve.wait_ge(normed, U * k + j + 1)
                dve.tensor_tensor(out[j][:, :, :], out[j][:, :, :], C.bcast("ln1_g"), ALU.mult).then_inc(gained, 1)

            def shift(k, j):
                dve.wait_ge(gained, U * k + j + 1)
                dve.tensor_tensor(out[j][:, :, :], out[j][:, :, :], C.bcast("ln1_b"), ALU.add).then_inc(done, 1)

            pipeline(dve, GROUPS, U, (13, number), (4, add), (2, offset), (7, part), (4, count), (0, gain), (8, subtract),
                     (4, aggregate), (0, shift))

        @block.gpsimd
        def _(pool):
            pipeline(pool, GROUPS, U, (8, lambda k, j: fetch.gather(pool, k, j, turned)),
                     (0, lambda k, j: ln.power(pool, C, U * k + j, j)))

        @block.tensor
        def _(pe):
            def turn(k, j):
                s = U * k + j
                pe.wait_ge(parted, s + 1)
                wait(pe, copied, s - 1)
                for i in range(2):
                    pe.transpose(t_ps[j % 2][:, i * P:(i + 1) * P], h[j][:, i, :], C.ident[:, :])
                    last = pe.transpose(t_ps[j % 2][:, (2 + i) * P:(3 + i) * P], mx[j][:, i, :], C.ident[:, :])
                last.then_inc(turned, 1)

            def multiply(k, j):
                s = U * k + j
                pe.wait_ge(copied, s + 1)
                wait(pe, added, s - 1)
                for i in range(2):
                    g = p_ps[j % 2][:, i * D:(i + 1) * D]
                    pe.matmul(g, C.ones3[:, :], C.bias[:, C.B_F:C.B_F + D], start=True, stop=False)
                    pe.matmul(g, xT[j % 2][:, i, :], C.wf[:, 0, :], start=False, stop=False)
                    last = pe.matmul(g, xT[j % 2][:, 2 + i, :], C.wf[:, 1, :], start=False, stop=True)
                last.then_inc(multiplied, 1)

            pipeline(pe, GROUPS, U, (1, turn), (0, multiply))

        @block.scalar
        def _(act):
            def copy(k, j):
                s = U * k + j
                act.wait_ge(turned, s + 1)
                wait(act, multiplied, s - 1)
                act.activation(xT[j % 2][:, :, :], t_ps[j % 2][:, :].rearrange("p (a b) -> p a b", a=4), ACT.Copy).then_inc(copied, 1)

            def scale(k, j):
                ln.scale_act(act, out[j], out[j], U * k + j, j).then_inc(normed, 1)

            pipeline(act, GROUPS, U, (5, copy), (0, scale))


def feed_forward(nc, C, name, x4_in, x3_in, y_out):
    HB = FFN // P
    with Stage(nc, name) as st:
        x4 = [st.sb(f"x4{j}", [P, 2, D]) for j in range(U)]
        x3 = [st.sb(f"x3{j}", [P, 2, D]) for j in range(U)]
        out = [st.sb(f"out{j}", [P, 2, D]) for j in range(U)]
        xT = [st.sb(f"xT{i}", [P, 2 * P]) for i in range(2)]
        hid = [st.sb(f"hid{i}", [P, HB, 2 * P]) for i in range(2)]
        t_ps = [st.bank(f"t{i}") for i in range(2)]
        h_ps = [st.bank(f"h{i}") for i in range(HB)]
        p_ps = [st.bank(f"p{i}") for i in range(2)]
        ln2, ln = Norm(st, "lnb"), Norm(st, "ln")
        loaded = [st.sem(f"loaded{j}") for j in range(U)]
        stored = [st.sem(f"stored{j}") for j in range(U)]
        turned, copied, hidden, active, multiplied, added, normed, gained, shifted, joined, done = (
            st.sem(n) for n in ("turned", "copied", "hidden", "active", "multiplied", "added", "normed", "gained", "shifted",
                                "joined", "done"))
        block = st.block()

        @block.sync
        def _(sp):
            def loads(k, j):
                load_rows(sp, x4[j], x4_in, k, j, loaded, False)
                wait(sp, joined, U * k + j - U + 1)
                load_rows(sp, x3[j], x3_in, k, j, loaded, False)

            sync_program(sp, 2, loads, 1, lambda k, j: store_rows(sp, y_out, out[j], k, j, stored, external=True),
                         loaded, added, stored, done)

        @block.tensor
        def _(pe):
            def turn(k, j):
                s = U * k + j
                pe.wait_ge(loaded[j], 32 * (k + 1))
                wait(pe, copied, s - 1)
                for i in range(2):
                    last = pe.transpose(t_ps[j % 2][:, i * P:(i + 1) * P], x4[j][:, i, :], C.ident[:, :])
                last.then_inc(turned, 1)

            def grow(k, j):
                s = U * k + j
                pe.wait_ge(copied, s + 1)
                for q in range(HB // 2):
                    wait(pe, active, (HB // 2) * (s - 2) + q + 1)
                    for b in range(2 * q, 2 * q + 2):
                        last = pe.matmul(h_ps[2 * (j % 2) + q][:, (b % 2) * 2 * P:(b % 2 + 1) * 2 * P],
                                         C.ffn1[:, b * P:(b + 1) * P], xT[j % 2][:, :], start=True, stop=True)
                    last.then_inc(hidden, 1)

            def shrink(k, j):
                s = U * k + j
                pe.wait_ge(active, (HB // 2) * (s + 1))
                wait(pe, added, s - 1)
                for i in range(2):
                    g = p_ps[j % 2][:, i * D:(i + 1) * D]
                    pe.matmul(g, C.ones3[:, :], C.bias[:, C.B_F2:C.B_F2 + D], start=True, stop=False)
                    for b in range(HB):
                        last = pe.matmul(g, hid[j % 2][:, b, i * P:(i + 1) * P], C.ffn2[:, b, :],
                                         start=False, stop=(b == HB - 1))
                last.then_inc(multiplied, 1)

            pipeline(pe, GROUPS, U, (2, turn), (1, grow), (0, shrink))

        @block.scalar
        def _(act):
            def copy(k, j):
                s = U * k + j
                act.wait_ge(turned, s + 1)
                wait(act, hidden, (HB // 2) * (s - 1))
                act.activation(xT[j % 2][:, :], t_ps[j % 2][:, 0:2 * P], ACT.Copy).then_inc(copied, 1)

            def activate(k, j):
                s = U * k + j
                wait(act, multiplied, s - 1)
                for q in range(HB // 2):
                    act.wait_ge(hidden, (HB // 2) * s + q + 1)
                    for b in range(2 * q, 2 * q + 2):
                        last = act.activation(hid[j % 2][:, b, :], h_ps[2 * (j % 2) + q][:, (b % 2) * 2 * P:(b % 2 + 1) * 2 * P],
                                              ACT.Gelu, bias=C.ffn1_b[:, b:b + 1])
                    last.then_inc(active, 1)

            def scale(k, j):
                ln.scale_act(act, out[j], out[j], U * k + j, j).then_inc(done, 1)

            pipeline(act, GROUPS, U, (8, copy), (7, activate), (0, scale))

        @block.vector
        def _(dve):
            def add(k, j):
                s = U * k + j
                dve.wait_ge(multiplied, s + 1)
                wait(dve, stored[j], 16 * k)
                dve.tensor_tensor(out[j][:, :, :], p_ps[j % 2][:, 0:2 * D].rearrange("p (a b) -> p a b", a=2), x4[j][:, :, :],
                                  ALU.add).then_inc(added, 1)

            def count2(k, j):
                dve.wait_ge(added, U * k + j + 1)
                ln2.count(dve, out[j], j)

            def aggregate2(k, j):
                ln2.aggregate(dve, U * k + j, j)

            def scale2(k, j):
                ln2.scale(dve, out[j], out[j], U * k + j, j).then_inc(normed, 1)

            def gain(k, j):
                dve.wait_ge(normed, U * k + j + 1)
                dve.tensor_tensor(out[j][:, :, :], out[j][:, :, :], C.bcast("ln2_g"), ALU.mult).then_inc(gained, 1)

            def shift(k, j):
                dve.wait_ge(gained, U * k + j + 1)
                dve.tensor_tensor(out[j][:, :, :], out[j][:, :, :], C.bcast("ln2_b"), ALU.add).then_inc(shifted, 1)

            def join(k, j):
                dve.wait_ge(shifted, U * k + j + 1)
                dve.tensor_tensor(out[j][:, :, :], out[j][:, :, :], x3[j][:, :, :], ALU.add).then_inc(joined, 1)

            def count(k, j):
                dve.wait_ge(joined, U * k + j + 1)
                ln.count(dve, out[j], j)

            def aggregate(k, j):
                ln.aggregate(dve, U * k + j, j)

            def offset(k, j):
                ln.offset(dve, U * k + j, j)

            pipeline(dve, GROUPS, U, (5, add), (3, scale2), (2, count), (5, count2), (3, gain), (2, aggregate),
                     (5, aggregate2), (3, shift), (0, offset), (3, join))

        @block.gpsimd
        def _(pool):
            pipeline(pool, GROUPS, U, (3, lambda k, j: ln2.power(pool, C, U * k + j, j)), (0, lambda k, j: ln.power(pool, C, U * k + j, j)))




class Constants:
    BC = ["bn_g1", "bn_be1", "bn_b1", "bn_g2", "bn_be2", "bn_b2", "ln1_g", "ln1_b", "ln2_g", "ln2_b"]
    B_LIN, B_GRU, B_L, B_IN, B_F, B_F2 = 0, D, 5 * D, 7 * D, 8 * D, 9 * D
    NB = 10 * D

    def __init__(self, nc, ctx):
        def sb(name, shape, dt=F32):
            return ctx.enter_context(nc.sbuf_tensor(name, shape, dt))

        self.ident, self.ones = sb("ident", [P, P]), sb("ones", [P, P])
        self.ones3, self.minus_half = sb("ones3", [3, P], BF16), sb("minus_half", [P, 2])
        self.lin, self.whh, self.wc = sb("lin", [P, D]), sb("whh", [P, 3 * D]), sb("wc", [P, 3, 3 * D])
        self.gat = sb("gat", [P, 2, D + 8])
        self.wl, self.wr, self.wel = sb("wl", [P, 2, D]), sb("wr", [P, 2, D]), sb("wel", [ED + 1, 2, D])
        self.win, self.wf = sb("win", [P, D]), sb("wf", [P, 2, D])
        self.ffn1, self.ffn2, self.ffn1_b = sb("ffn1", [P, FFN]), sb("ffn2", [P, 4, D]), sb("ffn1_b", [P, 4])
        self.bias, self.bc = sb("bias", [3, self.NB], BF16), sb("bc", [P, len(self.BC), D])
        self.bn = [(sb(f"bn_scale{i}", [P, D]), sb(f"bn_shift{i}", [P, D])) for i in range(2)]
        self.lists, self.nat_lists = sb("lists", [P, TILES, 6]), sb("nat_lists", [P, NAT, 1])
        self.place_f = sb("place_f", [P, STEPS, 2, 2])
        self.targets = sb("targets", [P, TILES * P])
        self.bias_dram = nc.dram_tensor("bias_dram", (3, self.NB), BF16).ap()
        self.pad = nc.dram_tensor("pad", (3, PAD), F32).ap()
        self.dst_row = nc.dram_tensor("dst_row", (1, TILES * P), F32).ap()
        self.bias_row = nc.dram_tensor("bias_row", (1, NAT * P), F32).ap()

    def bcast(self, name):
        return self.bc[:, self.BC.index(name), :].unsqueeze(1).to_broadcast([P, 2, D])


def graph_kernel(nc, A, out):
    with ExitStack() as ctx:
        C = Constants(nc, ctx)

        def table(name, width, n_rows=NP):
            return nc.dram_tensor(f"table_{name}", (n_rows, width), F32).ap()

        ha, hb, x1, x3 = (table(n, D) for n in ("ha", "hb", "x1", "x3"))
        agg, maxima, gsum = (table(n, w, (t + 1) * P) for n, w, t in (("agg", D, TILES), ("maxima", D, NAT), ("gsum", GT, TILES)))
        esum = C.edge_sums = table("esum", EW)
        gtab = table("gtab", GX)

        prepare_weights(nc, A, C)
        prepare_edges(nc, A, C)
        clear_tables(nc, C, esum, [(agg, D), (maxima, D), (gsum, GT)])
        sum_edges(nc, C, "Se", A["edge_attr"], esum, attributes=True)

        transform(nc, C, "T0", "copy", A["x"], project=(C.lin[:, :], C.B_LIN), p_out=ha, external=True)
        h, g = ha, hb
        for layer in range(3):
            sum_edges(nc, C, f"S{layer}", h, agg, places=(layer == 0))
            if layer < 2:
                gru(nc, C, f"G{layer}", layer, h, agg, g)
            else:
                gru(nc, C, f"G{layer}", layer, h, agg, x1, tail=dict(a=A["x"], project=("gat", 0), p_out=gtab, external=True))
            h, g = g, h

        attend_edges(nc, C, "A1", gtab, gsum)
        merge_attention(nc, C, "M1", gsum, gtab, ha, (0, 1, 2), C.bn[0])
        transform(nc, C, "T2", "bn", ha, bn=C.bn[0], project=("gat", 1), p_out=gtab)
        attend_edges(nc, C, "A2", gtab, gsum)
        merge_attention(nc, C, "M2", gsum, gtab, hb, (3, 4, 5), C.bn[1])
        transform(nc, C, "T3", "bn_ln", hb, x1, bn=C.bn[1], x_out=ha)

        sum_edges(nc, C, "S3", ha, agg)
        convolve(nc, C, "C1", 0, ha, agg, esum, hb)
        sum_edges(nc, C, "S4", hb, agg)
        convolve(nc, C, "C2", 1, hb, agg, esum, x3, tail=dict(a=ha, project=(C.win[:, :], C.B_IN), p_out=x1))

        max_edges(nc, C, "X5", x1, maxima)
        update(nc, C, "U5", x3, x1, maxima, esum, ha)
        feed_forward(nc, C, "F5", ha, x3, out)


def kernel(**inputs):
    import numpy as np
    import concourse.bacc as bacc
    from concourse.bass_utils import run_bass_kernel_spmd

    v = {name: np.asarray(a) for name, a in inputs.items()}

    def t(name):
        a = v[name]
        return np.ascontiguousarray(np.swapaxes(a, -1, -2))

    def row(name):
        return v[name].reshape(1, -1)

    host = {
        "x": v["x"], "src": v["src"], "dst": v["dst"], "edge_attr": v["edge_attr_32"],
        "lin_wT": t("L0_gnn_lin_w"), "lin_b": row("L0_gnn_lin_b"), "gru_wT": t("L0_gnn_weight"),
        "w_ihT": t("L0_gnn_w_ih"), "w_hhT": t("L0_gnn_w_hh"), "b_ih": row("L0_gnn_b_ih"), "b_hh": row("L0_gnn_b_hh"),
        "gat_W1": v["L1_gnn_W1"], "gat_W1T": t("L1_gnn_W1"), "gat_W2": v["L1_gnn_W2"], "gat_W2T": t("L1_gnn_W2"),
        "a1_src": v["L1_gnn_a1_src"], "a1_dst": v["L1_gnn_a1_dst"],
        "a2_src": v["L1_gnn_a2_src"], "a2_dst": v["L1_gnn_a2_dst"],
        "bn_b1": row("L1_gnn_b1"), "bn_g1": row("L1_gnn_g1"), "bn_be1": row("L1_gnn_beta1"),
        "bn_b2": row("L1_gnn_b2"), "bn_g2": row("L1_gnn_g2"), "bn_be2": row("L1_gnn_beta2"),
        "W_lT": t("L2_gnn_W_l"), "b_l": row("L2_gnn_b_l"), "W_rT": t("L2_gnn_W_r"),
        "W_e": v["L2_gnn_W_e"], "b_e": v["L2_gnn_b_e"],
        "W_in_w": v["L3_gnn_W_in_w"], "W_in_b": row("L3_gnn_W_in_b"),
        "W_updT": t("L3_gnn_W_upd_w"), "W_upd_b": v["L3_gnn_W_upd_b"],
        "W_out_w": v["L3_gnn_W_out_w"], "W_out_b": row("L3_gnn_W_out_b"),
        "ln1_g": row("L3_gnn_ln1_g"), "ln1_b": row("L3_gnn_ln1_b"),
        "ln2_g": row("L3_gnn_ln2_g"), "ln2_b": row("L3_gnn_ln2_b"),
        "ffn1_w": v["L3_gnn_ffn1_w"], "ffn1_b": v["L3_gnn_ffn1_b"],
        "ffn2_w": v["L3_gnn_ffn2_w"], "ffn2_b": row("L3_gnn_ffn2_b"),
    }
    nc = bacc.Bacc("TRN2", target_bir_lowering=False, num_devices=1)
    arrays, aps = {}, {}
    for name, a in host.items():
        arrays[f"in_{name}"] = np.ascontiguousarray(a)
        aps[name] = nc.dram_tensor(f"in_{name}", a.shape, mybir.dt.from_np(a.dtype), kind="ExternalInput").ap()
    out = nc.dram_tensor("out_x", (N, D), F32, kind="ExternalOutput").ap()
    graph_kernel(nc, aps, out)
    r = run_bass_kernel_spmd(nc, [arrays], core_ids=[0])
    return r.results[0]["out_x"]
```
